# Optimizing a Trainium2 kernel written in Bass

```python
import numpy as np
import jax
import jax.numpy as jnp

def _softmax(x, axis=-1):
    return jax.nn.softmax(x, axis=axis)

def _gelu(x):
    return jax.nn.gelu(x, approximate=True)

def _silu(x):
    return jax.nn.silu(x)

def _sigmoid(x):
    return jax.nn.sigmoid(x)

def _layernorm(x, axis=-1, eps=1e-05):
    m = jnp.mean(x, axis=axis, keepdims=True)
    v = jnp.var(x, axis=axis, keepdims=True)
    return (x - m) / jnp.sqrt(v + eps)

def _scatter_add(tgt, idx, src, axis=0):
    return tgt.at[idx].add(src)

def _segment_sum(src, seg, n):
    return jax.ops.segment_sum(src, seg, n)
kernel_name = 'mk_flamingo_gated_d2_seqx_r4_fb1efe'

def setup_inputs(seed: int=0):
    np.random.seed(seed)
    _w = jnp.asarray

    def _rec_inputs():
        import jax
        import jax.numpy as jnp
        _rk = jax.random.key(seed)
        x = -0.0002928 + 1 * jax.random.normal(jax.random.fold_in(_rk, 1), (2, 1024, 256), jnp.float32)
        _lenS = 1024 - jax.random.randint(jax.random.fold_in(_rk, 7), (2,), 0, max(1, 1024 // 4) + 1, jnp.int32)
        _lenS2 = 77 - jax.random.randint(jax.random.fold_in(_rk, 8), (2,), 0, max(1, 77 // 4) + 1, jnp.int32)
        _ctx_1024P = jax.random.normal(jax.random.fold_in(_rk, 11), (2, 16, 256), jnp.float32)
        _ctx_1024c = jax.random.dirichlet(jax.random.fold_in(_rk, 511), 0.3 * jnp.ones((16,), jnp.float32), (2, 77))
        _ctx_1024t = jnp.einsum('bsk,bkd->bsd', _ctx_1024c, _ctx_1024P)
        _ctx_1024t = _ctx_1024t * jax.lax.rsqrt(jnp.mean(jnp.square(_ctx_1024t)) + 1e-12) * 0.953939
        ctx_1024 = -1.39393e-06 + 0.999914 * (_ctx_1024t + 0.3 * jax.random.normal(jax.random.fold_in(_rk, 611), (2, 77, 256), jnp.float32))
        _validS = jnp.arange(1024)[None, :] < _lenS[:, None]
        _validS2 = jnp.arange(77)[None, :] < _lenS2[:, None]
        _causal = jnp.tril(jnp.ones((1024, 1024), dtype=bool))
        mask_Bx1x1xS2_bf1 = jnp.ones((2, 1, 1, 77), dtype=bool)
        mask_BxS2_ik0 = jnp.where(jnp.broadcast_to(_validS2[:, :], (2, 77)), 0, 1).astype(jnp.int32)
        _g = jax.random.normal(jax.random.fold_in(_rk, 9001), (2, 2), jnp.float32)
        _g = jnp.sign(_g) * jnp.maximum(jnp.abs(_g), 1.0) + (_g == 0) * 1.0
        g_xattn = _g[0]
        g_ffn = _g[1]
        return (x, ctx_1024, mask_Bx1x1xS2_bf1, mask_BxS2_ik0, g_xattn, g_ffn)
    x, ctx_1024, mask_Bx1x1xS2_bf1, mask_BxS2_ik0, g_xattn, g_ffn = _rec_inputs()

    def _L0_xattn_setup():
        import jax, jax.numpy as jnp
        import numpy as np
        D_MODEL = 256
        NUM_HEADS = 16
        D_K = D_MODEL // NUM_HEADS

        def _split_heads(x):
            B, T, _ = x.shape
            return x.reshape(B, T, NUM_HEADS, D_K).transpose(0, 2, 1, 3)
        key = jax.random.key(seed)
        ks = jax.random.split(key, 12)
        B, T = (2, 512)
        s = 1.0 / np.sqrt(D_MODEL)
        inp = {'q': jax.random.normal(ks[0], (B, T, D_MODEL), jnp.float32), 'k': jax.random.normal(ks[1], (B, T, D_MODEL), jnp.float32), 'v': jax.random.normal(ks[2], (B, T, D_MODEL), jnp.float32), 'mask': jnp.ones((B, 1, 1, T), dtype=bool), 'Wq': jax.random.normal(ks[3], (D_MODEL, D_MODEL), jnp.float32) * s, 'bq': jnp.zeros((D_MODEL,), jnp.float32), 'Wk': jax.random.normal(ks[4], (D_MODEL, D_MODEL), jnp.float32) * s, 'bk': jnp.zeros((D_MODEL,), jnp.float32), 'Wv': jax.random.normal(ks[5], (D_MODEL, D_MODEL), jnp.float32) * s, 'bv': jnp.zeros((D_MODEL,), jnp.float32), 'Wo': jax.random.normal(ks[6], (D_MODEL, D_MODEL), jnp.float32) * s, 'bo': jnp.zeros((D_MODEL,), jnp.float32)}
        return inp
    _L0_xattn_all = _L0_xattn_setup()
    _L0_xattn_in = {k: v for k, v in _L0_xattn_all.items() if k in ('Wq', 'bq', 'Wk', 'bk', 'Wv', 'bv', 'Wo', 'bo')}
    del _L0_xattn_all

    def _L0_ffn_setup():
        import jax, jax.numpy as jnp
        import numpy as np
        D_MODEL = 256
        D_FF = 1024
        NUM_M = 2
        E_ROUTER = 8 * NUM_M - 1
        D_FF_R = D_FF // NUM_M
        TOP_K = NUM_M * 2 - 1
        B, T = (2, 512)

        def _expert_stack(x, W1, b1, W2, b2):
            h = jax.nn.gelu(jnp.einsum('btd,edf->ebtf', x, W1) + b1[:, None, None, :], approximate=False)
            return jnp.einsum('ebtf,efd->ebtd', h, W2) + b2[:, None, None, :]
        key = jax.random.key(seed)
        ks = jax.random.split(key, 12)
        s = lambda fan_in: 1.0 / np.sqrt(fan_in)
        x = jax.random.normal(ks[0], (B, T, D_MODEL), dtype=jnp.float32)
        sW1 = jax.random.uniform(ks[1], (1, D_MODEL, D_FF), jnp.float32, -s(D_MODEL), s(D_MODEL))
        sb1 = jax.random.uniform(ks[2], (1, D_FF), jnp.float32, -s(D_MODEL), s(D_MODEL))
        sW2 = jax.random.uniform(ks[3], (1, D_FF, D_MODEL), jnp.float32, -s(D_FF), s(D_FF))
        sb2 = jax.random.uniform(ks[4], (1, D_MODEL), jnp.float32, -s(D_FF), s(D_FF))
        rW1 = jax.random.uniform(ks[5], (E_ROUTER, D_MODEL, D_FF_R), jnp.float32, -s(D_MODEL), s(D_MODEL))
        rb1 = jax.random.uniform(ks[6], (E_ROUTER, D_FF_R), jnp.float32, -s(D_MODEL), s(D_MODEL))
        rW2 = jax.random.uniform(ks[7], (E_ROUTER, D_FF_R, D_MODEL), jnp.float32, -s(D_FF_R), s(D_FF_R))
        rb2 = jax.random.uniform(ks[8], (E_ROUTER, D_MODEL), jnp.float32, -s(D_FF_R), s(D_FF_R))
        gW = jax.random.uniform(ks[9], (D_MODEL, E_ROUTER), jnp.float32, -s(D_MODEL), s(D_MODEL))
        gb = jax.random.uniform(ks[10], (E_ROUTER,), jnp.float32, -s(D_MODEL), s(D_MODEL))
        return {'x': x, 'sW1': sW1, 'sb1': sb1, 'sW2': sW2, 'sb2': sb2, 'rW1': rW1, 'rb1': rb1, 'rW2': rW2, 'rb2': rb2, 'gW': gW, 'gb': gb}
    _L0_ffn_all = _L0_ffn_setup()
    _L0_ffn_in = {k: v for k, v in _L0_ffn_all.items() if k in ('sW1', 'sb1', 'sW2', 'sb2', 'rW1', 'rb1', 'rW2', 'rb2', 'gW', 'gb')}
    del _L0_ffn_all

    def _L1_xattn_setup():
        import jax, jax.numpy as jnp
        import numpy as np
        B, LQ, LK, D = (4, 512, 512, 256)
        H = 16
        HD = D // H

        def _split_heads(x):
            b, l, _ = x.shape
            return x.reshape(b, l, H, HD).transpose(0, 2, 1, 3)
        key = jax.random.key(seed)
        ks = jax.random.split(key, 10)
        s = 0.02
        return {'hidden_states': jax.random.normal(ks[0], (B, LQ, D), jnp.float32), 'context': jax.random.normal(ks[1], (B, LK, D), jnp.float32), 'attention_mask': jax.random.randint(ks[2], (B, LK), 0, 2, jnp.int32), 'q_w': jax.random.normal(ks[3], (D, D), jnp.float32) * s, 'q_b': jnp.zeros((D,), jnp.float32), 'k_w': jax.random.normal(ks[4], (D, D), jnp.float32) * s, 'k_b': jnp.zeros((D,), jnp.float32), 'v_w': jax.random.normal(ks[5], (D, D), jnp.float32) * s, 'v_b': jnp.zeros((D,), jnp.float32)}
    _L1_xattn_all = _L1_xattn_setup()
    _L1_xattn_in = {k: v for k, v in _L1_xattn_all.items() if k in ('q_w', 'q_b', 'k_w', 'k_b', 'v_w', 'v_b')}
    del _L1_xattn_all

    def _L1_ffn_setup():
        import jax, jax.numpy as jnp
        import numpy as np
        B, S, D, H, E, K = (4, 512, 256, 512, 8, 2)
        TEMP = 5.0
        EPS = 1e-09
        key = jax.random.key(seed)
        k_x, k_wg, k_w1, k_w2 = jax.random.split(key, 4)
        scale = 0.02
        return {'x': jax.random.normal(k_x, (B, S, D), dtype=jnp.float32), 'Wg': jax.random.normal(k_wg, (D, E), dtype=jnp.float32) * scale, 'bg': jnp.zeros((E,), dtype=jnp.float32), 'W1': jax.random.normal(k_w1, (E, D, H), dtype=jnp.float32) * scale, 'b1': jnp.zeros((E, H), dtype=jnp.float32), 'W2': jax.random.normal(k_w2, (E, H, D), dtype=jnp.float32) * scale, 'b2': jnp.zeros((E, D), dtype=jnp.float32)}
    _L1_ffn_all = _L1_ffn_setup()
    _L1_ffn_in = {k: v for k, v in _L1_ffn_all.items() if k in ('Wg', 'bg', 'W1', 'b1', 'W2', 'b2')}
    del _L1_ffn_all
    return {'x': x, 'ctx_1024': ctx_1024, 'mask_Bx1x1xS2_bf1': mask_Bx1x1xS2_bf1, 'mask_BxS2_ik0': mask_BxS2_ik0, 'g_xattn': g_xattn, 'g_ffn': g_ffn, 'L0_xattn_Wq': _L0_xattn_in['Wq'], 'L0_xattn_bq': _L0_xattn_in['bq'], 'L0_xattn_Wk': _L0_xattn_in['Wk'], 'L0_xattn_bk': _L0_xattn_in['bk'], 'L0_xattn_Wv': _L0_xattn_in['Wv'], 'L0_xattn_bv': _L0_xattn_in['bv'], 'L0_xattn_Wo': _L0_xattn_in['Wo'], 'L0_xattn_bo': _L0_xattn_in['bo'], 'L0_ffn_sW1': _L0_ffn_in['sW1'], 'L0_ffn_sb1': _L0_ffn_in['sb1'], 'L0_ffn_sW2': _L0_ffn_in['sW2'], 'L0_ffn_sb2': _L0_ffn_in['sb2'], 'L0_ffn_rW1': _L0_ffn_in['rW1'], 'L0_ffn_rb1': _L0_ffn_in['rb1'], 'L0_ffn_rW2': _L0_ffn_in['rW2'], 'L0_ffn_rb2': _L0_ffn_in['rb2'], 'L0_ffn_gW': _L0_ffn_in['gW'], 'L0_ffn_gb': _L0_ffn_in['gb'], 'L1_xattn_q_w': _L1_xattn_in['q_w'], 'L1_xattn_q_b': _L1_xattn_in['q_b'], 'L1_xattn_k_w': _L1_xattn_in['k_w'], 'L1_xattn_k_b': _L1_xattn_in['k_b'], 'L1_xattn_v_w': _L1_xattn_in['v_w'], 'L1_xattn_v_b': _L1_xattn_in['v_b'], 'L1_ffn_Wg': _L1_ffn_in['Wg'], 'L1_ffn_bg': _L1_ffn_in['bg'], 'L1_ffn_W1': _L1_ffn_in['W1'], 'L1_ffn_b1': _L1_ffn_in['b1'], 'L1_ffn_W2': _L1_ffn_in['W2'], 'L1_ffn_b2': _L1_ffn_in['b2']}

def reference(x, ctx_1024, mask_Bx1x1xS2_bf1, mask_BxS2_ik0, g_xattn, g_ffn, L0_xattn_Wq, L0_xattn_bq, L0_xattn_Wk, L0_xattn_bk, L0_xattn_Wv, L0_xattn_bv, L0_xattn_Wo, L0_xattn_bo, L0_ffn_sW1, L0_ffn_sb1, L0_ffn_sW2, L0_ffn_sb2, L0_ffn_rW1, L0_ffn_rb1, L0_ffn_rW2, L0_ffn_rb2, L0_ffn_gW, L0_ffn_gb, L1_xattn_q_w, L1_xattn_q_b, L1_xattn_k_w, L1_xattn_k_b, L1_xattn_v_w, L1_xattn_v_b, L1_ffn_Wg, L1_ffn_bg, L1_ffn_W1, L1_ffn_b1, L1_ffn_W2, L1_ffn_b2):
    import jax
    import jax.numpy as jnp

    def _L0_xattn_ref(q, k, v, mask, Wq, bq, Wk, bk, Wv, bv, Wo, bo):
        import jax, jax.numpy as jnp
        import numpy as np
        D_MODEL = 256
        NUM_HEADS = 16
        D_K = D_MODEL // NUM_HEADS

        def _split_heads(x):
            B, T, _ = x.shape
            return x.reshape(B, T, NUM_HEADS, D_K).transpose(0, 2, 1, 3)
        B, Tq, _ = q.shape
        qh = _split_heads(q @ Wq + bq)
        kh = _split_heads(k @ Wk + bk)
        vh = _split_heads(v @ Wv + bv)
        scores = jnp.einsum('bhqd,bhkd->bhqk', qh, kh) / jnp.sqrt(jnp.float32(D_K))
        scores = jnp.where(mask, scores, -jnp.inf)
        attn = jax.nn.softmax(scores.astype(jnp.float32), axis=-1).astype(scores.dtype)
        out = jnp.einsum('bhqk,bhkd->bhqd', attn, vh)
        out = out.transpose(0, 2, 1, 3).reshape(B, Tq, D_MODEL)
        return out @ Wo + bo

    def _L0_ffn_ref(x, sW1, sb1, sW2, sb2, rW1, rb1, rW2, rb2, gW, gb):
        import jax, jax.numpy as jnp
        import numpy as np
        D_MODEL = 256
        D_FF = 1024
        NUM_M = 2
        E_ROUTER = 8 * NUM_M - 1
        D_FF_R = D_FF // NUM_M
        TOP_K = NUM_M * 2 - 1
        B, T = (2, 512)

        def _expert_stack(x, W1, b1, W2, b2):
            h = jax.nn.gelu(jnp.einsum('btd,edf->ebtf', x, W1) + b1[:, None, None, :], approximate=False)
            return jnp.einsum('ebtf,efd->ebtd', h, W2) + b2[:, None, None, :]
        shared_enc = _expert_stack(x, sW1, sb1, sW2, sb2).sum(0)
        weights = jax.nn.softmax(x @ gW + gb, axis=-1)
        topv, topi = jax.lax.top_k(weights, TOP_K)
        gated = (jax.nn.one_hot(topi, E_ROUTER, dtype=weights.dtype) * topv[..., None]).sum(axis=-2)
        router_out = _expert_stack(x, rW1, rb1, rW2, rb2)
        router_enc = jnp.einsum('ebtd,bte->btd', router_out, gated)
        return shared_enc + router_enc + x

    def _L1_xattn_ref(hidden_states, context, attention_mask, q_w, q_b, k_w, k_b, v_w, v_b):
        import jax, jax.numpy as jnp
        import numpy as np
        B, LQ, LK, D = (4, 512, 512, 256)
        H = 16
        HD = D // H

        def _split_heads(x):
            b, l, _ = x.shape
            return x.reshape(b, l, H, HD).transpose(0, 2, 1, 3)
        q = _split_heads(hidden_states @ q_w.T + q_b)
        k = _split_heads(context @ k_w.T + k_b)
        v = _split_heads(context @ v_w.T + v_b)
        scores = jnp.einsum('bhqd,bhkd->bhqk', q, k) / jnp.sqrt(jnp.float32(HD))
        mask = (attention_mask > 0)[:, None, None, :]
        scores = jnp.where(mask, -jnp.inf, scores)
        probs = jax.nn.softmax(scores, axis=-1)
        ctx = jnp.einsum('bhqk,bhkd->bhqd', probs, v)
        ctx = ctx.transpose(0, 2, 1, 3).reshape(ctx.shape[0], ctx.shape[2], H * HD)
        return ctx

    def _L1_ffn_ref(x, Wg, bg, W1, b1, W2, b2):
        import jax, jax.numpy as jnp
        import numpy as np
        B, S, D, H, E, K = (4, 512, 256, 512, 8, 2)
        TEMP = 5.0
        EPS = 1e-09
        logits = jnp.einsum('bsd,de->bse', x, Wg) + bg
        probs = jax.nn.softmax(logits / TEMP, axis=-1)
        vals, idx = jax.lax.top_k(probs, K)
        onehot = jax.nn.one_hot(idx, E, dtype=x.dtype)
        mask = jnp.einsum('bske,bsk->bse', onehot, vals)
        gates = mask / (jnp.sum(mask, axis=-1, keepdims=True) + EPS)
        h = jax.nn.gelu(jnp.einsum('bsd,edh->besh', x, W1) + b1[None, :, None, :], approximate=False)
        out = jnp.einsum('besh,ehd->besd', h, W2) + b2[None, :, None, :]
        y = jnp.einsum('bse,besd->bsd', gates, out)
        return y
    x = x + jnp.tanh(g_xattn[0]) * _L0_xattn_ref(_layernorm(x, axis=-1), ctx_1024, ctx_1024, mask_Bx1x1xS2_bf1, L0_xattn_Wq, L0_xattn_bq, L0_xattn_Wk, L0_xattn_bk, L0_xattn_Wv, L0_xattn_bv, L0_xattn_Wo, L0_xattn_bo)
    x = x + jnp.tanh(g_ffn[0]) * _L0_ffn_ref(_layernorm(x, axis=-1), L0_ffn_sW1, L0_ffn_sb1, L0_ffn_sW2, L0_ffn_sb2, L0_ffn_rW1, L0_ffn_rb1, L0_ffn_rW2, L0_ffn_rb2, L0_ffn_gW, L0_ffn_gb)
    x = x + jnp.tanh(g_xattn[1]) * _L1_xattn_ref(_layernorm(x, axis=-1), ctx_1024, mask_BxS2_ik0, L1_xattn_q_w, L1_xattn_q_b, L1_xattn_k_w, L1_xattn_k_b, L1_xattn_v_w, L1_xattn_v_b)
    x = x + jnp.tanh(g_ffn[1]) * _L1_ffn_ref(_layernorm(x, axis=-1), L1_ffn_Wg, L1_ffn_bg, L1_ffn_W1, L1_ffn_b1, L1_ffn_W2, L1_ffn_b2)
    return x

_drawn_inputs = setup_inputs


def setup_inputs(seed=0):
    import zlib

    import numpy as np

    out = dict(_drawn_inputs(seed))
    spreads = {'g_ffn': (-1.0, 0.6),
     'L0_xattn_bq': (0.0, 0.268),
     'L0_xattn_bk': (0.0, 0.8),
     'L0_xattn_bv': (0.0, 0.1),
     'L0_xattn_bo': (0.0, 0.1),
     'L1_xattn_q_b': (0.0, 0.523),
     'L1_xattn_k_b': (0.0, 0.8),
     'L1_xattn_v_b': (0.0, 0.1),
     'L1_ffn_bg': (0.0, 0.1),
     'L1_ffn_b1': (0.0, 0.1),
     'L1_ffn_b2': (0.0, 0.1)}
    factors = {'L0_ffn_rb1': 4.132, 'L0_ffn_rb2': 2.91}
    for name, (base, spread) in spreads.items():
        noise = np.random.default_rng([zlib.crc32(name.encode()), seed]).standard_normal(out[name].shape)
        drawn = base * np.exp(spread * noise) if base else spread * noise
        out[name] = jnp.asarray(drawn.astype(out[name].dtype))
    for name, factor in factors.items():
        out[name] = (out[name] * factor).astype(out[name].dtype)
    return out
```

```python
from contextlib import ExitStack

import numpy as np

import concourse.bass as bass
from concourse import mybir

F32 = mybir.dt.float32
F16 = mybir.dt.float16
BF16 = mybir.dt.bfloat16
I32 = mybir.dt.int32
U8 = mybir.dt.uint8
ACT = mybir.ActivationFunctionType
ALU = mybir.AluOpType
AX_X = mybir.AxisListType.X

P = 128
D = 256
DC = D // P
B = 2
S = 1024
NT = B * S // P
TB = NT // B
KEYS = 77
HEADS = 16
HD = D // HEADS
HQ = 4
NQ = HEADS // HQ
HID = 512
HC = HID // P
WCOLS = DC * HID + HC * D
WPART = WCOLS // 2
BCOLS = HID + D
WSCALE = 16.0
MASKED = -1e30
EPS = 1e-5

LAYERS = [
    dict(experts=15, topk=3, shared=2, inv_temp=1.0, renorm=False, out_proj=True),
    dict(experts=8, topk=2, shared=0, inv_temp=1.0 / 5.0, renorm=True, out_proj=False),
]


def routed_tiles(layer):
    c = LAYERS[layer]
    return (c["topk"] * NT * P + c["experts"] * (P - 1)) // P


MAXE = max(c["experts"] + c["shared"] for c in LAYERS)
SLOT_TILES = max(routed_tiles(n) + c["shared"] * NT for n, c in enumerate(LAYERS))


class Unit:

    def __init__(self, k, c):
        self.n = k * 2 + c
        self.u = c % 2
        self.i = k + c // 2
        self.c = c
        self.k = k

    def shifted(self, d):
        return Unit(self.k, self.c + d)


def run_pipeline(eng, step, n_units, lead, lag, pause=None, at_pause=None):
    lo, hi = lag, n_units - lead
    hi = lo + (hi - lo) // 2 * 2

    def peeled(n):
        if n == pause:
            at_pause()
        step(Unit(0, n), lambda d: 0 <= n + d < n_units)

    for n in range(-lead, lo):
        peeled(n)
    cuts = [lo, hi]
    if pause is not None and lo <= pause < hi:
        assert (pause - lo) % 2 == 0
        cuts = [lo, pause, hi]
    for start, end in zip(cuts, cuts[1:]):
        if start == pause:
            at_pause()
        if end > start:
            with eng.Fori(0, (end - start) // 2) as k:
                for c in (start, start + 1):
                    step(Unit(k, c), lambda d: True)
    for n in range(hi, n_units + lag):
        peeled(n)


class Chain:

    def __init__(self, eng, sem, base=0):
        self.eng, self.sem, self.base, self.n = eng, sem, base, 0

    def __call__(self, ins):
        self.n += 1
        ins.then_inc(self.sem, 1)
        self.eng.wait_ge(self.sem, self.base + self.n)


class Build:
    def __init__(self, nc, ctx, ins, out):
        self.nc, self.ctx, self.ins, self.out = nc, ctx, ins, out
        self.sems = []
        self.persistent()

    def sem(self, name):
        handle = self.nc.alloc_semaphore(name=name)
        self.sems.append(handle)
        return handle

    def recycle_semaphores(self):
        self.nc.all_engine_barrier()
        self.nc.clear_and_free_semaphores(self.sems)
        self.nc.all_engine_barrier()
        self.sems = []

    def sb(self, name, shape, dt):
        return self.ctx.enter_context(self.nc.sbuf_tensor(name, shape, dt))

    def persistent(self):
        nc, sb = self.nc, self.sb
        self.x = sb("x_all", [P, NT, D], F32)
        self.mv = sb("mean_var", [P, NT, 2], F32)
        self.rstd = sb("rstd", [P, NT], F32)
        self.ident = sb("ident", [P, P], F32)
        self.ones_row = sb("ones_row", [1, P], F32)
        self.ones_bf = sb("ones_bf", [P, P], BF16)
        self.before = sb("before", [P, P], BF16)
        self.ones16 = sb("ones16", [2, P], F16)
        self.gates_in = sb("gates_in", [P, 4], F32)
        self.tg = sb("tanh_gates", [P, 4], F32)
        self.head_mask = sb("head_mask", [P, 8], F32)
        self.half = sb("neg_half", [P, NT], F32)
        self.weights = sb("weights", [P, MAXE, 2, WCOLS], F16)
        self.eid = sb("expert_of_tile", [1, SLOT_TILES], I32)
        d = nc.dram_tensor
        self.xg = d("expert_rows_in", (SLOT_TILES * P, D), F32).ap()
        self.yg = d("expert_rows_out", (SLOT_TILES * P, D), F32).ap()
        self.bg = d("expert_biases", (MAXE, 2, BCOLS), F16).ap()

    def start(self):
        nc = self.nc
        with ExitStack() as tmp:
            zeros = tmp.enter_context(nc.sbuf_tensor("zeros", [P, 2 * D], F32))
            stats = tmp.enter_context(nc.sbuf_tensor("stats0", [P, NT, 6], F32))
            s_x, s_g, s_zero, s_fill = self.sem("x_loaded"), self.sem("gates_loaded"), self.sem("zero_ready"), self.sem("slots_filled")
            s_c, s_c2, s_v = self.sem("const_step"), self.sem("const_dve"), self.sem("stats0_step")
            block = tmp.enter_context(nc.Block())
            ins = self.ins

            @block.sync
            def _(sp):
                for q in range(4):
                    t0 = q * NT // 4
                    sp.dma_start(self.x[:, t0:t0 + NT // 4, :],
                                 ins["x"][t0 * P:(t0 + NT // 4) * P, :].rearrange("(t p) d -> p t d", p=P)).then_inc(s_x, 16)
                sp.dma_start(self.gates_in[:], ins["gates"]).then_inc(s_g, 16)
                sp.wait_ge(s_zero, 1)
                with sp.Fori(0, SLOT_TILES // 2) as t:
                    sp.dma_start(self.xg[bass.ds(t * (2 * P), 2 * P), :].rearrange("(a p) d -> p a d", p=P),
                                 zeros[:].rearrange("p (a d) -> p a d", a=2)).then_inc(s_fill, 16)
                if SLOT_TILES % 2:
                    sp.dma_start(self.xg[(SLOT_TILES - 1) * P:, :], zeros[:, 0:D]).then_inc(s_fill, 16)
                sp.wait_ge(s_fill, 16 * (SLOT_TILES // 2 + SLOT_TILES % 2))

            @block.gpsimd
            def _(pool):
                step = Chain(pool, s_c)
                nc.gpsimd.memset(zeros[:], 0.0).then_inc(s_zero, 1)
                step(nc.gpsimd.memset(self.ident[:], 0.0))
                step(nc.gpsimd.affine_select(out=self.ident[:], in_=self.ident[:], compare_op=ALU.not_equal, fill=1.0,
                                             base=0, pattern=[[-1, P]], channel_multiplier=1))
                step(nc.gpsimd.memset(self.ones_bf[:], 1.0))
                step(nc.gpsimd.affine_select(out=self.before[:], in_=self.ones_bf[:], compare_op=ALU.is_gt, fill=0.0,
                                             base=0, pattern=[[1, P]], channel_multiplier=-1))
                step(nc.gpsimd.memset(self.head_mask[:], 1.0))
                step(nc.gpsimd.affine_select(out=self.head_mask[:], in_=self.head_mask[:], compare_op=ALU.is_ge,
                                             fill=0.0, base=0, pattern=[[-HD, 8]], channel_multiplier=1))
                step(nc.gpsimd.affine_select(out=self.head_mask[:], in_=self.head_mask[:], compare_op=ALU.is_ge,
                                             fill=0.0, base=HD - 1, pattern=[[HD, 8]], channel_multiplier=-1))
                step(nc.gpsimd.memset(self.half[:], -0.5))
                step(nc.gpsimd.memset(self.ones_row[:], 1.0))
                step(nc.gpsimd.memset(self.ones16[:], 1.0))
                pool.wait_ge(s_v, 2 * NT + 1)
                step(nc.gpsimd.tensor_tensor(self.rstd[:], self.rstd[:], self.half[:], ALU.pow))

            @block.scalar
            def _(act):
                act.wait_ge(s_g, 16)
                nc.scalar.activation(self.tg[:], self.gates_in[:], ACT.Tanh).then_inc(s_c2, 1)
                act.wait_ge(s_c2, 1)

            @block.vector
            def _(dve):
                dve.wait_ge(s_x, 64)
                for t in range(NT):
                    nc.vector.bn_stats(stats[:, t, :], self.x[:, t, :]).then_inc(s_v, 1)
                dve.wait_ge(s_v, NT)
                for t in range(NT):
                    nc.vector.bn_aggr(self.mv[:, t, :], stats[:, t, :]).then_inc(s_v, 1)
                dve.wait_ge(s_v, 2 * NT)
                nc.vector.tensor_scalar(self.rstd[:], self.mv[:, :, 1], EPS, None, ALU.add).then_inc(s_v, 1)
                dve.wait_ge(s_v, 2 * NT + 1)

    def keep_row(self, dve, ready, ready_at, step, base, x_new, row, stats, mv1, T):
        nc = self.nc
        dve.wait_ge(ready, ready_at)
        nc.vector.bn_stats(stats[:], x_new[:]).then_inc(step, 1)
        dve.wait_ge(step, base + 1)
        nc.vector.tensor_scalar(row, x_new[:], 0.0, None, ALU.add)
        nc.vector.bn_aggr(mv1[:], stats[:]).then_inc(step, 1)
        dve.wait_ge(step, base + 2)
        nc.vector.tensor_scalar(self.mv[:, bass.ds(T, 1), :].rearrange("p a d -> p (a d)"), mv1[:], 0.0, None,
                                ALU.add).then_inc(step, 1)

    def store(self):
        s_out = self.sem("out_stored")
        with self.nc.Block() as block:
            @block.sync
            def _(sp):
                for q in range(4):
                    t0 = q * NT // 4
                    sp.dma_start(self.out[t0 * P:(t0 + NT // 4) * P, :].rearrange("(t p) d -> p t d", p=P),
                                 self.x[:, t0:t0 + NT // 4, :]).then_inc(s_out, 16)
                sp.wait_ge(s_out, 64)

    def attention(self, L):
        nc, cfg, ins = self.nc, LAYERS[L], self.ins
        out_proj = cfg["out_proj"]
        n_exp = cfg["experts"] + cfg["shared"]
        pre = f"l{L}_"
        sem = lambda name: self.sem(pre + name)
        with ExitStack() as tmp:
            sb = lambda name, shape, dt: tmp.enter_context(nc.sbuf_tensor(pre + name, shape, dt))
            psb = lambda name, shape: tmp.enter_context(nc.psum_tensor(pre + name, shape, F32))
            wq = sb("wq", [P, DC, D], F32)
            wo = sb("wo", [P, DC, D], F32) if out_proj else None
            bq, bk = sb("bq", [P, DC], F32), sb("bk", [P, DC], F32)
            bo = sb("bo", [1, D], F32) if out_proj else None
            keys_bd = sb("keys_bd", [P, B, NQ, HQ, KEYS], F32)
            vals = sb("vals", [KEYS, B, HEADS, HD + 1], F32)
            mask_row = sb("mask_row", [1, B, HQ, KEYS], BF16)

            with ExitStack() as setup:
                sbs = lambda name, shape, dt: setup.enter_context(nc.sbuf_tensor(pre + name, shape, dt))
                pss = lambda name, shape: setup.enter_context(nc.psum_tensor(pre + name, shape, F32))
                ctx_t = sbs("ctx_t", [P, DC, B * KEYS], F32)
                wk, wv = sbs("wk", [P, DC, D], F32), sbs("wv", [P, DC, D], F32)
                bv = sbs("bv", [1, D], F32)
                m_raw = sbs("m_raw", [1, B * KEYS], U8 if L == 0 else I32)
                m_f = sbs("m_f", [1, B * KEYS], F32)
                kt = sbs("kt", [P, DC, B * KEYS], F32)
                b_f = sbs("b_f", [MAXE, BCOLS], F32)
                b_s = sbs("b_s", [MAXE, 2, BCOLS], F16)
                ps_k = pss("ps_k", [P, DC, 512])
                ps_v = pss("ps_v", [P, B, 512])
                s_ld, s_k, s_v, s_kt, s_d, s_b = (sem(x) for x in ("params_loaded", "k_done", "v_done", "kt_done", "setup_step", "biases_loaded"))
                s_bs, s_bst = sem("bias_split"), sem("biases_stored")
                s_vals, s_bd = sem("vals_ready"), sem("keys_ready")
                block = setup.enter_context(nc.Block())
                split = lambda ap: ap.rearrange("(c p) n -> p c n", p=P)

                @block.sync
                def _(sp):
                    loads = [(ctx_t, split(ins["ctx_t"])), (wk, split(ins[f"wk{L}"])), (wv, split(ins[f"wv{L}"])),
                             (bk, ins[f"bk{L}"]), (bv, ins[f"bv{L}"]), (m_raw, ins[f"mask{L}"]),
                             (wq, split(ins[f"wq{L}"])), (bq, ins[f"bq{L}"])]
                    if out_proj:
                        loads += [(wo, split(ins["wo0"])), (bo, ins["bo0"])]
                    for dst, src in loads:
                        sp.dma_start(dst[:], src).then_inc(s_ld, 16)
                    sp.dma_start(b_f[0:n_exp, :], ins[f"biases{L}"]).then_inc(s_b, 16)
                    sp.wait_ge(s_bs, 3)
                    sp.dma_start(self.bg[0:n_exp], b_s[0:n_exp]).then_inc(s_bst, 16)
                    sp.wait_ge(s_bst, 16)

                n_loads = 16 * (10 if out_proj else 8)

                @block.tensor
                def _(pe):
                    pe.wait_ge(s_ld, n_loads)
                    for j in range(DC):
                        for c in range(DC):
                            mm = nc.tensor.matmul(ps_k[:, j, 0:B * KEYS], wk[:, c, j * P:(j + 1) * P], ctx_t[:, c, :],
                                                  start=(c == 0), stop=(c == DC - 1))
                        mm.then_inc(s_k, 1)
                    for b in range(B):
                        for c in range(DC):
                            nc.tensor.matmul(ps_v[0:KEYS, b, 0:D], ctx_t[:, c, b * KEYS:(b + 1) * KEYS], wv[:, c, :],
                                             start=(c == 0), stop=False)
                        nc.tensor.matmul(ps_v[0:KEYS, b, 0:D], self.ones_row[:, 0:KEYS], bv[:],
                                         start=False, stop=True).then_inc(s_v, 1)

                @block.scalar
                def _(act):
                    for j in range(DC):
                        act.wait_ge(s_k, j + 1)
                        nc.scalar.activation(kt[:, j, :], ps_k[:, j, 0:B * KEYS], ACT.Identity,
                                             bias=bk[:, j:j + 1]).then_inc(s_kt, 1)
                    act.wait_ge(s_b, 16)
                    nc.scalar.mul(b_f[0:n_exp, :], b_f[0:n_exp, :], WSCALE).then_inc(s_bs, 1)
                    act.wait_ge(s_bs, 1)
                    nc.scalar.copy(b_s[0:n_exp, 0, :], b_f[0:n_exp, :]).then_inc(s_bs, 1)

                @block.vector
                def _(dve):
                    nc.vector.memset(vals[:], 1.0).then_inc(s_d, 1)
                    dve.wait_ge(s_d, 1)
                    dve.wait_ge(s_ld, n_loads)
                    if L == 0:
                        nc.vector.tensor_scalar(m_f[:], m_raw[:], 0.0, MASKED, ALU.is_equal, ALU.mult).then_inc(s_d, 1)
                    else:
                        nc.vector.tensor_scalar(m_f[:], m_raw[:], 0.0, MASKED, ALU.is_gt, ALU.mult).then_inc(s_d, 1)
                    dve.wait_ge(s_d, 2)
                    for b in range(B):
                        row = m_f[:, b * KEYS:(b + 1) * KEYS].unsqueeze(1).broadcast_to([1, HQ, KEYS])
                        nc.vector.tensor_copy(mask_row[:, b], row).then_inc(s_d, 1)
                    dve.wait_ge(s_bs, 2)
                    nc.vector.tensor_tensor(b_s[0:n_exp, 1, :], b_f[0:n_exp, :], b_s[0:n_exp, 0, :],
                                            ALU.subtract).then_inc(s_bs, 1)
                    dve.wait_ge(s_v, B)
                    for b in range(B):
                        nc.vector.tensor_copy(vals[:, b, :, 0:HD],
                                              ps_v[0:KEYS, b, 0:D].rearrange("k (h d) -> k h d", h=HEADS)).then_inc(s_vals, 1)
                    dve.wait_ge(s_kt, DC)
                    for b in range(B):
                        for j in range(DC):
                            src = kt[:, j, b * KEYS:(b + 1) * KEYS].unsqueeze(1).broadcast_to([P, 8, KEYS])
                            msk = self.head_mask[:].unsqueeze(2).broadcast_to([P, 8, KEYS])
                            dst = keys_bd[:, b, 2 * j:2 * j + 2].rearrange("p q h k -> p (q h) k")
                            nc.vector.tensor_tensor(dst, src, msk, ALU.mult).then_inc(s_bd, 1)

            xn, xn_t, q_t = sb("xn", [P, 2, D], F32), sb("xn_t", [P, 2, DC, P], F32), sb("q_t", [P, 2, DC, P], F32)
            probs = sb("probs", [P, 2, HEADS, KEYS], F32)
            smax = sb("smax", [P, 2, NQ, HQ], F32)
            probs_t = sb("probs_t", [KEYS, NQ, HQ, P], F32)
            rec, att = sb("rec", [P, HEADS, 1], F32), sb("att", [P, HEADS, HD], F32)
            att_t = sb("att_t", [P, DC, P], F32)
            stats, mv1, x_new = sb("stats", [P, 6], F32), sb("mv1", [P, 2], F32), sb("x_new", [P, D], F32)
            stage = sb("stage", [P, 2, WPART], F32)
            ps_s = psb("ps_s", [P, NQ, 512])
            ps_t = psb("ps_t", [P, 2, 512])
            ps_a = psb("ps_a", [P, 512])
            ps_o = psb("ps_o", [P, 512])
            ps_xt = ps_a[:, 0:D]
            ps_q = ps_a[:, D:2 * D]
            ps_av = ps_o[:, 0:HEADS * (HD + 1)].rearrange("p (h e) -> p h e", h=HEADS)
            names = ("xn_ready", "xt_done", "xn_t_ready", "q_done", "q_t_ready", "scores_done", "smax_step", "shifted",
                     "probs_ready", "turned", "pt_ready_act", "pt_ready_dve", "av_done", "att_step", "att_turned",
                     "att_t_ready", "proj_done", "x_updated", "stats_step", "ps_a_free",
                     "w_high", "w_low", "rstd_step")
            s = {n: sem(n) for n in names}
            s_stage = [sem("w_staged0"), sem("w_staged1")]
            block = tmp.enter_context(nc.Block())
            tile_of = lambda un: un.i + TB * un.u
            per_unit = 2 * n_exp // NT
            assert per_unit in (1, 2)
            pieces = lambda un: [(un.n, 0), (un.n, 1)] if per_unit == 2 else [(un.i, un.u)]

            @block.sync
            def _(sp):
                def load(e, has):
                    for m in range(2):
                        sp.wait_ge(s["w_low"], e.n * 2 + m + 1)
                        sp.dma_start(stage[:, m, :], ins[f"weights{L}"][bass.ds(e.n, 1), :, m * WPART:(m + 1) * WPART]
                                     .rearrange("e p n -> p (e n)")).then_inc(s_stage[m], 16)

                run_pipeline(sp, load, n_exp, 0, 0)

            @block.gpsimd
            def _(pool):
                pool.wait_ge(s["rstd_step"], 1)
                nc.gpsimd.tensor_tensor(self.rstd[:], self.rstd[:], self.half[:], ALU.pow).then_inc(s["rstd_step"], 1)
                pool.wait_ge(s["rstd_step"], 2)

            @block.tensor
            def _(pe):
                def step(un, has):
                    ahead, here, behind = has(2), has(0), has(-1)
                    n, a, c = un.n, un.shifted(2), un.shifted(-1)
                    if behind and out_proj:
                        pe.wait_ge(s["att_step"], 2 * c.n + 2)
                        for j in range(DC):
                            mm = nc.tensor.transpose(ps_o[:, j * P:(j + 1) * P],
                                                     att[:].rearrange("p h d -> p (h d)")[:, j * P:(j + 1) * P], self.ident[:])
                        mm.then_inc(s["att_turned"], 1)
                    if here:
                        pe.wait_ge(s["probs_ready"], n + 1)
                        for r in range(2):
                            pe.wait_ge(s["pt_ready_act" if r == 0 else "pt_ready_dve"], 2 * n + 1)
                            for h in range(HQ):
                                mm = nc.tensor.transpose(ps_t[0:KEYS, r, h * P:(h + 1) * P], probs[:, un.u, HQ * r + h, :], self.ident[:])
                            mm.then_inc(s["turned"], 1)
                    if ahead:
                        pe.wait_ge(s["xn_ready"], a.n + 1)
                        pe.wait_ge(s["q_t_ready"], 2 * a.n + 1)
                        for j in range(DC):
                            mm = nc.tensor.transpose(ps_xt[:, j * P:(j + 1) * P], xn[:, a.u, j * P:(j + 1) * P], self.ident[:])
                        mm.then_inc(s["xt_done"], 1)
                    if behind and out_proj:
                        pe.wait_ge(s["att_t_ready"], c.n + 1)
                        for j in range(DC):
                            nc.tensor.matmul(ps_o[:, 0:D], att_t[:, j, :], wo[:, j, :], start=(j == 0), stop=False)
                        nc.tensor.matmul(ps_o[:, 0:D], self.ones_row[:], bo[:], start=False, stop=True).then_inc(s["proj_done"], 1)
                    if here:
                        for r in range(2, 4):
                            pe.wait_ge(s["pt_ready_act" if r == 2 else "pt_ready_dve"], 2 * n + 2)
                            for h in range(HQ):
                                mm = nc.tensor.transpose(ps_t[0:KEYS, r - 2, h * P:(h + 1) * P], probs[:, un.u, HQ * r + h, :], self.ident[:])
                            mm.then_inc(s["turned"], 1)
                    if ahead:
                        pe.wait_ge(s["xn_t_ready"], a.n + 1)
                        for j in range(DC):
                            for c_ in range(DC):
                                mm = nc.tensor.matmul(ps_q[:, j * P:(j + 1) * P], wq[:, c_, j * P:(j + 1) * P], xn_t[:, a.u, c_, :],
                                                      start=(c_ == 0), stop=(c_ == DC - 1))
                        mm.then_inc(s["q_done"], 1)
                    if here:
                        pe.wait_ge(s["x_updated"], n + 1)
                        for r in range(NQ):
                            pe.wait_ge(s["pt_ready_act" if r % 2 == 0 else "pt_ready_dve"], 2 * n + 2 + r // 2)
                            for h in range(HQ):
                                mm = nc.tensor.matmul(ps_av[:, HQ * r + h, :], probs_t[:, r, h, :], vals[:, un.u, HQ * r + h, :],
                                                      start=True, stop=True)
                            mm.then_inc(s["av_done"], 1)
                    if ahead:
                        pe.wait_ge(s["q_t_ready"], 2 * a.n + 3)
                        pe.wait_ge(s["shifted"], a.n + 1)
                        for q in range(NQ):
                            nc.tensor.matmul(ps_s[:, q, 0:HQ * KEYS], q_t[:, a.u, q // 2, :],
                                             keys_bd[:, a.u, q].rearrange("p h k -> p (h k)"), start=True, stop=False)
                            mm = nc.tensor.matmul(ps_s[:, q, 0:HQ * KEYS], self.ones_bf[0:1, :],
                                                  mask_row[:, a.u].rearrange("p h k -> p (h k)"), start=False, stop=True)
                        mm.then_inc(s["scores_done"], 1)

                run_pipeline(pe, step, NT, 2, 1)

            @block.scalar
            def _(act):
                act.sem_inc(s["q_t_ready"], 1)
                act.sem_inc(s["pt_ready_act"], 1)

                def weight_high(pieces):
                    for e, m in pieces:
                        act.wait_ge(s_stage[m], 16 * e + 16)
                        nc.scalar.activation(self.weights[:, bass.ds(e, 1), 0, m * WPART:(m + 1) * WPART].rearrange("p a n -> p (a n)"),
                                             stage[:, m, :], ACT.Copy, scale=WSCALE).then_inc(s["w_high"], 1)

                def step(un, has):
                    ahead, here, behind = has(2), has(0), has(-1)
                    n, a, c = un.n, un.shifted(2), un.shifted(-1)
                    if behind and out_proj:
                        act.wait_ge(s["att_turned"], c.n + 1)
                        nc.scalar.copy(att_t[:].rearrange("p c t -> p (c t)"), ps_o[:, 0:D]).then_inc(s["att_t_ready"], 1)
                    if here:
                        act.wait_ge(s["turned"], 4 * n + 1)
                        nc.scalar.copy(probs_t[:, 0].rearrange("k h t -> k (h t)"), ps_t[0:KEYS, 0, :]).then_inc(s["pt_ready_act"], 1)
                    if ahead:
                        act.wait_ge(s["xt_done"], a.n + 1)
                        nc.scalar.copy(xn_t[:, a.u].rearrange("p c t -> p (c t)"), ps_xt).then_inc(s["xn_t_ready"], 1)
                    if here:
                        act.wait_ge(s["turned"], 4 * n + 3)
                        nc.scalar.copy(probs_t[:, 2].rearrange("k h t -> k (h t)"), ps_t[0:KEYS, 0, :]).then_inc(s["pt_ready_act"], 1)
                    if ahead:
                        act.wait_ge(s["q_done"], a.n + 1)
                        for j in range(DC):
                            nc.scalar.activation(q_t[:, a.u, j, :], ps_q[:, j * P:(j + 1) * P], ACT.Identity,
                                                 bias=bq[:, j:j + 1]).then_inc(s["q_t_ready"], 1)
                        act.wait_ge(s["shifted"], a.n + 2)
                        nc.scalar.activation(probs[:, a.u].rearrange("p h k -> p (h k)"), probs[:, a.u].rearrange("p h k -> p (h k)"),
                                             ACT.Exp, scale=float(HD) ** -0.5).then_inc(s["probs_ready"], 1)
                    if here:
                        weight_high(pieces(un))

                run_pipeline(act, step, NT, 2, 1)
                weight_high([(e, m) for e in range(per_unit * NT // 2, n_exp) for m in range(2)])

            @block.vector
            def _(dve):
                dve.sem_inc(s["x_updated"], 1)
                dve.sem_inc(s["shifted"], 1)
                dve.sem_inc(s["pt_ready_dve"], 1)
                dve.sem_inc(s["w_low"], 2)

                def weight_low(pieces):
                    for e, m in pieces:
                        dve.wait_ge(s["w_high"], e * 2 + m + 1)
                        high, low = (self.weights[:, bass.ds(e, 1), w, m * WPART:(m + 1) * WPART].rearrange("p a n -> p (a n)") for w in (0, 1))
                        nc.vector.scalar_tensor_tensor(out=low, in0=stage[:, m, :], scalar=WSCALE, in1=high,
                                                       op0=ALU.mult, op1=ALU.subtract).then_inc(s["w_low"], 1)

                def update(c):
                    row = self.x[:, bass.ds(tile_of(c), 1), :].rearrange("p a d -> p (a d)")
                    if out_proj:
                        dve.wait_ge(s["proj_done"], c.n + 1)
                    branch = ps_o[:, 0:D] if out_proj else att[:].rearrange("p h d -> p (h d)")
                    nc.vector.scalar_tensor_tensor(out=x_new[:], in0=branch, scalar=self.tg[:, 2 * L:2 * L + 1],
                                                   in1=row, op0=ALU.mult, op1=ALU.add).then_inc(s["x_updated"], 1)
                    self.keep_row(dve, s["x_updated"], c.n + 2, s["stats_step"], 3 * c.n, x_new, row, stats, mv1, tile_of(c))

                def step(un, has):
                    ahead, here, behind = has(2), has(0), has(-1)
                    n, a, c = un.n, un.shifted(2), un.shifted(-1)
                    if ahead:
                        T = tile_of(a)
                        if not (isinstance(n, int) and n < 0):
                            dve.wait_ge(s["xt_done"], n + 1)
                        nc.vector.tensor_scalar(xn[:, a.u, :], self.x[:, bass.ds(T, 1), :].rearrange("p a d -> p (a d)"),
                                                self.mv[:, bass.ds(T, 1), 0], self.rstd[:, bass.ds(T, 1)],
                                                ALU.subtract, ALU.mult).then_inc(s["xn_ready"], 1)
                    if here:
                        dve.wait_ge(s["turned"], 4 * n + 2)
                        nc.vector.tensor_copy(probs_t[:, 1].rearrange("k h t -> k (h t)"), ps_t[0:KEYS, 1, :]).then_inc(s["pt_ready_dve"], 1)
                    if behind and out_proj:
                        update(c)
                    if here:
                        dve.wait_ge(s["turned"], 4 * n + 4)
                        nc.vector.tensor_copy(probs_t[:, 3].rearrange("k h t -> k (h t)"), ps_t[0:KEYS, 1, :]).then_inc(s["pt_ready_dve"], 1)
                        dve.wait_ge(s["av_done"], 4 * n + 4)
                        nc.vector.reciprocal(rec[:], ps_av[:, :, HD:HD + 1]).then_inc(s["att_step"], 1)
                        dve.wait_ge(s["att_step"], 2 * n + 1)
                        nc.vector.tensor_tensor(att[:], ps_av[:, :, 0:HD], rec[:].broadcast_to([P, HEADS, HD]),
                                                ALU.mult).then_inc(s["att_step"], 1)
                        if not out_proj:
                            dve.wait_ge(s["att_step"], 2 * n + 2)
                            update(un)
                    if ahead:
                        dve.wait_ge(s["scores_done"], a.n + 1)
                        sc = ps_s[:, :, 0:HQ * KEYS].rearrange("p q (h k) -> p q h k", h=HQ)
                        nc.vector.tensor_reduce(smax[:, a.u], sc, AX_X, ALU.max).then_inc(s["smax_step"], 1)
                        dve.wait_ge(s["smax_step"], a.n + 1)
                        nc.vector.tensor_tensor(probs[:, a.u].rearrange("p (q h) k -> p q h k", q=NQ), sc,
                                                smax[:, a.u].unsqueeze(3).broadcast_to([P, NQ, HQ, KEYS]),
                                                ALU.subtract).then_inc(s["shifted"], 1)
                    if here:
                        weight_low(pieces(un))

                run_pipeline(dve, step, NT, 2, 1)
                weight_low([(e, m) for e in range(per_unit * NT // 2, n_exp) for m in range(2)])
                dve.wait_ge(s["stats_step"], 3 * NT)
                nc.vector.tensor_scalar(self.rstd[:], self.mv[:, :, 1], EPS, None, ALU.add).then_inc(s["rstd_step"], 1)

    def route(self, L):
        nc, cfg, ins = self.nc, LAYERS[L], self.ins
        E, K, shared = cfg["experts"], cfg["topk"], cfg["shared"]
        R = routed_tiles(L)
        pre = f"l{L}_"
        sem = lambda name: self.sem(pre + name)
        self.layer_ctx = ExitStack()
        keep = lambda name, shape, dt: self.layer_ctx.enter_context(nc.sbuf_tensor(pre + name, shape, dt))
        self.xn = keep("xn_all", [P, NT, D], F32)
        self.slots = keep("slots", [P, NT, K], I32)
        self.gate = keep("gate", [P, NT, K], F32)
        with ExitStack() as tmp:
            sb = lambda name, shape, dt: tmp.enter_context(nc.sbuf_tensor(pre + name, shape, dt))
            psb = lambda name, shape: tmp.enter_context(nc.psum_tensor(pre + name, shape, F32))
            wg, bg = sb("wg", [P, DC, E], F32), sb("bg_row", [1, E], F32)
            xn, xn_t = sb("r_xn", [P, 2, D], F32), sb("r_xn_t", [P, 2, DC, P], F32)
            logits = sb("logits", [P, NT, E], F32)
            ps_xt, ps_l = psb("r_ps_xt", [P, 2, 512]), psb("r_ps_l", [P, 2, 512])
            s = {n: sem("r_" + n) for n in ("params", "xn_ready", "turned", "xn_t_ready", "logits_done", "logits_kept")}
            s_row = [sem("r_rows_stored0"), sem("r_rows_stored1")]

            with nc.Block() as block:
                @block.sync
                def _(sp):
                    sp.dma_start(wg[:], ins[f"wg{L}"].rearrange("(c p) e -> p c e", p=P)).then_inc(s["params"], 16)
                    sp.dma_start(bg[:], ins[f"bg{L}"]).then_inc(s["params"], 16)
                    if shared:
                        def rows(t, has):
                            sp.wait_ge(s["xn_ready"], t.n + 1)
                            for h in range(shared):
                                sp.dma_start(self.xg[bass.ds((h * NT + t.n) * P, P), :], xn[:, t.u, :]).then_inc(s_row[t.u], 16)

                        for u in range(2):
                            sp.sem_inc(s_row[u], 16 * shared)
                        run_pipeline(sp, rows, NT, 0, 0)
                        for u in range(2):
                            sp.wait_ge(s_row[u], 16 * shared * (NT // 2 + 1))

                @block.tensor
                def _(pe):
                    pe.wait_ge(s["params"], 32)

                    def step(t, has):
                        if has(1):
                            a = t.shifted(1)
                            pe.wait_ge(s["xn_ready"], a.n + 1)
                            for j in range(DC):
                                mm = nc.tensor.transpose(ps_xt[:, a.u, j * P:(j + 1) * P], xn[:, a.u, j * P:(j + 1) * P], self.ident[:])
                            mm.then_inc(s["turned"], 1)
                        if has(0):
                            pe.wait_ge(s["xn_t_ready"], t.n + 1)
                            pe.wait_ge(s["logits_kept"], t.n + 1)
                            for j in range(DC):
                                nc.tensor.matmul(ps_l[:, t.u, 0:E], xn_t[:, t.u, j, :], wg[:, j, :], start=(j == 0), stop=False)
                            nc.tensor.matmul(ps_l[:, t.u, 0:E], self.ones_row[:], bg[:], start=False, stop=True).then_inc(s["logits_done"], 1)

                    run_pipeline(pe, step, NT, 1, 0)

                @block.scalar
                def _(act):
                    def step(t, has):
                        act.wait_ge(s["turned"], t.n + 1)
                        nc.scalar.copy(xn_t[:, t.u].rearrange("p c t -> p (c t)"), ps_xt[:, t.u, 0:D]).then_inc(s["xn_t_ready"], 1)

                    run_pipeline(act, step, NT, 0, 0)

                @block.vector
                def _(dve):
                    dve.sem_inc(s["logits_kept"], 2)

                    def step(t, has):
                        if has(2):
                            a = t.shifted(2)
                            row = self.x[:, bass.ds(a.n, 1), :].rearrange("p a d -> p (a d)")
                            if not (isinstance(t.n, int) and t.n < 0):
                                dve.wait_ge(s["turned"], t.n + 1)
                                if shared:
                                    dve.wait_ge(s_row[t.u], 16 * shared * (t.i + 2))
                            for dst in (xn[:, a.u, :], self.xn[:, bass.ds(a.n, 1), :].rearrange("p a d -> p (a d)")):
                                ins_ = nc.vector.tensor_scalar(dst, row, self.mv[:, bass.ds(a.n, 1), 0], self.rstd[:, bass.ds(a.n, 1)],
                                                               ALU.subtract, ALU.mult)
                            ins_.then_inc(s["xn_ready"], 1)
                        if has(0):
                            dve.wait_ge(s["logits_done"], t.n + 1)
                            nc.vector.tensor_scalar(logits[:, bass.ds(t.n, 1), :].rearrange("p a e -> p (a e)"), ps_l[:, t.u, 0:E],
                                                    0.0, None, ALU.add).then_inc(s["logits_kept"], 1)

                    run_pipeline(dve, step, NT, 2, 0)

            iota_e, iota_n = sb("iota_e", [P, E], F32), sb("iota_n", [1, R], F32)
            mx, den = sb("mx", [P, NT], F32), sb("den", [P, NT], F32)
            prob = sb("prob", [P, NT, E], F32)
            top8, idx8 = sb("top8", [P, NT, 8], F32), sb("idx8", [P, NT, 8], mybir.dt.uint32)
            idx_f = sb("idx_f", [P, NT, 8], F32)
            chosen = sb("chosen", [P, K, NT, E], F32)
            mask = sb("mask", [P, NT, E], BF16)
            tot_i, tiles, zero_e = sb("tot_i", [P, E], I32), sb("tiles", [P, E], F32), sb("zero_e", [P, E], F32)
            ends, first = sb("ends", [P, E], F32), sb("first_slot", [P, E], F32)
            slot_of, pick = sb("slot_of", [P, NT, E], F32), sb("pick", [P, NT, E], F32)
            slot_f = sb("slot_f", [P, NT, K], F32)
            past = sb("past", [1, R, E], F32)
            eid_f = sb("eid_f", [1, SLOT_TILES], F32)
            ps_rank, ps_tot = psb("ps_rank", [P, 512]), psb("ps_tot", [P, 512])
            q = {n: sem("q_" + n) for n in ("shifted", "exp", "mask", "rank", "iota", "step")}
            bc = lambda ap: ap.unsqueeze(2).broadcast_to([P, NT, E])

            with nc.Block() as block:
                @block.gpsimd
                def _(pool):
                    nc.gpsimd.iota(iota_e[:], pattern=[[1, E]], base=0, channel_multiplier=0,
                                   allow_small_or_imprecise_dtypes=True).then_inc(q["iota"], 1)
                    nc.gpsimd.iota(iota_n[:], pattern=[[1, R]], base=0, channel_multiplier=0,
                                   allow_small_or_imprecise_dtypes=True).then_inc(q["iota"], 1)
                    nc.gpsimd.memset(zero_e[:], 0.0).then_inc(q["iota"], 1)

                @block.scalar
                def _(act):
                    act.wait_ge(q["shifted"], 1)
                    nc.scalar.activation(prob[:], prob[:], ACT.Exp, scale=cfg["inv_temp"]).then_inc(q["exp"], 1)

                @block.tensor
                def _(pe):
                    pe.wait_ge(q["mask"], 1)
                    flat = lambda ap: ap.rearrange("p t e -> p (t e)")
                    ranks = ps_rank[:, 0:NT * E].rearrange("p (t e) -> p t e", t=NT)
                    nc.tensor.matmul(ps_rank[:, 0:NT * E], self.before[:], flat(mask[:]), start=True, stop=False)
                    for t in range(NT - 1):
                        nc.tensor.matmul(ranks[:, t + 1:, :], self.ones_bf[:],
                                         mask[:, t:t + 1, :].broadcast_to([P, NT - 1 - t, E]), start=False, stop=(t == NT - 2))
                    for t in range(NT):
                        mm = nc.tensor.matmul(ps_tot[:, 0:E], self.ones_bf[:], mask[:, t, :], start=(t == 0), stop=(t == NT - 1))
                    mm.then_inc(q["rank"], 1)

                @block.vector
                def _(dve):
                    v, step = nc.vector, Chain(dve, q["step"])
                    step(v.tensor_reduce(mx[:], logits[:], AX_X, ALU.max))
                    v.tensor_tensor(prob[:], logits[:], bc(mx[:]), ALU.subtract).then_inc(q["shifted"], 1)
                    dve.wait_ge(q["exp"], 1)
                    step(v.tensor_reduce(den[:], prob[:], AX_X, ALU.add))
                    step(v.reciprocal(den[:], den[:]))
                    step(v.tensor_tensor(prob[:], prob[:], bc(den[:]), ALU.mult))
                    for t in range(NT):
                        ins_ = v.max(out=top8[:, t, :], in_=prob[:, t, :])
                    step(ins_)
                    for t in range(NT):
                        ins_ = v.max_index(out=idx8[:, t, :], in_max=top8[:, t, :], in_values=prob[:, t, :])
                    step(ins_)
                    step(v.tensor_copy(idx_f[:], idx8[:]))
                    dve.wait_ge(q["iota"], 3)
                    for j in range(K):
                        ins_ = v.tensor_tensor(chosen[:, j], bc(idx_f[:, :, j]), iota_e[:].unsqueeze(1).broadcast_to([P, NT, E]), ALU.is_equal)
                    step(ins_)
                    for j in range(1, K):
                        last = j == K - 1
                        ins_ = v.tensor_tensor(mask[:] if last else pick[:], chosen[:, 0] if j == 1 else pick[:], chosen[:, j], ALU.add)
                        if not last:
                            step(ins_)
                    ins_.then_inc(q["mask"], 1)
                    if cfg["renorm"]:
                        step(v.tensor_reduce(den[:], top8[:, :, 0:K], AX_X, ALU.add))
                        step(v.tensor_scalar(den[:], den[:], 1e-9, None, ALU.add))
                        step(v.reciprocal(den[:], den[:]))
                        step(v.tensor_tensor(self.gate[:], top8[:, :, 0:K], den[:].unsqueeze(2).broadcast_to([P, NT, K]), ALU.mult))
                    else:
                        step(v.tensor_copy(self.gate[:], top8[:, :, 0:K]))
                    dve.wait_ge(q["rank"], 1)
                    step(v.tensor_scalar(tot_i[:], ps_tot[:, 0:E], float(P - 1), None, ALU.add))
                    step(v.tensor_scalar(tot_i[:], tot_i[:], P.bit_length() - 1, None, ALU.logical_shift_right))
                    step(v.tensor_copy(tiles[:], tot_i[:]))
                    step(v.tensor_tensor_scan(ends[:], tiles[:], zero_e[:], 0.0, ALU.add, ALU.add))
                    step(v.tensor_tensor(first[:], ends[:], tiles[:], ALU.subtract))
                    step(v.tensor_scalar(first[:], first[:], float(shared * NT), float(P), ALU.add, ALU.mult))
                    step(v.tensor_tensor(slot_of[:], ps_rank[:, 0:NT * E].rearrange("p (t e) -> p t e", t=NT),
                                         first[:].unsqueeze(1).broadcast_to([P, NT, E]), ALU.add))
                    for j in range(K):
                        step(v.tensor_tensor(pick[:], slot_of[:], chosen[:, j], ALU.mult))
                        step(v.tensor_reduce(slot_f[:, :, j], pick[:], AX_X, ALU.add))
                    step(v.tensor_copy(self.slots[:], slot_f[:]))
                    step(v.tensor_tensor(past[:], iota_n[:].unsqueeze(2).broadcast_to([1, R, E]),
                                         ends[0:1, :].unsqueeze(1).broadcast_to([1, R, E]), ALU.is_ge))
                    n0 = shared * NT
                    for h in range(shared):
                        step(v.memset(eid_f[:, h * NT:(h + 1) * NT], float(E + h)))
                    step(v.tensor_reduce(eid_f[:, n0:n0 + R], past[:], AX_X, ALU.add))
                    step(v.tensor_scalar(eid_f[:, n0:n0 + R], eid_f[:, n0:n0 + R], float(E - 1), None, ALU.min))
                    step(v.tensor_copy(self.eid[:, 0:n0 + R], eid_f[:, 0:n0 + R]))

    def experts(self, L):
        nc, cfg = self.nc, LAYERS[L]
        K, shared = cfg["topk"], cfg["shared"]
        n_exp = cfg["experts"] + shared
        N = shared * NT + routed_tiles(L)
        pre = f"l{L}_e_"
        sem = lambda name: self.sem(pre + name)
        with ExitStack() as tmp:
            sb = lambda name, shape, dt: tmp.enter_context(nc.sbuf_tensor(pre + name, shape, dt))
            psb = lambda name, shape: tmp.enter_context(nc.psum_tensor(pre + name, shape, F32))
            xin = sb("xin", [P, 2, D], F32)
            xh, xl = sb("xh", [P, 2, DC, P], F16), sb("xl", [P, 2, DC, P], F16)
            b1, b2 = sb("b1", [2, 2, HID], F16), sb("b2", [2, 2, D], F16)
            h = sb("h", [P, 2, HID], F32)
            hh, hl = sb("hh", [P, 2, HC, P], F16), sb("hl", [P, 2, HC, P], F16)
            y = sb("y", [P, 2, D], F32)
            ps_x, ps_h, ps_t, ps_y = psb("ps_x", [P, 2, 512]), psb("ps_h", [P, HID]), psb("ps_t", [P, HID]), psb("ps_y", [P, 2, 512])
            s = {n: sem(n) for n in ("scattered", "x_turned", "xh_ready", "xl_ready", "h_done", "h_ready", "h_turned",
                                     "hh_ready", "hl_ready", "y_done", "y_ready")}
            s_x, s_b1, s_b2, s_y = ([sem(f"{n}{u}") for u in range(2)] for n in ("x_in", "b1_in", "b2_in", "y_stored"))
            block = tmp.enter_context(nc.Block())

            @block.gpsimd
            def _(pool):
                for t in range(NT):
                    for j in range(K):
                        nc.gpsimd.indirect_dma_start(self.xg, bass.IndirectOffsetOnAxis(ap=self.slots[:, t, j:j + 1], axis=0),
                                                     self.xn[:, t, :], None).then_inc(s["scattered"], 16)
                pool.wait_ge(s["scattered"], 16 * NT * K)

            @block.sync
            def _(sp):
                for u in range(2):
                    sp.sem_inc(s_y[u], 16)

                def expert(m):
                    return sp.value_load(self.eid[0:1, bass.ds(m.n, 1)], min_val=0, max_val=n_exp - 1)

                def step(t, has):
                    if has(4):
                        m = t.shifted(4)
                        sp.wait_ge(s["x_turned"], m.n + 1)
                        sp.dma_start(xin[:, m.u, :], self.xg[bass.ds(m.n * P, P), :]).then_inc(s_x[m.u], 16)
                    if has(3):
                        m = t.shifted(3)
                        e = expert(m)
                        sp.wait_ge(s["h_done"], m.n + 1)
                        sp.dma_start(b1[:, m.u, :], self.bg[bass.ds(e, 1), :, 0:HID].rearrange("e r n -> (e r) n")).then_inc(s_b1[m.u], 16)
                    if has(2):
                        m = t.shifted(2)
                        e = expert(m)
                        sp.wait_ge(s["y_done"], m.n + 1)
                        sp.dma_start(b2[:, m.u, :], self.bg[bass.ds(e, 1), :, HID:BCOLS].rearrange("e r n -> (e r) n")).then_inc(s_b2[m.u], 16)
                    if has(0):
                        sp.wait_ge(s["y_ready"], t.n + 3)
                        sp.dma_start(self.yg[bass.ds(t.n * P, P), :], y[:, t.u, :]).then_inc(s_y[t.u], 16)

                run_pipeline(sp, step, N, 4, 0, pause=shared * NT - 4,
                             at_pause=lambda: sp.wait_ge(s["scattered"], 16 * NT * K))
                for u in range(2):
                    sp.wait_ge(s_y[u], 16 * ((N + 1 - u) // 2) + 16)

            @block.tensor
            def _(pe):
                pe.sem_inc(s["x_turned"], 2)
                pe.sem_inc(s["h_done"], 2)
                pe.sem_inc(s["y_done"], 2)

                def weight(e, part, a, n):
                    return self.weights[:, bass.ds(e, 1), part, a:a + n].rearrange("p e n -> p (e n)")

                def step(t, has):
                    if has(0):
                        pe.wait_ge(s["h_ready"], t.n + 1)
                        for c in range(HC):
                            mm = nc.tensor.transpose(ps_t[:, c * P:(c + 1) * P], h[:, t.u, c * P:(c + 1) * P], self.ident[:])
                        mm.then_inc(s["h_turned"], 1)
                    if has(2):
                        m = t.shifted(2)
                        pe.wait_ge(s_x[m.u], 16 * m.i + 16)
                        for c in range(DC):
                            mm = nc.tensor.transpose(ps_x[:, m.u, c * P:(c + 1) * P], xin[:, m.u, c * P:(c + 1) * P], self.ident[:])
                        mm.then_inc(s["x_turned"], 1)
                    if has(1):
                        m = t.shifted(1)
                        e = pe.value_load(self.eid[0:1, bass.ds(m.n, 1)], min_val=0, max_val=n_exp - 1)
                        pe.wait_ge(s["xl_ready"], m.n + 1)
                        for c in range(DC):
                            for part, w in ((xh, 0), (xh, 1), (xl, 0)):
                                nc.tensor.matmul(ps_h[:], part[:, m.u, c, :], weight(e, w, c * HID, HID),
                                                 start=(c == 0 and part is xh and w == 0), stop=False)
                        pe.wait_ge(s_b1[m.u], 16 * m.i + 16)
                        nc.tensor.matmul(ps_h[:], self.ones16[:], b1[:, m.u, :], start=False, stop=True).then_inc(s["h_done"], 1)
                    if has(0):
                        e = pe.value_load(self.eid[0:1, bass.ds(t.n, 1)], min_val=0, max_val=n_exp - 1)
                        pe.wait_ge(s["hl_ready"], t.n + 1)
                        pe.wait_ge(s["y_ready"], t.n + 1)
                        for c in range(HC):
                            for part, w in ((hh, 0), (hh, 1), (hl, 0)):
                                nc.tensor.matmul(ps_y[:, t.u, 0:D], part[:, t.u, c, :], weight(e, w, DC * HID + c * D, D),
                                                 start=(c == 0 and part is hh and w == 0), stop=False)
                        pe.wait_ge(s_b2[t.u], 16 * t.i + 16)
                        nc.tensor.matmul(ps_y[:, t.u, 0:D], self.ones16[:], b2[:, t.u, :], start=False, stop=True).then_inc(s["y_done"], 1)

                run_pipeline(pe, step, N, 2, 0)

            @block.scalar
            def _(act):
                def step(t, has):
                    if has(0):
                        act.wait_ge(s["h_turned"], t.n + 1)
                        nc.scalar.copy(hh[:, t.u].rearrange("p c t -> p (c t)"), ps_t[:]).then_inc(s["hh_ready"], 1)
                    if has(2):
                        m = t.shifted(2)
                        act.wait_ge(s["x_turned"], m.n + 3)
                        nc.scalar.copy(xh[:, m.u].rearrange("p c t -> p (c t)"), ps_x[:, m.u, 0:D]).then_inc(s["xh_ready"], 1)
                    if has(1):
                        m = t.shifted(1)
                        act.wait_ge(s["h_done"], m.n + 3)
                        nc.scalar.activation(h[:, m.u, :], ps_h[:], ACT.Gelu, scale=1.0 / WSCALE).then_inc(s["h_ready"], 1)

                run_pipeline(act, step, N, 2, 0)

            @block.vector
            def _(dve):
                dve.sem_inc(s["y_ready"], 2)

                def step(t, has):
                    if has(0):
                        dve.wait_ge(s["hh_ready"], t.n + 1)
                        nc.vector.tensor_tensor(hl[:, t.u].rearrange("p c t -> p (c t)"), ps_t[:], hh[:, t.u].rearrange("p c t -> p (c t)"),
                                                ALU.subtract).then_inc(s["hl_ready"], 1)
                    if has(2):
                        m = t.shifted(2)
                        dve.wait_ge(s["xh_ready"], m.n + 1)
                        nc.vector.tensor_tensor(xl[:, m.u].rearrange("p c t -> p (c t)"), ps_x[:, m.u, 0:D],
                                                xh[:, m.u].rearrange("p c t -> p (c t)"), ALU.subtract).then_inc(s["xl_ready"], 1)
                    if has(0):
                        dve.wait_ge(s["y_done"], t.n + 3)
                        dve.wait_ge(s_y[t.u], 16 * t.i + 16)
                        nc.vector.tensor_scalar(y[:, t.u, :], ps_y[:, t.u, 0:D], 1.0 / WSCALE, None, ALU.mult).then_inc(s["y_ready"], 1)

                run_pipeline(dve, step, N, 2, 0)

    def combine(self, L):
        nc, cfg = self.nc, LAYERS[L]
        K, shared = cfg["topk"], cfg["shared"]
        pre = f"l{L}_c_"
        sem = lambda name: self.sem(pre + name)
        with ExitStack() as tmp:
            sb = lambda name, shape, dt: tmp.enter_context(nc.sbuf_tensor(pre + name, shape, dt))
            yr = sb("y_routed", [P, 2, K, D], F32)
            ys = sb("y_shared", [P, 2, shared, D], F32) if shared else None
            acc = sb("acc", [P, D], F32)
            stats, mv1, x_new = sb("stats", [P, 6], F32), sb("mv1", [P, 2], F32), sb("x_new", [P, D], F32)
            s = {n: sem(n) for n in ("acc_step", "used", "kept", "rstd_step", "stats_step")}
            s_r, s_s = [sem("gathered0"), sem("gathered1")], [sem("shared_in0"), sem("shared_in1")]
            n_acc = K + (shared if shared else 0)
            block = tmp.enter_context(nc.Block())

            @block.gpsimd
            def _(pool):
                for t in range(NT):
                    pool.wait_ge(s["used"], t + 1)
                    for j in range(K):
                        nc.gpsimd.indirect_dma_start(yr[:, t % 2, j, :], None, self.yg,
                                                     bass.IndirectOffsetOnAxis(ap=self.slots[:, t, j:j + 1], axis=0)).then_inc(s_r[t % 2], 16)
                pool.wait_ge(s["rstd_step"], 1)
                nc.gpsimd.tensor_tensor(self.rstd[:], self.rstd[:], self.half[:], ALU.pow).then_inc(s["rstd_step"], 1)
                pool.wait_ge(s["rstd_step"], 2)

            @block.sync
            def _(sp):
                if shared:
                    def load(t, has):
                        sp.wait_ge(s["used"], t.n + 1)
                        for q in range(shared):
                            sp.dma_start(ys[:, t.u, q, :], self.yg[bass.ds((q * NT + t.n) * P, P), :]).then_inc(s_s[t.u], 16)

                    run_pipeline(sp, load, NT, 0, 0)

            @block.vector
            def _(dve):
                dve.sem_inc(s["used"], 2)

                def step(t, has):
                    one = lambda ap: ap.rearrange("p a d -> p (a d)")
                    row, xn = one(self.x[:, bass.ds(t.n, 1), :]), one(self.xn[:, bass.ds(t.n, 1), :])
                    done = 0

                    def link(ins_):
                        nonlocal done
                        done += 1
                        ins_.then_inc(s["acc_step"], 1)
                        dve.wait_ge(s["acc_step"], t.n * n_acc + done)

                    if shared:
                        dve.wait_ge(s_s[t.u], 16 * shared * (t.i + 1))
                        link(nc.vector.tensor_tensor(acc[:], xn, ys[:, t.u, 0, :], ALU.add))
                        link(nc.vector.tensor_tensor(acc[:], acc[:], ys[:, t.u, 1, :], ALU.add))
                    dve.wait_ge(s_r[t.u], 16 * K * (t.i + 1))
                    for j in range(K):
                        g = self.gate[:, bass.ds(t.n, 1), j]
                        if j == 0 and not shared:
                            link(nc.vector.tensor_scalar(acc[:], yr[:, t.u, j, :], g, None, ALU.mult))
                        else:
                            link(nc.vector.scalar_tensor_tensor(out=acc[:], in0=yr[:, t.u, j, :], scalar=g, in1=acc[:],
                                                                op0=ALU.mult, op1=ALU.add))
                    nc.vector.scalar_tensor_tensor(out=x_new[:], in0=acc[:], scalar=self.tg[:, 2 * L + 1:2 * L + 2], in1=row,
                                                   op0=ALU.mult, op1=ALU.add).then_inc(s["used"], 1)
                    self.keep_row(dve, s["used"], t.n + 3, s["stats_step"], 3 * t.n, x_new, row, stats, mv1, t.n)

                run_pipeline(dve, step, NT, 0, 0)
                dve.wait_ge(s["stats_step"], 3 * NT)
                nc.vector.tensor_scalar(self.rstd[:], self.mv[:, :, 1], EPS, None, ALU.add).then_inc(s["rstd_step"], 1)
        self.layer_ctx.close()


def flamingo_layers(nc, ins, out):
    with ExitStack() as ctx:
        b = Build(nc, ctx, ins, out)
        b.start()
        for L in range(len(LAYERS)):
            b.attention(L)
            if STOP == ("attention", L):
                b.store()
                return
            b.route(L)
            b.experts(L)
            b.combine(L)
            b.recycle_semaphores()
            if STOP == ("combine", L):
                b.store()
                return
        b.store()


def laid_out(v):
    rows = lambda w: np.ascontiguousarray(w)
    cols = lambda b: np.ascontiguousarray(b.reshape(DC, P).T)
    ctx = v["ctx_1024"].reshape(B * KEYS, D)

    def experts(w1, w2):
        e = w1.shape[0]
        a = w1.reshape(e, DC, P, HID).transpose(0, 2, 1, 3).reshape(e, P, DC * HID)
        b = w2.reshape(e, HC, P, D).transpose(0, 2, 1, 3).reshape(e, P, HC * D)
        return np.ascontiguousarray(np.concatenate([a, b], axis=2))

    sw1 = v["L0_ffn_sW1"].reshape(D, 2, HID).transpose(1, 0, 2)
    sw2 = v["L0_ffn_sW2"].reshape(2, HID, D)
    sb1 = v["L0_ffn_sb1"].reshape(2, HID)
    sb2 = np.concatenate([v["L0_ffn_sb2"], np.zeros((1, D), np.float32)], axis=0)
    return {
        "x": rows(v["x"].reshape(B * S, D)),
        "ctx_t": rows(ctx.T),
        "gates": rows(np.broadcast_to(np.stack([v["g_xattn"][0], v["g_ffn"][0], v["g_xattn"][1], v["g_ffn"][1]]), (P, 4))),
        "mask0": rows(v["mask_Bx1x1xS2_bf1"].reshape(1, B * KEYS).view(np.uint8)),
        "mask1": rows(v["mask_BxS2_ik0"].reshape(1, B * KEYS)),
        "wq0": rows(v["L0_xattn_Wq"]), "wk0": rows(v["L0_xattn_Wk"]), "wv0": rows(v["L0_xattn_Wv"]), "wo0": rows(v["L0_xattn_Wo"]),
        "bq0": cols(v["L0_xattn_bq"]), "bk0": cols(v["L0_xattn_bk"]), "bv0": rows(v["L0_xattn_bv"][None]), "bo0": rows(v["L0_xattn_bo"][None]),
        "wq1": rows(v["L1_xattn_q_w"].T), "wk1": rows(v["L1_xattn_k_w"].T), "wv1": rows(v["L1_xattn_v_w"].T),
        "bq1": cols(v["L1_xattn_q_b"]), "bk1": cols(v["L1_xattn_k_b"]), "bv1": rows(v["L1_xattn_v_b"][None]),
        "weights0": experts(np.concatenate([v["L0_ffn_rW1"], sw1]), np.concatenate([v["L0_ffn_rW2"], sw2])),
        "biases0": rows(np.concatenate([np.concatenate([v["L0_ffn_rb1"], sb1]), np.concatenate([v["L0_ffn_rb2"], sb2])], axis=1)),
        "weights1": experts(v["L1_ffn_W1"], v["L1_ffn_W2"]),
        "biases1": rows(np.concatenate([v["L1_ffn_b1"], v["L1_ffn_b2"]], axis=1)),
        "wg0": rows(v["L0_ffn_gW"]), "bg0": rows(v["L0_ffn_gb"][None]),
        "wg1": rows(v["L1_ffn_Wg"]), "bg1": rows(v["L1_ffn_bg"][None]),
    }


STOP = None


def kernel(**inputs):
    import concourse.bacc as bacc
    from concourse.bass_utils import run_bass_kernel_spmd

    arrays = {f"in_{k}": a for k, a in laid_out({k: np.asarray(a) for k, a in inputs.items()}).items()}
    nc = bacc.Bacc("TRN2", target_bir_lowering=False, num_devices=1)
    ins = {k[3:]: nc.dram_tensor(k, a.shape, mybir.dt.from_np(a.dtype), kind="ExternalInput").ap() for k, a in arrays.items()}
    out = nc.dram_tensor("out", (B * S, D), F32, kind="ExternalOutput").ap()
    flamingo_layers(nc, ins, out)
    r = run_bass_kernel_spmd(nc, [arrays], core_ids=[0])
    return r.results[0]["out"].reshape(B, S, D)
```

```python
from contextlib import ExitStack

import numpy as np

import concourse.bass as bass
from concourse import mybir

F32 = mybir.dt.float32
F16 = mybir.dt.float16
BF16 = mybir.dt.bfloat16
I32 = mybir.dt.int32
U8 = mybir.dt.uint8
ACT = mybir.ActivationFunctionType
ALU = mybir.AluOpType
AX_X = mybir.AxisListType.X

P = 128
D = 256
DC = D // P
B = 2
S = 1024
NT = B * S // P
TB = NT // B
KEYS = 77
HEADS = 16
HD = D // HEADS
HQ = 4
NQ = HEADS // HQ
PROWS = HEADS * KEYS
PC = -(-PROWS // P)
VH = 3
PROUND = 4
HID = 512
HC = HID // P
WCOLS = DC * HID + HC * D
WPART = WCOLS // 2
BCOLS = HID + D
WSCALE = 16.0
MASKED = -1e30
EPS = 1e-5

LAYERS = [
    dict(experts=15, topk=3, shared=2, inv_temp=1.0, renorm=False, out_proj=True),
    dict(experts=8, topk=2, shared=0, inv_temp=1.0 / 5.0, renorm=True, out_proj=False),
]


def chunk_rows(c):
    return min(P, PROWS - c * P)


def chunk_heads(c):
    first, last = c * P // KEYS, (c * P + chunk_rows(c) - 1) // KEYS
    assert last - first < VH
    return first, last - first + 1


def routed_tiles(layer):
    c = LAYERS[layer]
    return (c["topk"] * NT * P + c["experts"] * (P - 1)) // P


MAXE = max(c["experts"] + c["shared"] for c in LAYERS)
SLOT_TILES = max(routed_tiles(n) + c["shared"] * NT for n, c in enumerate(LAYERS))


class Unit:

    def __init__(self, k, c):
        self.n = k * 2 + c
        self.u = c % 2
        self.i = k + c // 2
        self.c = c
        self.k = k

    def shifted(self, d):
        return Unit(self.k, self.c + d)


def run_pipeline(eng, step, n_units, lead, lag, pause=None, at_pause=None):
    lo, hi = lag, n_units - lead
    hi = lo + (hi - lo) // 2 * 2

    def peeled(n):
        if n == pause:
            at_pause()
        step(Unit(0, n), lambda d: 0 <= n + d < n_units)

    for n in range(-lead, lo):
        peeled(n)
    cuts = [lo, hi]
    if pause is not None and lo <= pause < hi:
        assert (pause - lo) % 2 == 0
        cuts = [lo, pause, hi]
    for start, end in zip(cuts, cuts[1:]):
        if start == pause:
            at_pause()
        if end > start:
            with eng.Fori(0, (end - start) // 2) as k:
                for c in (start, start + 1):
                    step(Unit(k, c), lambda d: True)
    for n in range(hi, n_units + lag):
        peeled(n)


class Chain:

    def __init__(self, eng, sem, base=0):
        self.eng, self.sem, self.base, self.n = eng, sem, base, 0

    def __call__(self, ins):
        self.n += 1
        ins.then_inc(self.sem, 1)
        self.eng.wait_ge(self.sem, self.base + self.n)


class Build:
    def __init__(self, nc, ctx, ins, out):
        self.nc, self.ctx, self.ins, self.out = nc, ctx, ins, out
        self.sems = []
        self.persistent()

    def sem(self, name):
        handle = self.nc.alloc_semaphore(name=name)
        self.sems.append(handle)
        return handle

    def recycle_semaphores(self):
        self.nc.all_engine_barrier()
        self.nc.clear_and_free_semaphores(self.sems)
        self.nc.all_engine_barrier()
        self.sems = []

    def sb(self, name, shape, dt):
        return self.ctx.enter_context(self.nc.sbuf_tensor(name, shape, dt))

    def persistent(self):
        nc, sb = self.nc, self.sb
        self.x = sb("x_all", [P, NT, D], F32)
        self.mv = sb("mean_var", [P, NT, 2], F32)
        self.rstd = sb("rstd", [P, NT], F32)
        self.ident = sb("ident", [P, P], F32)
        self.ones_row = sb("ones_row", [1, P], F32)
        self.ones_bf = sb("ones_bf", [P, P], BF16)
        self.before = sb("before", [P, P], BF16)
        self.ones16 = sb("ones16", [2, P], F16)
        self.gates_in = sb("gates_in", [P, 4], F32)
        self.tg = sb("tanh_gates", [P, 4], F32)
        self.head_mask = sb("head_mask", [P, 8], F32)
        self.row_head = sb("row_head", [P, PC, VH], F32)
        self.zeros16 = sb("zeros16", [1, D + HEADS], F16)
        self.half = sb("neg_half", [P, NT], F32)
        self.weights = sb("weights", [P, MAXE, 2, WCOLS], F16)
        self.eid = sb("expert_of_tile", [1, SLOT_TILES], I32)
        d = nc.dram_tensor
        self.xg = d("expert_rows_in", (SLOT_TILES * P, D), F32).ap()
        self.yg = d("expert_rows_out", (SLOT_TILES * P, D), F32).ap()
        self.bg = d("expert_biases", (MAXE, 2, BCOLS), F16).ap()

    def start(self):
        nc = self.nc
        with ExitStack() as tmp:
            zeros = tmp.enter_context(nc.sbuf_tensor("zeros", [P, 2 * D], F32))
            stats = tmp.enter_context(nc.sbuf_tensor("stats0", [P, NT, 6], F32))
            s_x, s_g, s_zero, s_fill = self.sem("x_loaded"), self.sem("gates_loaded"), self.sem("zero_ready"), self.sem("slots_filled")
            s_c, s_c2, s_v = self.sem("const_step"), self.sem("const_dve"), self.sem("stats0_step")
            block = tmp.enter_context(nc.Block())
            ins = self.ins

            @block.sync
            def _(sp):
                for q in range(4):
                    t0 = q * NT // 4
                    sp.dma_start(self.x[:, t0:t0 + NT // 4, :],
                                 ins["x"][t0 * P:(t0 + NT // 4) * P, :].rearrange("(t p) d -> p t d", p=P)).then_inc(s_x, 16)
                sp.dma_start(self.gates_in[:], ins["gates"]).then_inc(s_g, 16)
                sp.wait_ge(s_zero, 1)
                with sp.Fori(0, SLOT_TILES // 2) as t:
                    sp.dma_start(self.xg[bass.ds(t * (2 * P), 2 * P), :].rearrange("(a p) d -> p a d", p=P),
                                 zeros[:].rearrange("p (a d) -> p a d", a=2)).then_inc(s_fill, 16)
                if SLOT_TILES % 2:
                    sp.dma_start(self.xg[(SLOT_TILES - 1) * P:, :], zeros[:, 0:D]).then_inc(s_fill, 16)
                sp.wait_ge(s_fill, 16 * (SLOT_TILES // 2 + SLOT_TILES % 2))

            @block.gpsimd
            def _(pool):
                step = Chain(pool, s_c)
                nc.gpsimd.memset(zeros[:], 0.0).then_inc(s_zero, 1)
                step(nc.gpsimd.memset(self.ident[:], 0.0))
                step(nc.gpsimd.affine_select(out=self.ident[:], in_=self.ident[:], compare_op=ALU.not_equal, fill=1.0,
                                             base=0, pattern=[[-1, P]], channel_multiplier=1))
                step(nc.gpsimd.memset(self.ones_bf[:], 1.0))
                step(nc.gpsimd.affine_select(out=self.before[:], in_=self.ones_bf[:], compare_op=ALU.is_gt, fill=0.0,
                                             base=0, pattern=[[1, P]], channel_multiplier=-1))
                step(nc.gpsimd.memset(self.head_mask[:], 1.0))
                step(nc.gpsimd.affine_select(out=self.head_mask[:], in_=self.head_mask[:], compare_op=ALU.is_ge,
                                             fill=0.0, base=0, pattern=[[-HD, 8]], channel_multiplier=1))
                step(nc.gpsimd.affine_select(out=self.head_mask[:], in_=self.head_mask[:], compare_op=ALU.is_ge,
                                             fill=0.0, base=HD - 1, pattern=[[HD, 8]], channel_multiplier=-1))
                step(nc.gpsimd.memset(self.row_head[:], 1.0))
                for c in range(PC):
                    off = c * P - KEYS * chunk_heads(c)[0]
                    ins_ = nc.gpsimd.affine_select(out=self.row_head[:, c], in_=self.row_head[:, c], compare_op=ALU.is_ge, fill=0.0,
                                                   base=off, pattern=[[-KEYS, VH]], channel_multiplier=1)
                step(ins_)
                for c in range(PC):
                    off = c * P - KEYS * chunk_heads(c)[0]
                    ins_ = nc.gpsimd.affine_select(out=self.row_head[:, c], in_=self.row_head[:, c], compare_op=ALU.is_ge, fill=0.0,
                                                   base=KEYS - 1 - off, pattern=[[KEYS, VH]], channel_multiplier=-1)
                step(ins_)
                step(nc.gpsimd.memset(self.zeros16[:], 0.0))
                step(nc.gpsimd.memset(self.half[:], -0.5))
                step(nc.gpsimd.memset(self.ones_row[:], 1.0))
                step(nc.gpsimd.memset(self.ones16[:], 1.0))
                pool.wait_ge(s_v, 2 * NT + 1)
                step(nc.gpsimd.tensor_tensor(self.rstd[:], self.rstd[:], self.half[:], ALU.pow))

            @block.scalar
            def _(act):
                act.wait_ge(s_g, 16)
                nc.scalar.activation(self.tg[:], self.gates_in[:], ACT.Tanh).then_inc(s_c2, 1)
                act.wait_ge(s_c2, 1)

            @block.vector
            def _(dve):
                dve.wait_ge(s_x, 64)
                for t in range(NT):
                    nc.vector.bn_stats(stats[:, t, :], self.x[:, t, :]).then_inc(s_v, 1)
                dve.wait_ge(s_v, NT)
                for t in range(NT):
                    nc.vector.bn_aggr(self.mv[:, t, :], stats[:, t, :]).then_inc(s_v, 1)
                dve.wait_ge(s_v, 2 * NT)
                nc.vector.tensor_scalar(self.rstd[:], self.mv[:, :, 1], EPS, None, ALU.add).then_inc(s_v, 1)
                dve.wait_ge(s_v, 2 * NT + 1)

    def keep_row(self, dve, ready, ready_at, step, base, x_new, row, stats, mv1, T):
        nc = self.nc
        dve.wait_ge(ready, ready_at)
        nc.vector.bn_stats(stats[:], x_new[:]).then_inc(step, 1)
        dve.wait_ge(step, base + 1)
        nc.vector.tensor_scalar(row, x_new[:], 0.0, None, ALU.add)
        nc.vector.bn_aggr(mv1[:], stats[:]).then_inc(step, 1)
        dve.wait_ge(step, base + 2)
        nc.vector.tensor_scalar(self.mv[:, bass.ds(T, 1), :].rearrange("p a d -> p (a d)"), mv1[:], 0.0, None,
                                ALU.add).then_inc(step, 1)

    def store(self):
        s_out = self.sem("out_stored")
        with self.nc.Block() as block:
            @block.sync
            def _(sp):
                for q in range(4):
                    t0 = q * NT // 4
                    sp.dma_start(self.out[t0 * P:(t0 + NT // 4) * P, :].rearrange("(t p) d -> p t d", p=P),
                                 self.x[:, t0:t0 + NT // 4, :]).then_inc(s_out, 16)
                sp.wait_ge(s_out, 64)

    def attention(self, L):
        nc, cfg, ins = self.nc, LAYERS[L], self.ins
        out_proj = cfg["out_proj"]
        n_exp = cfg["experts"] + cfg["shared"]
        pre = f"l{L}_"
        sem = lambda name: self.sem(pre + name)
        with ExitStack() as tmp:
            sb = lambda name, shape, dt: tmp.enter_context(nc.sbuf_tensor(pre + name, shape, dt))
            psb = lambda name, shape: tmp.enter_context(nc.psum_tensor(pre + name, shape, F32))
            wq = sb("wq", [P, DC, D], F32)
            wo = sb("wo", [P, DC, D], F32) if out_proj else None
            bq, bk = sb("bq", [P, DC], F32), sb("bk", [P, DC], F32)
            bo16 = sb("bo16", [1, 2, D], F16) if out_proj else None
            keys_bd = sb("keys_bd", [P, B, NQ, HQ, KEYS], F32)
            vals = sb("vals", [P, B, PC, VH, HD + 1], F32)
            mask_row = sb("mask_row", [1, B, HQ, KEYS], BF16)

            with ExitStack() as setup:
                sbs = lambda name, shape, dt: setup.enter_context(nc.sbuf_tensor(pre + name, shape, dt))
                pss = lambda name, shape: setup.enter_context(nc.psum_tensor(pre + name, shape, F32))
                ctx_t = sbs("ctx_t", [P, DC, B * KEYS], F32)
                wk, wv = sbs("wk", [P, DC, D], F32), sbs("wv", [P, DC, D], F32)
                bv = sbs("bv", [1, D], F32)
                bo = sbs("bo", [1, D], F32) if out_proj else None
                ctx_rows = sbs("ctx_rows", [P, DC, HEADS, KEYS], F32)
                m_raw = sbs("m_raw", [1, B * KEYS], U8 if L == 0 else I32)
                m_f = sbs("m_f", [1, B * KEYS], F32)
                kt = sbs("kt", [P, DC, B * KEYS], F32)
                b_f = sbs("b_f", [MAXE, BCOLS], F32)
                b_s = sbs("b_s", [MAXE, 2, BCOLS], F16)
                ps_k = pss("ps_k", [P, DC, 512])
                ps_v = pss("ps_v", [P, B, 512])
                v_cols = [ps_v[:, b, 0:PC * VH * HD].rearrange("p (c j d) -> p c j d", c=PC, j=VH) for b in range(B)]
                s_ld, s_k, s_v, s_kt, s_d, s_b = (sem(x) for x in ("params_loaded", "k_done", "v_done", "kt_done", "setup_step", "biases_loaded"))
                s_bs, s_bst = sem("bias_split"), sem("biases_stored")
                s_vals, s_bd, s_rows = sem("vals_ready"), sem("keys_ready"), sem("ctx_rows_ready")
                block = setup.enter_context(nc.Block())
                split = lambda ap: ap.rearrange("(c p) n -> p c n", p=P)

                @block.sync
                def _(sp):
                    loads = [(ctx_t, split(ins["ctx_t"])), (wk, split(ins[f"wk{L}"])), (wv, split(ins[f"wv{L}"])),
                             (bk, ins[f"bk{L}"]), (bv, ins[f"bv{L}"]), (m_raw, ins[f"mask{L}"]),
                             (wq, split(ins[f"wq{L}"])), (bq, ins[f"bq{L}"])]
                    if out_proj:
                        loads += [(wo, split(ins["wo0"])), (bo, ins["bo0"])]
                    for dst, src in loads:
                        sp.dma_start(dst[:], src).then_inc(s_ld, 16)
                    sp.dma_start(b_f[0:n_exp, :], ins[f"biases{L}"]).then_inc(s_b, 16)
                    sp.wait_ge(s_bs, 3)
                    sp.dma_start(self.bg[0:n_exp], b_s[0:n_exp]).then_inc(s_bst, 16)
                    sp.wait_ge(s_bst, 16)

                n_loads = 16 * (10 if out_proj else 8)

                @block.tensor
                def _(pe):
                    pe.wait_ge(s_ld, n_loads)
                    for j in range(DC):
                        for c in range(DC):
                            mm = nc.tensor.matmul(ps_k[:, j, 0:B * KEYS], wk[:, c, j * P:(j + 1) * P], ctx_t[:, c, :],
                                                  start=(c == 0), stop=(c == DC - 1))
                        mm.then_inc(s_k, 1)
                    for b in range(B):
                        pe.wait_ge(s_rows, DC * (b + 1))
                        for k in range(PC):
                            rows, (h0, nh) = chunk_rows(k), chunk_heads(k)
                            out = v_cols[b][0:rows, k, 0:nh].rearrange("p j d -> p (j d)")
                            for c in range(DC):
                                lhs = ctx_rows[:, c].rearrange("p h k -> p (h k)")[:, k * P:k * P + rows]
                                nc.tensor.matmul(out, lhs, wv[:, c, h0 * HD:(h0 + nh) * HD], start=(c == 0), stop=False)
                            mm = nc.tensor.matmul(out, self.ones_row[:, 0:rows], bv[:, h0 * HD:(h0 + nh) * HD], start=False, stop=True)
                        mm.then_inc(s_v, 1)

                @block.scalar
                def _(act):
                    for j in range(DC):
                        act.wait_ge(s_k, j + 1)
                        nc.scalar.activation(kt[:, j, :], ps_k[:, j, 0:B * KEYS], ACT.Identity,
                                             bias=bk[:, j:j + 1]).then_inc(s_kt, 1)
                    act.wait_ge(s_b, 16)
                    nc.scalar.mul(b_f[0:n_exp, :], b_f[0:n_exp, :], WSCALE).then_inc(s_bs, 1)
                    act.wait_ge(s_bs, 1)
                    nc.scalar.copy(b_s[0:n_exp, 0, :], b_f[0:n_exp, :]).then_inc(s_bs, 1)

                @block.vector
                def _(dve):
                    nc.vector.memset(vals[:], 0.0).then_inc(s_d, 1)
                    dve.wait_ge(s_d, 1)
                    dve.wait_ge(s_ld, n_loads)
                    for b in range(B):
                        if b:
                            dve.wait_ge(s_v, b)
                        for c in range(DC):
                            src = ctx_t[:, c, b * KEYS:(b + 1) * KEYS].unsqueeze(1).broadcast_to([P, HEADS, KEYS])
                            nc.vector.tensor_copy(ctx_rows[:, c], src).then_inc(s_rows, 1)
                    if L == 0:
                        nc.vector.tensor_scalar(m_f[:], m_raw[:], 0.0, MASKED, ALU.is_equal, ALU.mult).then_inc(s_d, 1)
                    else:
                        nc.vector.tensor_scalar(m_f[:], m_raw[:], 0.0, MASKED, ALU.is_gt, ALU.mult).then_inc(s_d, 1)
                    dve.wait_ge(s_d, 2)
                    for b in range(B):
                        row = m_f[:, b * KEYS:(b + 1) * KEYS].unsqueeze(1).broadcast_to([1, HQ, KEYS])
                        nc.vector.tensor_copy(mask_row[:, b], row).then_inc(s_d, 1)
                    dve.wait_ge(s_bs, 2)
                    nc.vector.tensor_tensor(b_s[0:n_exp, 1, :], b_f[0:n_exp, :], b_s[0:n_exp, 0, :],
                                            ALU.subtract).then_inc(s_bs, 1)
                    dve.wait_ge(s_v, B)
                    for b in range(B):
                        for k in range(PC):
                            rows, (h0, nh) = chunk_rows(k), chunk_heads(k)
                            own = self.row_head[0:rows, k, 0:nh].unsqueeze(2).broadcast_to([rows, nh, HD])
                            nc.vector.tensor_tensor(vals[0:rows, b, k, 0:nh, 0:HD], v_cols[b][0:rows, k, 0:nh], own, ALU.mult)
                        nc.vector.tensor_copy(vals[:, b, :, :, HD], self.row_head[:]).then_inc(s_vals, 1)
                    if out_proj:
                        nc.vector.tensor_copy(bo16[:, 0], bo[:]).then_inc(s_d, 1)
                        dve.wait_ge(s_d, 3 + B)
                        nc.vector.tensor_tensor(bo16[:, 1], bo[:], bo16[:, 0], ALU.subtract).then_inc(s_d, 1)
                    dve.wait_ge(s_kt, DC)
                    for b in range(B):
                        for j in range(DC):
                            src = kt[:, j, b * KEYS:(b + 1) * KEYS].unsqueeze(1).broadcast_to([P, 8, KEYS])
                            msk = self.head_mask[:].unsqueeze(2).broadcast_to([P, 8, KEYS])
                            dst = keys_bd[:, b, 2 * j:2 * j + 2].rearrange("p q h k -> p (q h) k")
                            nc.vector.tensor_tensor(dst, src, msk, ALU.mult).then_inc(s_bd, 1)

            xn, xn_t, q_t = sb("xn", [P, 2, D], F32), sb("xn_t", [P, 2, DC, P], F32), sb("q_t", [P, 2, DC, P], F32)
            probs = sb("probs", [P, 2, HEADS, KEYS], F32)
            smax = sb("smax", [P, 2, NQ, HQ], F32)
            probs_t = sb("probs_t", [P, PC, P], F32)
            rec, att = sb("rec", [P, HEADS, 1], F32), sb("att", [P, HEADS, HD], F32)
            att_t = sb("att_t", [P, DC, P], F32)
            stats, mv1, x_new = sb("stats", [P, 6], F32), sb("mv1", [P, 2], F32), sb("x_new", [P, D], F32)
            stage = sb("stage", [P, 2, WPART], F32)
            ps_s = psb("ps_s", [P, NQ, 512])
            ps_tq, ps_tx, ps_ta, ps_o_bank = (psb(x, [P, 512]) for x in ("ps_tq", "ps_tx", "ps_ta", "ps_o"))
            scores = ps_s[:, :, 0:HQ * KEYS].rearrange("p q (h k) -> p q h k", h=HQ)
            ps_q, ps_xt, ps_o = ps_tq[:, 0:D], ps_tx[:, 0:D], ps_o_bank[:, 0:D]
            ps_av = ps_ta[:, 0:HEADS * (HD + 1)].rearrange("p (h e) -> p h e", h=HEADS)
            rounds = [range(r, min(r + PROUND, PC)) for r in range(0, PC, PROUND)]
            turned_at = [ps[:].rearrange("p (c t) -> p c t", c=PROUND) for ps in (ps_tq, ps_tx, ps_ta)]
            NR = len(rounds)
            names = ("xn_ready", "xt_done", "xn_t_ready", "q_done", "q_t_ready", "scores_done", "smax_step", "shifted",
                     "probs_ready", "turned", "pt_ready", "av_done", "att_step", "att_turned",
                     "att_t_ready", "proj_done", "x_updated", "stats_step", "w_high", "w_low", "rstd_step")
            s = {n: sem(n) for n in names}
            s_stage = [sem("w_staged0"), sem("w_staged1")]
            block = tmp.enter_context(nc.Block())
            tile_of = lambda un: un.i + TB * un.u
            LEAD, LAG = 3, 2
            per_unit = 2 * n_exp // NT
            assert per_unit in (1, 2)
            pieces = lambda un: [(un.n, 0), (un.n, 1)] if per_unit == 2 else [(un.i, un.u)]

            @block.sync
            def _(sp):
                def load(e, has):
                    for m in range(2):
                        sp.wait_ge(s["w_low"], e.n * 2 + m + 1)
                        sp.dma_start(stage[:, m, :], ins[f"weights{L}"][bass.ds(e.n, 1), :, m * WPART:(m + 1) * WPART]
                                     .rearrange("e p n -> p (e n)")).then_inc(s_stage[m], 16)

                run_pipeline(sp, load, n_exp, 0, 0)

            @block.gpsimd
            def _(pool):
                pool.wait_ge(s["rstd_step"], 1)
                nc.gpsimd.tensor_tensor(self.rstd[:], self.rstd[:], self.half[:], ALU.pow).then_inc(s["rstd_step"], 1)
                pool.wait_ge(s["rstd_step"], 2)

            @block.tensor
            def _(pe):
                def step(un, has):
                    n = un.n
                    if has(1):
                        a = un.shifted(1)
                        pe.wait_ge(s["q_t_ready"], DC * a.n + DC)
                        pe.wait_ge(s["shifted"], a.n + 1)
                        for q in range(NQ):
                            nc.tensor.matmul(ps_s[:, q, 0:HQ * KEYS], q_t[:, a.u, q // 2, :],
                                             keys_bd[:, a.u, q].rearrange("p h k -> p (h k)"), start=True, stop=False)
                            mm = nc.tensor.matmul(ps_s[:, q, 0:HQ * KEYS], self.ones_bf[0:1, :],
                                                  mask_row[:, a.u].rearrange("p h k -> p (h k)"), start=False, stop=True)
                        mm.then_inc(s["scores_done"], 1)
                    if has(0):
                        pe.wait_ge(s["probs_ready"], n + 1)
                        rows_of = probs[:, un.u].rearrange("p h k -> p (h k)")
                        for r, chunks in enumerate(rounds):
                            if r == 1 and has(2):
                                pe.wait_ge(s["xn_t_ready"], n + 3)
                            if r == 2:
                                pe.wait_ge(s["att_step"], 2 * n + 2)
                            for i, c in enumerate(chunks):
                                mm = nc.tensor.transpose(turned_at[r][0:chunk_rows(c), i, :], rows_of[:, c * P:c * P + chunk_rows(c)], self.ident[:])
                            mm.then_inc(s["turned"], 1)
                    if has(-1) and out_proj:
                        c = un.shifted(-1)
                        pe.wait_ge(s["att_step"], 2 * n + 2)
                        pe.wait_ge(s["x_updated"], n)
                        for j in range(DC):
                            mm = nc.tensor.transpose(ps_o[:, j * P:(j + 1) * P],
                                                     att[:].rearrange("p h d -> p (h d)")[:, j * P:(j + 1) * P], self.ident[:])
                        mm.then_inc(s["att_turned"], 1)
                    if has(2):
                        a = un.shifted(2)
                        pe.wait_ge(s["xn_t_ready"], a.n + 1)
                        if has(0):
                            pe.wait_ge(s["pt_ready"], NR * n + 1)
                        for j in range(DC):
                            for c in range(DC):
                                mm = nc.tensor.matmul(ps_q[:, j * P:(j + 1) * P], wq[:, c, j * P:(j + 1) * P], xn_t[:, a.u, c, :],
                                                      start=(c == 0), stop=(c == DC - 1))
                        mm.then_inc(s["q_done"], 1)
                    if has(3):
                        a = un.shifted(3)
                        pe.wait_ge(s["xn_ready"], a.n + 1)
                        if has(0):
                            pe.wait_ge(s["pt_ready"], NR * n + 2)
                        elif has(2):
                            pe.wait_ge(s["xn_t_ready"], n + 3)
                        for j in range(DC):
                            mm = nc.tensor.transpose(ps_xt[:, j * P:(j + 1) * P], xn[:, a.u, j * P:(j + 1) * P], self.ident[:])
                        mm.then_inc(s["xt_done"], 1)
                    if has(-1) and out_proj:
                        pe.wait_ge(s["att_t_ready"], n)
                        for j in range(DC):
                            nc.tensor.matmul(ps_o, att_t[:, j, :], wo[:, j, :], start=(j == 0), stop=False)
                        nc.tensor.matmul(ps_o, self.ones16[0:1, :], bo16[:, 0], start=False, stop=False)
                        nc.tensor.matmul(ps_o, self.ones16[0:1, :], bo16[:, 1], start=False, stop=True).then_inc(s["proj_done"], 1)
                    if has(0):
                        pe.wait_ge(s["pt_ready"], NR * n + NR)
                        nc.tensor.matmul(ps_ta[:, 0:HEADS * (HD + 1)], self.zeros16[:, 0:P], self.zeros16[:], start=True, stop=True)
                        for c in range(PC):
                            h0, nh = chunk_heads(c)
                            mm = nc.tensor.matmul(ps_av[:, h0:h0 + nh, :].rearrange("p h e -> p (h e)"), probs_t[0:chunk_rows(c), c, :],
                                                  vals[0:chunk_rows(c), un.u, c, 0:nh, :].rearrange("p j e -> p (j e)"),
                                                  start=False, stop=True, skip_group_check=True)
                        mm.then_inc(s["av_done"], 1)

                run_pipeline(pe, step, NT, LEAD, LAG)

            @block.scalar
            def _(act):
                def weight_high(pieces):
                    for e, m in pieces:
                        act.wait_ge(s_stage[m], 16 * e + 16)
                        nc.scalar.activation(self.weights[:, bass.ds(e, 1), 0, m * WPART:(m + 1) * WPART].rearrange("p a n -> p (a n)"),
                                             stage[:, m, :], ACT.Copy, scale=WSCALE).then_inc(s["w_high"], 1)

                def step(un, has):
                    n = un.n
                    if has(0):
                        act.wait_ge(s["shifted"], n + 2)
                        rows_of = probs[:, un.u].rearrange("p h k -> p (h k)")
                        nc.scalar.activation(rows_of, rows_of, ACT.Exp, scale=float(HD) ** -0.5).then_inc(s["probs_ready"], 1)
                        weight_high(pieces(un)[:1])
                        for r, chunks in enumerate(rounds):
                            act.wait_ge(s["turned"], NR * n + r + 1)
                            if chunk_rows(chunks[-1]) < P:
                                nc.scalar.copy(probs_t[:, chunks[0]:chunks[-1], :], turned_at[r][:, 0:len(chunks) - 1, :])
                                rows = chunk_rows(chunks[-1])
                                nc.scalar.copy(probs_t[0:rows, chunks[-1], :], turned_at[r][0:rows, len(chunks) - 1, :]).then_inc(s["pt_ready"], 1)
                            else:
                                nc.scalar.copy(probs_t[:, chunks[0]:chunks[-1] + 1, :], turned_at[r][:, 0:len(chunks), :]).then_inc(s["pt_ready"], 1)
                    if has(-1) and out_proj:
                        act.wait_ge(s["att_turned"], n)
                        nc.scalar.copy(att_t[:].rearrange("p c t -> p (c t)"), ps_o).then_inc(s["att_t_ready"], 1)
                    if has(2):
                        a = un.shifted(2)
                        act.wait_ge(s["q_done"], a.n + 1)
                        for j in range(DC):
                            nc.scalar.activation(q_t[:, a.u, j, :], ps_q[:, j * P:(j + 1) * P], ACT.Identity,
                                                 bias=bq[:, j:j + 1]).then_inc(s["q_t_ready"], 1)
                    if has(3):
                        a = un.shifted(3)
                        act.wait_ge(s["xt_done"], a.n + 1)
                        nc.scalar.copy(xn_t[:, a.u].rearrange("p c t -> p (c t)"), ps_xt).then_inc(s["xn_t_ready"], 1)
                    if has(0):
                        weight_high(pieces(un)[1:])

                run_pipeline(act, step, NT, LEAD, LAG)
                weight_high([(e, m) for e in range(per_unit * NT // 2, n_exp) for m in range(2)])

            @block.vector
            def _(dve):
                dve.sem_inc(s["x_updated"], 1)
                dve.sem_inc(s["shifted"], 1)
                dve.sem_inc(s["att_step"], 2)
                dve.sem_inc(s["w_low"], 2)

                def weight_low(pieces):
                    for e, m in pieces:
                        dve.wait_ge(s["w_high"], e * 2 + m + 1)
                        high, low = (self.weights[:, bass.ds(e, 1), w, m * WPART:(m + 1) * WPART].rearrange("p a n -> p (a n)") for w in (0, 1))
                        nc.vector.scalar_tensor_tensor(out=low, in0=stage[:, m, :], scalar=WSCALE, in1=high,
                                                       op0=ALU.mult, op1=ALU.subtract).then_inc(s["w_low"], 1)

                def update(c):
                    row = self.x[:, bass.ds(tile_of(c), 1), :].rearrange("p a d -> p (a d)")
                    if out_proj:
                        dve.wait_ge(s["proj_done"], c.n + 1)
                    branch = ps_o if out_proj else att[:].rearrange("p h d -> p (h d)")
                    nc.vector.scalar_tensor_tensor(out=x_new[:], in0=branch, scalar=self.tg[:, 2 * L:2 * L + 1],
                                                   in1=row, op0=ALU.mult, op1=ALU.add).then_inc(s["x_updated"], 1)
                    self.keep_row(dve, s["x_updated"], c.n + 2, s["stats_step"], 3 * c.n, x_new, row, stats, mv1, tile_of(c))

                def step(un, has):
                    n = un.n
                    if has(-2) and out_proj:
                        update(un.shifted(-2))
                    if has(-1):
                        dve.wait_ge(s["av_done"], n)
                        nc.vector.reciprocal(rec[:], ps_av[:, :, HD:HD + 1]).then_inc(s["att_step"], 1)
                        dve.wait_ge(s["att_step"], 2 * n + 1)
                        nc.vector.tensor_tensor(att[:], ps_av[:, :, 0:HD], rec[:].broadcast_to([P, HEADS, HD]),
                                                ALU.mult).then_inc(s["att_step"], 1)
                        if not out_proj:
                            dve.wait_ge(s["att_step"], 2 * n + 2)
                            update(un.shifted(-1))
                    if has(3):
                        a = un.shifted(3)
                        T = tile_of(a)
                        if not (isinstance(n, int) and n < -1):
                            dve.wait_ge(s["xt_done"], n + 2)
                        nc.vector.tensor_scalar(xn[:, a.u, :], self.x[:, bass.ds(T, 1), :].rearrange("p a d -> p (a d)"),
                                                self.mv[:, bass.ds(T, 1), 0], self.rstd[:, bass.ds(T, 1)],
                                                ALU.subtract, ALU.mult).then_inc(s["xn_ready"], 1)
                    if has(1):
                        a = un.shifted(1)
                        dve.wait_ge(s["scores_done"], a.n + 1)
                        nc.vector.tensor_reduce(smax[:, a.u], scores, AX_X, ALU.max).then_inc(s["smax_step"], 1)
                        dve.wait_ge(s["smax_step"], a.n + 1)
                        nc.vector.tensor_tensor(probs[:, a.u].rearrange("p (q h) k -> p q h k", q=NQ), scores,
                                                smax[:, a.u].unsqueeze(3).broadcast_to([P, NQ, HQ, KEYS]),
                                                ALU.subtract).then_inc(s["shifted"], 1)
                    if has(0):
                        weight_low(pieces(un))

                run_pipeline(dve, step, NT, LEAD, LAG)
                weight_low([(e, m) for e in range(per_unit * NT // 2, n_exp) for m in range(2)])
                dve.wait_ge(s["stats_step"], 3 * NT)
                nc.vector.tensor_scalar(self.rstd[:], self.mv[:, :, 1], EPS, None, ALU.add).then_inc(s["rstd_step"], 1)

    def route(self, L):
        nc, cfg, ins = self.nc, LAYERS[L], self.ins
        E, K, shared = cfg["experts"], cfg["topk"], cfg["shared"]
        R = routed_tiles(L)
        pre = f"l{L}_"
        sem = lambda name: self.sem(pre + name)
        self.layer_ctx = ExitStack()
        keep = lambda name, shape, dt: self.layer_ctx.enter_context(nc.sbuf_tensor(pre + name, shape, dt))
        self.xn = keep("xn_all", [P, NT, D], F32)
        self.slots = keep("slots", [P, NT, K], I32)
        self.gate = keep("gate", [P, NT, K], F32)
        with ExitStack() as tmp:
            sb = lambda name, shape, dt: tmp.enter_context(nc.sbuf_tensor(pre + name, shape, dt))
            psb = lambda name, shape: tmp.enter_context(nc.psum_tensor(pre + name, shape, F32))
            wg, bg = sb("wg", [P, DC, E], F32), sb("bg_row", [1, E], F32)
            xn, xn_t = sb("r_xn", [P, 2, D], F32), sb("r_xn_t", [P, 2, DC, P], F32)
            logits = sb("logits", [P, NT, E], F32)
            ps_xt, ps_l = psb("r_ps_xt", [P, 2, 512]), psb("r_ps_l", [P, 2, 512])
            s = {n: sem("r_" + n) for n in ("params", "xn_ready", "turned", "xn_t_ready", "logits_done", "logits_kept")}
            s_row = [sem("r_rows_stored0"), sem("r_rows_stored1")]

            with nc.Block() as block:
                @block.sync
                def _(sp):
                    sp.dma_start(wg[:], ins[f"wg{L}"].rearrange("(c p) e -> p c e", p=P)).then_inc(s["params"], 16)
                    sp.dma_start(bg[:], ins[f"bg{L}"]).then_inc(s["params"], 16)
                    if shared:
                        def rows(t, has):
                            sp.wait_ge(s["xn_ready"], t.n + 1)
                            for h in range(shared):
                                sp.dma_start(self.xg[bass.ds((h * NT + t.n) * P, P), :], xn[:, t.u, :]).then_inc(s_row[t.u], 16)

                        for u in range(2):
                            sp.sem_inc(s_row[u], 16 * shared)
                        run_pipeline(sp, rows, NT, 0, 0)
                        for u in range(2):
                            sp.wait_ge(s_row[u], 16 * shared * (NT // 2 + 1))

                @block.tensor
                def _(pe):
                    pe.wait_ge(s["params"], 32)

                    def step(t, has):
                        if has(1):
                            a = t.shifted(1)
                            pe.wait_ge(s["xn_ready"], a.n + 1)
                            for j in range(DC):
                                mm = nc.tensor.transpose(ps_xt[:, a.u, j * P:(j + 1) * P], xn[:, a.u, j * P:(j + 1) * P], self.ident[:])
                            mm.then_inc(s["turned"], 1)
                        if has(0):
                            pe.wait_ge(s["xn_t_ready"], t.n + 1)
                            pe.wait_ge(s["logits_kept"], t.n + 1)
                            for j in range(DC):
                                nc.tensor.matmul(ps_l[:, t.u, 0:E], xn_t[:, t.u, j, :], wg[:, j, :], start=(j == 0), stop=False)
                            nc.tensor.matmul(ps_l[:, t.u, 0:E], self.ones_row[:], bg[:], start=False, stop=True).then_inc(s["logits_done"], 1)

                    run_pipeline(pe, step, NT, 1, 0)

                @block.scalar
                def _(act):
                    def step(t, has):
                        act.wait_ge(s["turned"], t.n + 1)
                        nc.scalar.copy(xn_t[:, t.u].rearrange("p c t -> p (c t)"), ps_xt[:, t.u, 0:D]).then_inc(s["xn_t_ready"], 1)

                    run_pipeline(act, step, NT, 0, 0)

                @block.vector
                def _(dve):
                    dve.sem_inc(s["logits_kept"], 2)

                    def step(t, has):
                        if has(2):
                            a = t.shifted(2)
                            row = self.x[:, bass.ds(a.n, 1), :].rearrange("p a d -> p (a d)")
                            if not (isinstance(t.n, int) and t.n < 0):
                                dve.wait_ge(s["turned"], t.n + 1)
                                if shared:
                                    dve.wait_ge(s_row[t.u], 16 * shared * (t.i + 2))
                            for dst in (xn[:, a.u, :], self.xn[:, bass.ds(a.n, 1), :].rearrange("p a d -> p (a d)")):
                                ins_ = nc.vector.tensor_scalar(dst, row, self.mv[:, bass.ds(a.n, 1), 0], self.rstd[:, bass.ds(a.n, 1)],
                                                               ALU.subtract, ALU.mult)
                            ins_.then_inc(s["xn_ready"], 1)
                        if has(0):
                            dve.wait_ge(s["logits_done"], t.n + 1)
                            nc.vector.tensor_scalar(logits[:, bass.ds(t.n, 1), :].rearrange("p a e -> p (a e)"), ps_l[:, t.u, 0:E],
                                                    0.0, None, ALU.add).then_inc(s["logits_kept"], 1)

                    run_pipeline(dve, step, NT, 2, 0)

            iota_e, iota_n = sb("iota_e", [P, E], F32), sb("iota_n", [1, R], F32)
            mx, den = sb("mx", [P, NT], F32), sb("den", [P, NT], F32)
            prob = sb("prob", [P, NT, E], F32)
            top8, idx8 = sb("top8", [P, NT, 8], F32), sb("idx8", [P, NT, 8], mybir.dt.uint32)
            idx_f = sb("idx_f", [P, NT, 8], F32)
            chosen = sb("chosen", [P, K, NT, E], F32)
            mask = sb("mask", [P, NT, E], BF16)
            tot_i, tiles, zero_e = sb("tot_i", [P, E], I32), sb("tiles", [P, E], F32), sb("zero_e", [P, E], F32)
            ends, first = sb("ends", [P, E], F32), sb("first_slot", [P, E], F32)
            slot_of, pick = sb("slot_of", [P, NT, E], F32), sb("pick", [P, NT, E], F32)
            slot_f = sb("slot_f", [P, NT, K], F32)
            past = sb("past", [1, R, E], F32)
            eid_f = sb("eid_f", [1, SLOT_TILES], F32)
            ps_rank, ps_tot = psb("ps_rank", [P, 512]), psb("ps_tot", [P, 512])
            q = {n: sem("q_" + n) for n in ("shifted", "exp", "mask", "rank", "iota", "step")}
            bc = lambda ap: ap.unsqueeze(2).broadcast_to([P, NT, E])

            with nc.Block() as block:
                @block.gpsimd
                def _(pool):
                    nc.gpsimd.iota(iota_e[:], pattern=[[1, E]], base=0, channel_multiplier=0,
                                   allow_small_or_imprecise_dtypes=True).then_inc(q["iota"], 1)
                    nc.gpsimd.iota(iota_n[:], pattern=[[1, R]], base=0, channel_multiplier=0,
                                   allow_small_or_imprecise_dtypes=True).then_inc(q["iota"], 1)
                    nc.gpsimd.memset(zero_e[:], 0.0).then_inc(q["iota"], 1)

                @block.scalar
                def _(act):
                    act.wait_ge(q["shifted"], 1)
                    nc.scalar.activation(prob[:], prob[:], ACT.Exp, scale=cfg["inv_temp"]).then_inc(q["exp"], 1)

                @block.tensor
                def _(pe):
                    pe.wait_ge(q["mask"], 1)
                    flat = lambda ap: ap.rearrange("p t e -> p (t e)")
                    ranks = ps_rank[:, 0:NT * E].rearrange("p (t e) -> p t e", t=NT)
                    nc.tensor.matmul(ps_rank[:, 0:NT * E], self.before[:], flat(mask[:]), start=True, stop=False)
                    for t in range(NT - 1):
                        nc.tensor.matmul(ranks[:, t + 1:, :], self.ones_bf[:],
                                         mask[:, t:t + 1, :].broadcast_to([P, NT - 1 - t, E]), start=False, stop=(t == NT - 2))
                    for t in range(NT):
                        mm = nc.tensor.matmul(ps_tot[:, 0:E], self.ones_bf[:], mask[:, t, :], start=(t == 0), stop=(t == NT - 1))
                    mm.then_inc(q["rank"], 1)

                @block.vector
                def _(dve):
                    v, step = nc.vector, Chain(dve, q["step"])
                    step(v.tensor_reduce(mx[:], logits[:], AX_X, ALU.max))
                    v.tensor_tensor(prob[:], logits[:], bc(mx[:]), ALU.subtract).then_inc(q["shifted"], 1)
                    dve.wait_ge(q["exp"], 1)
                    step(v.tensor_reduce(den[:], prob[:], AX_X, ALU.add))
                    step(v.reciprocal(den[:], den[:]))
                    step(v.tensor_tensor(prob[:], prob[:], bc(den[:]), ALU.mult))
                    for t in range(NT):
                        ins_ = v.max(out=top8[:, t, :], in_=prob[:, t, :])
                    step(ins_)
                    for t in range(NT):
                        ins_ = v.max_index(out=idx8[:, t, :], in_max=top8[:, t, :], in_values=prob[:, t, :])
                    step(ins_)
                    step(v.tensor_copy(idx_f[:], idx8[:]))
                    dve.wait_ge(q["iota"], 3)
                    for j in range(K):
                        ins_ = v.tensor_tensor(chosen[:, j], bc(idx_f[:, :, j]), iota_e[:].unsqueeze(1).broadcast_to([P, NT, E]), ALU.is_equal)
                    step(ins_)
                    for j in range(1, K):
                        last = j == K - 1
                        ins_ = v.tensor_tensor(mask[:] if last else pick[:], chosen[:, 0] if j == 1 else pick[:], chosen[:, j], ALU.add)
                        if not last:
                            step(ins_)
                    ins_.then_inc(q["mask"], 1)
                    if cfg["renorm"]:
                        step(v.tensor_reduce(den[:], top8[:, :, 0:K], AX_X, ALU.add))
                        step(v.tensor_scalar(den[:], den[:], 1e-9, None, ALU.add))
                        step(v.reciprocal(den[:], den[:]))
                        step(v.tensor_tensor(self.gate[:], top8[:, :, 0:K], den[:].unsqueeze(2).broadcast_to([P, NT, K]), ALU.mult))
                    else:
                        step(v.tensor_copy(self.gate[:], top8[:, :, 0:K]))
                    dve.wait_ge(q["rank"], 1)
                    step(v.tensor_scalar(tot_i[:], ps_tot[:, 0:E], float(P - 1), None, ALU.add))
                    step(v.tensor_scalar(tot_i[:], tot_i[:], P.bit_length() - 1, None, ALU.logical_shift_right))
                    step(v.tensor_copy(tiles[:], tot_i[:]))
                    step(v.tensor_tensor_scan(ends[:], tiles[:], zero_e[:], 0.0, ALU.add, ALU.add))
                    step(v.tensor_tensor(first[:], ends[:], tiles[:], ALU.subtract))
                    step(v.tensor_scalar(first[:], first[:], float(shared * NT), float(P), ALU.add, ALU.mult))
                    step(v.tensor_tensor(slot_of[:], ps_rank[:, 0:NT * E].rearrange("p (t e) -> p t e", t=NT),
                                         first[:].unsqueeze(1).broadcast_to([P, NT, E]), ALU.add))
                    for j in range(K):
                        step(v.tensor_tensor(pick[:], slot_of[:], chosen[:, j], ALU.mult))
                        step(v.tensor_reduce(slot_f[:, :, j], pick[:], AX_X, ALU.add))
                    step(v.tensor_copy(self.slots[:], slot_f[:]))
                    step(v.tensor_tensor(past[:], iota_n[:].unsqueeze(2).broadcast_to([1, R, E]),
                                         ends[0:1, :].unsqueeze(1).broadcast_to([1, R, E]), ALU.is_ge))
                    n0 = shared * NT
                    for h in range(shared):
                        step(v.memset(eid_f[:, h * NT:(h + 1) * NT], float(E + h)))
                    step(v.tensor_reduce(eid_f[:, n0:n0 + R], past[:], AX_X, ALU.add))
                    step(v.tensor_scalar(eid_f[:, n0:n0 + R], eid_f[:, n0:n0 + R], float(E - 1), None, ALU.min))
                    step(v.tensor_copy(self.eid[:, 0:n0 + R], eid_f[:, 0:n0 + R]))

    def experts(self, L):
        nc, cfg = self.nc, LAYERS[L]
        K, shared = cfg["topk"], cfg["shared"]
        n_exp = cfg["experts"] + shared
        N = shared * NT + routed_tiles(L)
        pre = f"l{L}_e_"
        sem = lambda name: self.sem(pre + name)
        with ExitStack() as tmp:
            sb = lambda name, shape, dt: tmp.enter_context(nc.sbuf_tensor(pre + name, shape, dt))
            psb = lambda name, shape: tmp.enter_context(nc.psum_tensor(pre + name, shape, F32))
            xin = sb("xin", [P, 2, D], F32)
            xh, xl = sb("xh", [P, 2, DC, P], F16), sb("xl", [P, 2, DC, P], F16)
            b1, b2 = sb("b1", [2, 2, HID], F16), sb("b2", [2, 2, D], F16)
            h = sb("h", [P, 2, HID], F32)
            hh, hl = sb("hh", [P, 2, HC, P], F16), sb("hl", [P, 2, HC, P], F16)
            y = sb("y", [P, 2, D], F32)
            ps_x, ps_h, ps_t, ps_y = psb("ps_x", [P, 2, 512]), psb("ps_h", [P, HID]), psb("ps_t", [P, HID]), psb("ps_y", [P, 2, 512])
            s = {n: sem(n) for n in ("scattered", "x_turned", "xh_ready", "xl_ready", "h_done", "h_ready", "h_turned",
                                     "hh_ready", "hl_ready", "y_done", "y_ready")}
            s_x, s_b1, s_b2, s_y = ([sem(f"{n}{u}") for u in range(2)] for n in ("x_in", "b1_in", "b2_in", "y_stored"))
            block = tmp.enter_context(nc.Block())

            @block.gpsimd
            def _(pool):
                for t in range(NT):
                    for j in range(K):
                        nc.gpsimd.indirect_dma_start(self.xg, bass.IndirectOffsetOnAxis(ap=self.slots[:, t, j:j + 1], axis=0),
                                                     self.xn[:, t, :], None).then_inc(s["scattered"], 16)
                pool.wait_ge(s["scattered"], 16 * NT * K)

            @block.sync
            def _(sp):
                for u in range(2):
                    sp.sem_inc(s_y[u], 16)

                def expert(m):
                    return sp.value_load(self.eid[0:1, bass.ds(m.n, 1)], min_val=0, max_val=n_exp - 1)

                def step(t, has):
                    if has(4):
                        m = t.shifted(4)
                        sp.wait_ge(s["x_turned"], m.n + 1)
                        sp.dma_start(xin[:, m.u, :], self.xg[bass.ds(m.n * P, P), :]).then_inc(s_x[m.u], 16)
                    if has(3):
                        m = t.shifted(3)
                        e = expert(m)
                        sp.wait_ge(s["h_done"], m.n + 1)
                        sp.dma_start(b1[:, m.u, :], self.bg[bass.ds(e, 1), :, 0:HID].rearrange("e r n -> (e r) n")).then_inc(s_b1[m.u], 16)
                    if has(2):
                        m = t.shifted(2)
                        e = expert(m)
                        sp.wait_ge(s["y_done"], m.n + 1)
                        sp.dma_start(b2[:, m.u, :], self.bg[bass.ds(e, 1), :, HID:BCOLS].rearrange("e r n -> (e r) n")).then_inc(s_b2[m.u], 16)
                    if has(0):
                        sp.wait_ge(s["y_ready"], t.n + 3)
                        sp.dma_start(self.yg[bass.ds(t.n * P, P), :], y[:, t.u, :]).then_inc(s_y[t.u], 16)

                run_pipeline(sp, step, N, 4, 0, pause=shared * NT - 4,
                             at_pause=lambda: sp.wait_ge(s["scattered"], 16 * NT * K))
                for u in range(2):
                    sp.wait_ge(s_y[u], 16 * ((N + 1 - u) // 2) + 16)

            @block.tensor
            def _(pe):
                pe.sem_inc(s["x_turned"], 2)
                pe.sem_inc(s["h_done"], 2)
                pe.sem_inc(s["y_done"], 2)

                def weight(e, part, a, n):
                    return self.weights[:, bass.ds(e, 1), part, a:a + n].rearrange("p e n -> p (e n)")

                def step(t, has):
                    if has(0):
                        pe.wait_ge(s["h_ready"], t.n + 1)
                        for c in range(HC):
                            mm = nc.tensor.transpose(ps_t[:, c * P:(c + 1) * P], h[:, t.u, c * P:(c + 1) * P], self.ident[:])
                        mm.then_inc(s["h_turned"], 1)
                    if has(2):
                        m = t.shifted(2)
                        pe.wait_ge(s_x[m.u], 16 * m.i + 16)
                        for c in range(DC):
                            mm = nc.tensor.transpose(ps_x[:, m.u, c * P:(c + 1) * P], xin[:, m.u, c * P:(c + 1) * P], self.ident[:])
                        mm.then_inc(s["x_turned"], 1)
                    if has(1):
                        m = t.shifted(1)
                        e = pe.value_load(self.eid[0:1, bass.ds(m.n, 1)], min_val=0, max_val=n_exp - 1)
                        pe.wait_ge(s["xl_ready"], m.n + 1)
                        for c in range(DC):
                            for part, w in ((xh, 0), (xh, 1), (xl, 0)):
                                nc.tensor.matmul(ps_h[:], part[:, m.u, c, :], weight(e, w, c * HID, HID),
                                                 start=(c == 0 and part is xh and w == 0), stop=False)
                        pe.wait_ge(s_b1[m.u], 16 * m.i + 16)
                        nc.tensor.matmul(ps_h[:], self.ones16[:], b1[:, m.u, :], start=False, stop=True).then_inc(s["h_done"], 1)
                    if has(0):
                        e = pe.value_load(self.eid[0:1, bass.ds(t.n, 1)], min_val=0, max_val=n_exp - 1)
                        pe.wait_ge(s["hl_ready"], t.n + 1)
                        pe.wait_ge(s["y_ready"], t.n + 1)
                        for c in range(HC):
                            for part, w in ((hh, 0), (hh, 1), (hl, 0)):
                                nc.tensor.matmul(ps_y[:, t.u, 0:D], part[:, t.u, c, :], weight(e, w, DC * HID + c * D, D),
                                                 start=(c == 0 and part is hh and w == 0), stop=False)
                        pe.wait_ge(s_b2[t.u], 16 * t.i + 16)
                        nc.tensor.matmul(ps_y[:, t.u, 0:D], self.ones16[:], b2[:, t.u, :], start=False, stop=True).then_inc(s["y_done"], 1)

                run_pipeline(pe, step, N, 2, 0)

            @block.scalar
            def _(act):
                def step(t, has):
                    if has(0):
                        act.wait_ge(s["h_turned"], t.n + 1)
                        nc.scalar.copy(hh[:, t.u].rearrange("p c t -> p (c t)"), ps_t[:]).then_inc(s["hh_ready"], 1)
                    if has(2):
                        m = t.shifted(2)
                        act.wait_ge(s["x_turned"], m.n + 3)
                        nc.scalar.copy(xh[:, m.u].rearrange("p c t -> p (c t)"), ps_x[:, m.u, 0:D]).then_inc(s["xh_ready"], 1)
                    if has(1):
                        m = t.shifted(1)
                        act.wait_ge(s["h_done"], m.n + 3)
                        nc.scalar.activation(h[:, m.u, :], ps_h[:], ACT.Gelu, scale=1.0 / WSCALE).then_inc(s["h_ready"], 1)

                run_pipeline(act, step, N, 2, 0)

            @block.vector
            def _(dve):
                dve.sem_inc(s["y_ready"], 2)

                def step(t, has):
                    if has(0):
                        dve.wait_ge(s["hh_ready"], t.n + 1)
                        nc.vector.tensor_tensor(hl[:, t.u].rearrange("p c t -> p (c t)"), ps_t[:], hh[:, t.u].rearrange("p c t -> p (c t)"),
                                                ALU.subtract).then_inc(s["hl_ready"], 1)
                    if has(2):
                        m = t.shifted(2)
                        dve.wait_ge(s["xh_ready"], m.n + 1)
                        nc.vector.tensor_tensor(xl[:, m.u].rearrange("p c t -> p (c t)"), ps_x[:, m.u, 0:D],
                                                xh[:, m.u].rearrange("p c t -> p (c t)"), ALU.subtract).then_inc(s["xl_ready"], 1)
                    if has(0):
                        dve.wait_ge(s["y_done"], t.n + 3)
                        dve.wait_ge(s_y[t.u], 16 * t.i + 16)
                        nc.vector.tensor_scalar(y[:, t.u, :], ps_y[:, t.u, 0:D], 1.0 / WSCALE, None, ALU.mult).then_inc(s["y_ready"], 1)

                run_pipeline(dve, step, N, 2, 0)

    def combine(self, L):
        nc, cfg = self.nc, LAYERS[L]
        K, shared = cfg["topk"], cfg["shared"]
        pre = f"l{L}_c_"
        sem = lambda name: self.sem(pre + name)
        with ExitStack() as tmp:
            sb = lambda name, shape, dt: tmp.enter_context(nc.sbuf_tensor(pre + name, shape, dt))
            yr = sb("y_routed", [P, 2, K, D], F32)
            ys = sb("y_shared", [P, 2, shared, D], F32) if shared else None
            acc = sb("acc", [P, D], F32)
            stats, mv1, x_new = sb("stats", [P, 6], F32), sb("mv1", [P, 2], F32), sb("x_new", [P, D], F32)
            s = {n: sem(n) for n in ("acc_step", "used", "kept", "rstd_step", "stats_step")}
            s_r, s_s = [sem("gathered0"), sem("gathered1")], [sem("shared_in0"), sem("shared_in1")]
            n_acc = K + (shared if shared else 0)
            block = tmp.enter_context(nc.Block())

            @block.gpsimd
            def _(pool):
                for t in range(NT):
                    pool.wait_ge(s["used"], t + 1)
                    for j in range(K):
                        nc.gpsimd.indirect_dma_start(yr[:, t % 2, j, :], None, self.yg,
                                                     bass.IndirectOffsetOnAxis(ap=self.slots[:, t, j:j + 1], axis=0)).then_inc(s_r[t % 2], 16)
                pool.wait_ge(s["rstd_step"], 1)
                nc.gpsimd.tensor_tensor(self.rstd[:], self.rstd[:], self.half[:], ALU.pow).then_inc(s["rstd_step"], 1)
                pool.wait_ge(s["rstd_step"], 2)

            @block.sync
            def _(sp):
                if shared:
                    def load(t, has):
                        sp.wait_ge(s["used"], t.n + 1)
                        for q in range(shared):
                            sp.dma_start(ys[:, t.u, q, :], self.yg[bass.ds((q * NT + t.n) * P, P), :]).then_inc(s_s[t.u], 16)

                    run_pipeline(sp, load, NT, 0, 0)

            @block.vector
            def _(dve):
                dve.sem_inc(s["used"], 2)

                def step(t, has):
                    one = lambda ap: ap.rearrange("p a d -> p (a d)")
                    row, xn = one(self.x[:, bass.ds(t.n, 1), :]), one(self.xn[:, bass.ds(t.n, 1), :])
                    done = 0

                    def link(ins_):
                        nonlocal done
                        done += 1
                        ins_.then_inc(s["acc_step"], 1)
                        dve.wait_ge(s["acc_step"], t.n * n_acc + done)

                    if shared:
                        dve.wait_ge(s_s[t.u], 16 * shared * (t.i + 1))
                        link(nc.vector.tensor_tensor(acc[:], xn, ys[:, t.u, 0, :], ALU.add))
                        link(nc.vector.tensor_tensor(acc[:], acc[:], ys[:, t.u, 1, :], ALU.add))
                    dve.wait_ge(s_r[t.u], 16 * K * (t.i + 1))
                    for j in range(K):
                        g = self.gate[:, bass.ds(t.n, 1), j]
                        if j == 0 and not shared:
                            link(nc.vector.tensor_scalar(acc[:], yr[:, t.u, j, :], g, None, ALU.mult))
                        else:
                            link(nc.vector.scalar_tensor_tensor(out=acc[:], in0=yr[:, t.u, j, :], scalar=g, in1=acc[:],
                                                                op0=ALU.mult, op1=ALU.add))
                    nc.vector.scalar_tensor_tensor(out=x_new[:], in0=acc[:], scalar=self.tg[:, 2 * L + 1:2 * L + 2], in1=row,
                                                   op0=ALU.mult, op1=ALU.add).then_inc(s["used"], 1)
                    self.keep_row(dve, s["used"], t.n + 3, s["stats_step"], 3 * t.n, x_new, row, stats, mv1, t.n)

                run_pipeline(dve, step, NT, 0, 0)
                dve.wait_ge(s["stats_step"], 3 * NT)
                nc.vector.tensor_scalar(self.rstd[:], self.mv[:, :, 1], EPS, None, ALU.add).then_inc(s["rstd_step"], 1)
        self.layer_ctx.close()


def flamingo_layers(nc, ins, out):
    with ExitStack() as ctx:
        b = Build(nc, ctx, ins, out)
        b.start()
        for L in range(len(LAYERS)):
            b.attention(L)
            if STOP == ("attention", L):
                b.store()
                return
            b.route(L)
            b.experts(L)
            b.combine(L)
            b.recycle_semaphores()
            if STOP == ("combine", L):
                b.store()
                return
        b.store()


def laid_out(v):
    rows = lambda w: np.ascontiguousarray(w)
    cols = lambda b: np.ascontiguousarray(b.reshape(DC, P).T)
    ctx = v["ctx_1024"].reshape(B * KEYS, D)

    def experts(w1, w2):
        e = w1.shape[0]
        a = w1.reshape(e, DC, P, HID).transpose(0, 2, 1, 3).reshape(e, P, DC * HID)
        b = w2.reshape(e, HC, P, D).transpose(0, 2, 1, 3).reshape(e, P, HC * D)
        return np.ascontiguousarray(np.concatenate([a, b], axis=2))

    sw1 = v["L0_ffn_sW1"].reshape(D, 2, HID).transpose(1, 0, 2)
    sw2 = v["L0_ffn_sW2"].reshape(2, HID, D)
    sb1 = v["L0_ffn_sb1"].reshape(2, HID)
    sb2 = np.concatenate([v["L0_ffn_sb2"], np.zeros((1, D), np.float32)], axis=0)
    return {
        "x": rows(v["x"].reshape(B * S, D)),
        "ctx_t": rows(ctx.T),
        "gates": rows(np.broadcast_to(np.stack([v["g_xattn"][0], v["g_ffn"][0], v["g_xattn"][1], v["g_ffn"][1]]), (P, 4))),
        "mask0": rows(v["mask_Bx1x1xS2_bf1"].reshape(1, B * KEYS).view(np.uint8)),
        "mask1": rows(v["mask_BxS2_ik0"].reshape(1, B * KEYS)),
        "wq0": rows(v["L0_xattn_Wq"]), "wk0": rows(v["L0_xattn_Wk"]), "wv0": rows(v["L0_xattn_Wv"]), "wo0": rows(v["L0_xattn_Wo"]),
        "bq0": cols(v["L0_xattn_bq"]), "bk0": cols(v["L0_xattn_bk"]), "bv0": rows(v["L0_xattn_bv"][None]), "bo0": rows(v["L0_xattn_bo"][None]),
        "wq1": rows(v["L1_xattn_q_w"].T), "wk1": rows(v["L1_xattn_k_w"].T), "wv1": rows(v["L1_xattn_v_w"].T),
        "bq1": cols(v["L1_xattn_q_b"]), "bk1": cols(v["L1_xattn_k_b"]), "bv1": rows(v["L1_xattn_v_b"][None]),
        "weights0": experts(np.concatenate([v["L0_ffn_rW1"], sw1]), np.concatenate([v["L0_ffn_rW2"], sw2])),
        "biases0": rows(np.concatenate([np.concatenate([v["L0_ffn_rb1"], sb1]), np.concatenate([v["L0_ffn_rb2"], sb2])], axis=1)),
        "weights1": experts(v["L1_ffn_W1"], v["L1_ffn_W2"]),
        "biases1": rows(np.concatenate([v["L1_ffn_b1"], v["L1_ffn_b2"]], axis=1)),
        "wg0": rows(v["L0_ffn_gW"]), "bg0": rows(v["L0_ffn_gb"][None]),
        "wg1": rows(v["L1_ffn_Wg"]), "bg1": rows(v["L1_ffn_bg"][None]),
    }


STOP = None


def kernel(**inputs):
    import concourse.bacc as bacc
    from concourse.bass_utils import run_bass_kernel_spmd

    arrays = {f"in_{k}": a for k, a in laid_out({k: np.asarray(a) for k, a in inputs.items()}).items()}
    nc = bacc.Bacc("TRN2", target_bir_lowering=False, num_devices=1)
    ins = {k[3:]: nc.dram_tensor(k, a.shape, mybir.dt.from_np(a.dtype), kind="ExternalInput").ap() for k, a in arrays.items()}
    out = nc.dram_tensor("out", (B * S, D), F32, kind="ExternalOutput").ap()
    flamingo_layers(nc, ins, out)
    r = run_bass_kernel_spmd(nc, [arrays], core_ids=[0])
    return r.results[0]["out"].reshape(B, S, D)
```

```python
from contextlib import ExitStack

import numpy as np

import concourse.bass as bass
from concourse import mybir

F32 = mybir.dt.float32
F16 = mybir.dt.float16
BF16 = mybir.dt.bfloat16
I32 = mybir.dt.int32
U8 = mybir.dt.uint8
ACT = mybir.ActivationFunctionType
ALU = mybir.AluOpType
AX_X = mybir.AxisListType.X

P = 128
D = 256
DC = D // P
B = 2
S = 1024
NT = B * S // P
TB = NT // B
KEYS = 77
HEADS = 16
HD = D // HEADS
HQ = 4
NQ = HEADS // HQ
PROWS = HEADS * KEYS
PC = -(-PROWS // P)
VH = 3
PROUND = 4
HID = 512
HC = HID // P
WCOLS = DC * HID + HC * D
WPART = WCOLS // 2
BCOLS = HID + D
WSCALE = 16.0
EPS = 1e-5

LAYERS = [
    dict(experts=15, topk=3, shared=2, inv_temp=1.0, renorm=False, out_proj=True, by_slot=False),
    dict(experts=8, topk=2, shared=0, inv_temp=1.0 / 5.0, renorm=True, out_proj=False, by_slot=True),
]


def chunk_rows(c):
    return min(P, PROWS - c * P)


def chunk_heads(c):
    first, last = c * P // KEYS, (c * P + chunk_rows(c) - 1) // KEYS
    assert last - first < VH
    return first, last - first + 1


def routed_tiles(layer):
    c = LAYERS[layer]
    return (c["topk"] * NT * P + c["experts"] * (P - 1)) // P


MAXE = max(c["experts"] + c["shared"] for c in LAYERS)
DEFER = 3
MAXK = max(c["topk"] for c in LAYERS)
ME = max(c["experts"] for c in LAYERS)
SLOT_TILES = max(routed_tiles(n) + c["shared"] * NT for n, c in enumerate(LAYERS))
FILL_FROM = LAYERS[0]["shared"] * NT
FILL = -(-routed_tiles(0) // (MAXE - DEFER))
ROW_TILES = FILL_FROM + FILL * (MAXE - DEFER)
assert ROW_TILES >= SLOT_TILES


class Unit:

    def __init__(self, k, c, per=2):
        self.n = k * per + c
        self.u = c % 2
        self.i = k * (per // 2) + c // 2
        self.c, self.k, self.per = c, k, per

    def shifted(self, d):
        return Unit(self.k, self.c + d, self.per)


def run_pipeline(eng, step, n_units, lead, lag, pause=None, at_pause=None, per=2):
    lo, hi = lag, n_units - lead
    cuts = [lo, hi]
    if pause is not None and lo <= pause < hi:
        cuts = [lo, pause, hi]

    def straight(start, end):
        for n in range(start, end):
            if n == pause:
                at_pause()
            step(Unit(0, n, per), lambda d: 0 <= n + d < n_units)

    straight(-lead, lo)
    for start, end in zip(cuts, cuts[1:]):
        looped = max(0, (end - start) // per * per)
        if looped and start == pause:
            at_pause()
        if looped:
            with eng.Fori(0, looped // per) as k:
                for c in range(start, start + per):
                    step(Unit(k, c, per), lambda d: True)
        if not (looped and start + looped == end):
            straight(start + looped, end)
    straight(hi, n_units + lag)


class Chain:

    def __init__(self, eng, sem, base=0):
        self.eng, self.sem, self.base, self.n = eng, sem, base, 0

    def __call__(self, ins):
        self.n += 1
        ins.then_inc(self.sem, 1)
        self.eng.wait_ge(self.sem, self.base + self.n)


class Build:
    def __init__(self, nc, ctx, ins, out):
        self.nc, self.ctx, self.ins, self.out = nc, ctx, ins, out
        self.sems = []
        self.persistent()

    def sem(self, name):
        handle = self.nc.alloc_semaphore(name=name)
        self.sems.append(handle)
        return handle

    def recycle_semaphores(self):
        self.nc.all_engine_barrier()
        self.nc.clear_and_free_semaphores(self.sems)
        self.nc.all_engine_barrier()
        self.sems = []

    def sb(self, name, shape, dt):
        return self.ctx.enter_context(self.nc.sbuf_tensor(name, shape, dt))

    def persistent(self):
        nc, sb = self.nc, self.sb
        self.x = sb("x_all", [P, NT, D], F32)
        self.xn = sb("xn_all", [P, NT, D], F32)
        self.mean = sb("mean", [P, NT], F32)
        self.rstd = sb("rstd", [P, NT], F32)
        self.logits = sb("logits", [P, NT, ME], F32)
        self.slots = sb("slots", [P, NT, MAXK], I32)
        self.gate = sb("gate", [P, NT, MAXK], F32)
        slot_tiles = max(routed_tiles(n) for n, c in enumerate(LAYERS) if c["by_slot"])
        self.row_of_slot = sb("row_of_slot", [P, slot_tiles], I32)
        self.dest_of_slot = sb("dest_of_slot", [P, slot_tiles], I32)
        self.zeros = sb("zeros", [P, D], F32)
        self.ident = sb("ident", [P, P], F32)
        self.ones_row = sb("ones_row", [1, P], F32)
        self.ones_bf = sb("ones_bf", [P, P], BF16)
        self.before = sb("before", [P, P], BF16)
        self.ones16 = sb("ones16", [2, P], F16)
        self.gates_in = sb("gates_in", [P, 4], F32)
        self.tg = sb("tanh_gates", [P, 4], F32)
        self.head_mask = sb("head_mask", [P, 8], F32)
        self.row_head = sb("row_head", [P, PC, VH], F32)
        self.zeros16 = sb("zeros16", [1, D + HEADS], F16)
        self.half = sb("neg_half", [P, NT], F32)
        self.weights = sb("weights", [P, MAXE, 2, WCOLS], F16)
        self.ends = sb("ends", [P, ME], F32)
        self.tile_no = sb("tile_no", [1, SLOT_TILES], F32)
        self.eid = sb("expert_of_tile", [1, SLOT_TILES], I32)
        d = nc.dram_tensor
        self.xg = d("expert_rows_in", (ROW_TILES * P, D), F32).ap()
        self.xd = d("rows_normalised", (NT * P, D), F32).ap()
        self.yg = d("expert_rows_out", (SLOT_TILES * P, D), F32).ap()
        self.bg = d("expert_biases", (MAXE, 2, BCOLS), F16).ap()

    def start(self):
        nc = self.nc
        self.tables(0)
        with ExitStack() as tmp:
            stats = tmp.enter_context(nc.sbuf_tensor("stats0", [P, NT, 6], F32))
            mv = tmp.enter_context(nc.sbuf_tensor("mv0", [P, NT, 2], F32))
            s_x, s_g = self.sem("x_loaded"), self.sem("gates_loaded")
            s_c, s_c2, s_v = self.sem("const_step"), self.sem("const_dve"), self.sem("stats0_step")
            n_const = 15
            prep_sync, prep_tensor, prep_scalar, prep_vector = self.prepare(0, tmp, lambda eng: eng.wait_ge(s_c, n_const))
            block = tmp.enter_context(nc.Block())
            ins = self.ins

            @block.tensor
            def _(pe):
                prep_tensor(pe)

            @block.sync
            def _(sp):
                sp.dma_start(self.gates_in[:], ins["gates"]).then_inc(s_g, 16)

                def rows():
                    for q in range(4):
                        t0 = q * NT // 4
                        sp.dma_start(self.x[:, t0:t0 + NT // 4, :],
                                     ins["x"][t0 * P:(t0 + NT // 4) * P, :].rearrange("(t p) d -> p t d", p=P)).then_inc(s_x, 16)

                prep_sync(sp, rows)

            @block.gpsimd
            def _(pool):
                step = Chain(pool, s_c)
                step(nc.gpsimd.memset(self.zeros[:], 0.0))
                step(nc.gpsimd.memset(self.ident[:], 0.0))
                step(nc.gpsimd.affine_select(out=self.ident[:], in_=self.ident[:], compare_op=ALU.not_equal, fill=1.0,
                                             base=0, pattern=[[-1, P]], channel_multiplier=1))
                step(nc.gpsimd.memset(self.ones_bf[:], 1.0))
                step(nc.gpsimd.affine_select(out=self.before[:], in_=self.ones_bf[:], compare_op=ALU.is_gt, fill=0.0,
                                             base=0, pattern=[[1, P]], channel_multiplier=-1))
                step(nc.gpsimd.memset(self.head_mask[:], 1.0))
                step(nc.gpsimd.affine_select(out=self.head_mask[:], in_=self.head_mask[:], compare_op=ALU.is_ge,
                                             fill=0.0, base=0, pattern=[[-HD, 8]], channel_multiplier=1))
                step(nc.gpsimd.affine_select(out=self.head_mask[:], in_=self.head_mask[:], compare_op=ALU.is_ge,
                                             fill=0.0, base=HD - 1, pattern=[[HD, 8]], channel_multiplier=-1))
                step(nc.gpsimd.memset(self.row_head[:], 1.0))
                for c in range(PC):
                    off = c * P - KEYS * chunk_heads(c)[0]
                    ins_ = nc.gpsimd.affine_select(out=self.row_head[:, c], in_=self.row_head[:, c], compare_op=ALU.is_ge, fill=0.0,
                                                   base=off, pattern=[[-KEYS, VH]], channel_multiplier=1)
                step(ins_)
                for c in range(PC):
                    off = c * P - KEYS * chunk_heads(c)[0]
                    ins_ = nc.gpsimd.affine_select(out=self.row_head[:, c], in_=self.row_head[:, c], compare_op=ALU.is_ge, fill=0.0,
                                                   base=KEYS - 1 - off, pattern=[[KEYS, VH]], channel_multiplier=-1)
                step(ins_)
                step(nc.gpsimd.memset(self.zeros16[:], 0.0))
                step(nc.gpsimd.memset(self.half[:], -0.5))
                step(nc.gpsimd.memset(self.ones_row[:], 1.0))
                step(nc.gpsimd.memset(self.ones16[:], 1.0))
                assert step.n == n_const, step.n
                pool.wait_ge(s_v, 2 * NT + 1)
                step(nc.gpsimd.tensor_tensor(self.rstd[:], self.rstd[:], self.half[:], ALU.pow))

            @block.scalar
            def _(act):
                act.wait_ge(s_g, 16)
                nc.scalar.activation(self.tg[:], self.gates_in[:], ACT.Tanh).then_inc(s_c2, 1)
                act.wait_ge(s_c2, 1)
                prep_scalar(act)

            @block.vector
            def _(dve):
                def statistics():
                    dve.wait_ge(s_x, 64)
                    for t in range(NT):
                        nc.vector.bn_stats(stats[:, t, :], self.x[:, t, :]).then_inc(s_v, 1)
                    dve.wait_ge(s_v, NT)
                    for t in range(NT):
                        nc.vector.bn_aggr(mv[:, t, :], stats[:, t, :]).then_inc(s_v, 1)
                    dve.wait_ge(s_v, 2 * NT)
                    nc.vector.tensor_copy(self.mean[:], mv[:, :, 0])
                    nc.vector.tensor_scalar(self.rstd[:], mv[:, :, 1], EPS, None, ALU.add).then_inc(s_v, 1)

                prep_vector(dve, statistics)

    def tables(self, L):
        self.table_ctx = ExitStack()
        sb = lambda name, shape, dt: self.table_ctx.enter_context(self.nc.sbuf_tensor(f"l{L}_{name}", shape, dt))
        self.wq, self.wo = sb("wq", [P, DC, D], F32), sb("wo", [P, DC, D], F32) if LAYERS[L]["out_proj"] else None
        self.wg, self.bg_row = sb("wg", [P, DC, ME], F32), sb("bg_row", [P, ME], F32)
        self.bq = sb("bq", [P, DC], F32)
        self.bo16 = sb("bo16", [1, 2, D], F16)
        self.keys_bd = sb("keys_bd", [P, B, NQ, HQ, KEYS], F32)
        self.vals = sb("vals", [P, B, PC, VH, HD + 1], F32)

    def bias_rows(self, E):
        room = self.weights[:, E:].rearrange("p e w n -> p (e w n)")
        assert E * BCOLS * 2 <= (MAXE - DEFER - E) * 2 * WCOLS
        return room[:, 0:2 * E * BCOLS].bitcast(F32).rearrange("p (e n) -> p e n", e=E)

    def lent(self, at, shape):
        size = 2 * int(np.prod(shape[1:]))
        assert at + size <= DEFER * 2 * WCOLS
        room = self.weights[:, MAXE - DEFER:].rearrange("p e w n -> p (e w n)")[0:shape[0], at:at + size].bitcast(F32)
        return at + size, room

    def prepare(self, L, stack, consts_ready):
        nc, cfg, ins = self.nc, LAYERS[L], self.ins
        out_proj, E = cfg["out_proj"], cfg["experts"]
        n_exp = E + cfg["shared"]
        pre = f"l{L}_"
        sem = lambda name: self.sem(pre + name)
        sbs = lambda name, shape, dt: stack.enter_context(nc.sbuf_tensor(pre + name, shape, dt))
        pss = lambda name, shape: stack.enter_context(nc.psum_tensor(pre + name, shape, F32))
        bk = sbs("bk", [P, DC], F32)
        ctx_t = sbs("ctx_t", [P, DC, B * KEYS], F32)
        wk, wv = sbs("wk", [P, DC, D], F32), sbs("wv", [P, DC, D], F32)
        bv = sbs("bv", [1, D], F32)
        bo = sbs("bo", [1, D], F32) if out_proj else None
        room = self.weights[:].rearrange("p e w n -> p (e w n)")
        row_key = room[0:KEYS, 0:2 * PROWS].bitcast(F32)
        b_f = room[0:MAXE, 2 * PROWS:2 * (PROWS + BCOLS)].bitcast(F32)
        at = 2 * (PROWS + BCOLS)
        v = room[0:KEYS, at:at + 2 * B * HEADS * (HD + 1)].bitcast(F32).rearrange("k (b h e) -> k b h e", b=B, h=HEADS)
        MT = U8 if L == 0 else I32
        m_row, m_col = sbs("m_row", [P, B * KEYS], MT), sbs("m_col", [KEYS, B], MT)
        valid, masked, valid_col = sbs("valid", [P, B * KEYS], F32), sbs("masked", [P, B * KEYS], F32), sbs("valid_col", [KEYS, B], F32)
        count, k_mean = sbs("count", [P, B], F32), sbs("k_mean", [P, DC, B], F32)
        k_fill = sbs("k_fill", [P, DC, B, KEYS], F32)
        kt = sbs("kt", [P, DC, B * KEYS], F32)
        at += 2 * B * HEADS * (HD + 1)
        b_s = room[0:MAXE, at:at + 2 * BCOLS].rearrange("e (w n) -> e w n", w=2)
        ps_k, ps_v, ps_r = pss("ps_k", [P, 512]), pss("ps_v", [P, B, D]), pss("ps_r", [P, B, 512])
        k_cols = [ps_k[:, j * B * KEYS:(j + 1) * B * KEYS] for j in range(DC)]
        v_rows = [ps_r[:, b, 0:PC * VH * (HD + 1)].rearrange("p (c j e) -> p c j e", c=PC, j=VH) for b in range(B)]
        s_ld, s_k, s_v, s_kt, s_d, s_b = (sem(x) for x in ("params_loaded", "k_done", "v_done", "kt_done", "setup_step", "biases_loaded"))
        s_bs, s_bst, s_mask, s_ml = sem("bias_split"), sem("biases_stored"), sem("mask_ready"), sem("mask_loaded")
        s_vals, s_bd, s_key, s_vkept, s_rows = (sem(x) for x in ("vals_ready", "keys_ready", "row_key_ready", "v_kept", "v_rows_done"))
        split = lambda ap: ap.rearrange("(c p) n -> p c n", p=P)

        def sync(sp, beside=lambda: None):
            for dst, src in ((m_row, ins[f"mask{L}"]), (m_col, ins[f"mask_col{L}"])):
                sp.dma_start(dst[:], src).then_inc(s_ml, 16)
            loads = [(ctx_t, split(ins["ctx_t"])), (wk, split(ins[f"wk{L}"])), (wv, split(ins[f"wv{L}"])),
                     (bk, ins[f"bk{L}"]), (bv, ins[f"bv{L}"]), 
                     (self.wq, split(ins[f"wq{L}"])), (self.bq, ins[f"bq{L}"]),
                     (self.wg[:, :, 0:E], split(ins[f"wg{L}"])), (self.bg_row[:, 0:E], ins[f"bg{L}"])]
            if out_proj:
                loads += [(self.wo, split(ins["wo0"])), (bo, ins["bo0"])]
            for dst, src in loads:
                sp.dma_start(dst if isinstance(dst, bass.AP) else dst[:], src).then_inc(s_ld, 16)
            sp.dma_start(b_f[0:n_exp, :], ins[f"biases{L}"]).then_inc(s_b, 16)
            beside()
            sp.wait_ge(s_bs, 3)
            sp.dma_start(self.bg[0:n_exp], b_s[0:n_exp]).then_inc(s_bst, 16)
            sp.wait_ge(s_bst, 16)

        n_loads = 16 * (11 if out_proj else 9)

        def tensor(pe, beside=lambda: None):
            pe.wait_ge(s_ld, n_loads)
            for j in range(DC):
                for c in range(DC):
                    mm = nc.tensor.matmul(k_cols[j], wk[:, c, j * P:(j + 1) * P], ctx_t[:, c, :],
                                          start=(c == 0), stop=(c == DC - 1))
                mm.then_inc(s_k, 1)
            consts_ready(pe)
            for b in range(B):
                for c in range(DC):
                    nc.tensor.matmul(ps_v[0:KEYS, b, 0:D], ctx_t[:, c, b * KEYS:(b + 1) * KEYS], wv[:, c, :],
                                     start=(c == 0), stop=False)
                nc.tensor.matmul(ps_v[0:KEYS, b, 0:D], self.ones_row[:, 0:KEYS], bv[:], start=False, stop=True).then_inc(s_v, 1)
            pe.wait_ge(s_key, 1)
            for b in range(B):
                if b == B - 1:
                    beside()
                pe.wait_ge(s_vkept, b + 1)
                for k in range(PC):
                    rows, (h0, nh) = chunk_rows(k), chunk_heads(k)
                    mm = nc.tensor.matmul(v_rows[b][0:rows, k, 0:nh].rearrange("p j e -> p (j e)"), row_key[:, k * P:k * P + rows],
                                          v[:, b, h0:h0 + nh].rearrange("k h e -> k (h e)"), start=True, stop=True)
                mm.then_inc(s_rows, 1)

        def scalar(act):
            consts_ready(act)
            nc.scalar.copy(row_key.rearrange("p (h k) -> p h k", h=HEADS),
                           self.ident[0:KEYS, 0:KEYS].unsqueeze(1).broadcast_to([KEYS, HEADS, KEYS])).then_inc(s_key, 1)
            act.wait_ge(s_k, DC)
            for j in range(DC):
                nc.scalar.activation(kt[:, j, :], k_cols[j], ACT.Identity,
                                     bias=bk[:, j:j + 1]).then_inc(s_kt, 1)
            act.wait_ge(s_v, B)
            act.wait_ge(s_mask, 1)
            for b in range(B):
                nc.scalar.copy(v[:, b, :, HD:HD + 1], valid_col[:, b:b + 1].unsqueeze(1).broadcast_to([KEYS, HEADS, 1]))
                nc.scalar.activation(v[:, b, :, 0:HD], ps_v[0:KEYS, b, :].rearrange("k (h d) -> k h d", h=HEADS), ACT.Copy,
                                     scale=valid_col[:, b:b + 1]).then_inc(s_vkept, 1)
            act.wait_ge(s_b, 16)
            nc.scalar.mul(b_f[0:n_exp, :], b_f[0:n_exp, :], WSCALE).then_inc(s_bs, 1)
            act.wait_ge(s_bs, 1)
            nc.scalar.copy(b_s[0:n_exp, 0, :], b_f[0:n_exp, :]).then_inc(s_bs, 1)

        def vector(dve, beside=lambda: None, beside_late=lambda: None):
            step = Chain(dve, s_d)
            step(nc.vector.memset(self.vals[:], 0.0))
            dve.wait_ge(s_ml, 32)
            counts = ALU.is_gt if L == 0 else ALU.is_le
            step(nc.vector.tensor_scalar(valid_col[:], m_col[:], 0.0, None, counts))
            nc.vector.tensor_scalar(valid[:], m_row[:], 0.0, None, counts).then_inc(s_mask, 1)
            dve.wait_ge(s_mask, 1)
            step(nc.vector.tensor_reduce(count[:], valid[:].rearrange("p (b k) -> p b k", b=B), AX_X, ALU.add))
            step(nc.vector.reciprocal(count[:], count[:]))
            step(nc.vector.tensor_scalar(masked[:], valid[:], -1.0, 1.0, ALU.mult, ALU.add))
            beside()
            dve.wait_ge(s_bs, 2)
            nc.vector.tensor_tensor(b_s[0:n_exp, 1, :], b_f[0:n_exp, :], b_s[0:n_exp, 0, :],
                                    ALU.subtract).then_inc(s_bs, 1)
            consts_ready(dve)
            dve.wait_ge(s_kt, DC)
            by_chunk = lambda ap: ap.unsqueeze(1).broadcast_to([P, DC, B * KEYS])
            step(nc.vector.tensor_tensor(kt[:], kt[:], by_chunk(valid[:]), ALU.mult))
            step(nc.vector.tensor_reduce(k_mean[:], kt[:].rearrange("p c (b k) -> p c b k", b=B), AX_X, ALU.add))
            step(nc.vector.tensor_tensor(k_mean[:], k_mean[:], count[:].unsqueeze(1).broadcast_to([P, DC, B]), ALU.mult))
            for c in range(DC):
                ins_ = nc.vector.tensor_tensor(k_fill[:, c], masked[:].rearrange("p (b k) -> p b k", b=B),
                                               k_mean[:, c].unsqueeze(2).broadcast_to([P, B, KEYS]), ALU.mult)
            step(ins_)
            step(nc.vector.tensor_tensor(kt[:], kt[:], k_fill[:].rearrange("p c b k -> p c (b k)"), ALU.add))
            for b in range(B):
                for j in range(DC):
                    src = kt[:, j, b * KEYS:(b + 1) * KEYS].unsqueeze(1).broadcast_to([P, 8, KEYS])
                    msk = self.head_mask[:].unsqueeze(2).broadcast_to([P, 8, KEYS])
                    dst = self.keys_bd[:, b, 2 * j:2 * j + 2].rearrange("p q h k -> p (q h) k")
                    nc.vector.tensor_tensor(dst, src, msk, ALU.mult).then_inc(s_bd, 1)
            beside_late()
            for b in range(B):
                dve.wait_ge(s_rows, b + 1)
                for k in range(PC):
                    rows, (h0, nh) = chunk_rows(k), chunk_heads(k)
                    own = self.row_head[0:rows, k, 0:nh].unsqueeze(2).broadcast_to([rows, nh, HD + 1])
                    nc.vector.tensor_tensor(self.vals[0:rows, b, k, 0:nh, :], v_rows[b][0:rows, k, 0:nh], own, ALU.mult)
            if out_proj:
                step(nc.vector.tensor_copy(self.bo16[:, 0], bo[:]))
                nc.vector.tensor_tensor(self.bo16[:, 1], bo[:], self.bo16[:, 0], ALU.subtract)

        return sync, tensor, scalar, vector

    def attention(self, L):
        nc, cfg, ins = self.nc, LAYERS[L], self.ins
        out_proj, E = cfg["out_proj"], cfg["experts"]
        n_exp = E + cfg["shared"]
        pre = f"l{L}_"
        sem = lambda name: self.sem(pre + name)
        wq, wo, bq, bo16 = self.wq, self.wo, self.bq, self.bo16
        keys_bd, vals = self.keys_bd, self.vals
        with ExitStack() as tmp:
            sb = lambda name, shape, dt: tmp.enter_context(nc.sbuf_tensor(pre + name, shape, dt))
            psb = lambda name, shape: tmp.enter_context(nc.psum_tensor(pre + name, shape, F32))
            rows_n = sb("rows_n", [P, 2, D], F32)
            xn, q_t = sb("xn", [P, 2, D], F32), sb("q_t", [P, 2, DC, P], F32)
            xn_t = sb("xn_t", [P, 2, 2, DC, P], F32)
            at, probs = self.lent(0, [P, 2 * PROWS])
            probs = probs.rearrange("p (u h k) -> p u h k", u=2, h=HEADS)
            at, probs_t = self.lent(at, [P, PC * P])
            probs_t = probs_t.rearrange("p (c t) -> p c t", c=PC)
            at, stage = self.lent(at, [P, 2 * WPART])
            stage = stage.rearrange("p (u n) -> p u n", u=2)
            smax = sb("smax", [P, 2, NQ, HQ], F32)
            rec, att = sb("rec", [P, HEADS, 1], F32), sb("att", [P, HEADS, HD], F32)
            att_t = sb("att_t", [P, DC, P], F32)
            stats, mv1, x_new = sb("stats", [P, 6], F32), sb("mv1", [P, 2], F32), sb("x_new", [P, D], F32)
            ps_s = psb("ps_s", [P, NQ, 512])
            ps_tq, ps_tx, ps_ta, ps_o_bank = (psb(x, [P, 512]) for x in ("ps_tq", "ps_tx", "ps_ta", "ps_o"))
            scores = ps_s[:, :, 0:HQ * KEYS].rearrange("p q (h k) -> p q h k", h=HQ)
            ps_q, ps_o = ps_tq[:, 0:D], ps_o_bank[:, 0:D]
            ps_av = ps_ta[:, 0:HEADS * (HD + 1)].rearrange("p (h e) -> p h e", h=HEADS)
            ps_l = ps_ta[:, HEADS * (HD + 1):HEADS * (HD + 1) + NT * E].rearrange("p (t e) -> p t e", t=NT)
            rounds = [range(r, min(r + PROUND, PC)) for r in range(0, PC, PROUND)]
            turned_at = [ps[:].rearrange("p (c t) -> p c t", c=PROUND) for ps in (ps_tq, ps_tx, ps_ta)]
            NR = len(rounds)
            names = ("xn_ready", "xt_done", "xn_t_ready", "q_done", "q_t_ready", "scores_done", "smax_step", "shifted",
                     "probs_ready", "turned", "pt_ready", "av_done", "att_step", "att_turned",
                     "att_t_ready", "proj_done", "x_updated", "stats_step", "rows_ready", "rows_kept", "logits_done", "w_high", "w_low", "rstd_done", "logits_out")
            s = {n: sem(n) for n in names}
            self.rows_stored, self.biases_in = sem("rows_stored"), sem("biases_in")
            s_stage, s_fill = [sem("w_staged0"), sem("w_staged1")], sem("slots_filled")
            block = tmp.enter_context(nc.Block())
            tile_of = lambda un: un.i + TB * un.u
            UPD = 2 if out_proj else 1
            LEAD, LAG = 3, UPD + 2
            n_split = n_exp if n_exp <= MAXE - DEFER else MAXE - DEFER
            per_unit = -(-2 * n_split // NT)
            assert per_unit in (1, 2)

            def pieces(un):
                if isinstance(un.n, int) and un.n * per_unit >= 2 * n_split:
                    return []
                return [(un.n, 0), (un.n, 1)] if per_unit == 2 else [(un.i, un.u)]

            @block.sync
            def _(sp):
                def load(e, has):
                    for m in range(2):
                        sp.wait_ge(s["w_low"], e.n * 2 + m + 1)
                        sp.dma_start(stage[:, m, :], ins[f"weights{L}"][bass.ds(e.n, 1), :, m * WPART:(m + 1) * WPART]
                                     .rearrange("e p n -> p (e n)")).then_inc(s_stage[m], 16)
                    if L == 0:
                        sp.dma_start(self.xg[bass.ds(e.n * (FILL * P) + FILL_FROM * P, FILL * P), :].rearrange("(a p) d -> p a d", p=P),
                                     self.zeros[:].unsqueeze(1).broadcast_to([P, FILL, D])).then_inc(s_fill, 16)

                run_pipeline(sp, load, n_split, 0, 0)
                if L == 0:
                    sp.wait_ge(s_fill, 16 * n_split)
                if cfg["by_slot"]:
                    src = ins[f"biases{L}"].rearrange("e n -> (e n)").unsqueeze(0).broadcast_to([P, E * BCOLS])
                    sp.dma_start(self.bias_rows(E).rearrange("p e n -> p (e n)"), src).then_inc(self.biases_in, 16)
                    for n in range(NT):
                        T = tile_of(Unit(0, n))
                        sp.wait_ge(s["rows_kept"], n + 3)
                        sp.dma_start(self.xd[T * P:(T + 1) * P, :], self.xn[:, T, :]).then_inc(self.rows_stored, 16)

            @block.gpsimd
            def _(pool):
                pool.sem_inc(s["rows_kept"], 2)
                for n in range(NT + 1):
                    if n < NT:
                        T = tile_of(Unit(0, n))
                        pool.wait_ge(s["stats_step"], 3 * n + 3)
                        nc.gpsimd.tensor_tensor(self.rstd[:, T:T + 1], self.rstd[:, T:T + 1], self.half[:, 0:1], ALU.pow).then_inc(s["rstd_done"], 1)
                    if n >= 1:
                        T = tile_of(Unit(0, n - 1))
                        pool.wait_ge(s["rows_ready"], n)
                        nc.gpsimd.tensor_copy(self.xn[:, T, :], rows_n[:, (n - 1) % 2, :]).then_inc(s["rows_kept"], 1)

            @block.tensor
            def _(pe):
                def step(un, has):
                    n = un.n
                    if has(1):
                        a = un.shifted(1)
                        pe.wait_ge(s["q_t_ready"], DC * a.n + DC)
                        pe.wait_ge(s["shifted"], a.n + 1)
                        for q in range(NQ):
                            mm = nc.tensor.matmul(ps_s[:, q, 0:HQ * KEYS], q_t[:, a.u, q // 2, :],
                                                  keys_bd[:, a.u, q].rearrange("p h k -> p (h k)"), start=True, stop=True)
                        mm.then_inc(s["scores_done"], 1)
                    if has(0):
                        pe.wait_ge(s["probs_ready"], n + 1)
                        rows_of = probs[:, un.u].rearrange("p h k -> p (h k)")
                        for r, chunks in enumerate(rounds):
                            if r == 1:
                                pe.wait_ge(s["xn_t_ready"], n + 3)
                            if r == 2:
                                pe.wait_ge(s["att_step"], 2 * n + 2)
                            for i, c in enumerate(chunks):
                                mm = nc.tensor.transpose(turned_at[r][0:chunk_rows(c), i, :], rows_of[:, c * P:c * P + chunk_rows(c)], self.ident[:])
                            mm.then_inc(s["turned"], 1)
                    if has(-1) and out_proj:
                        c = un.shifted(-1)
                        pe.wait_ge(s["att_step"], 2 * n + 2)
                        pe.wait_ge(s["x_updated"], n)
                        for j in range(DC):
                            mm = nc.tensor.transpose(ps_o[:, j * P:(j + 1) * P],
                                                     att[:].rearrange("p h d -> p (h d)")[:, j * P:(j + 1) * P], self.ident[:])
                        mm.then_inc(s["att_turned"], 1)
                    if has(2):
                        a = un.shifted(2)
                        pe.wait_ge(s["xn_t_ready"], a.n + 1)
                        if has(0):
                            pe.wait_ge(s["pt_ready"], NR * n + 1)
                        for j in range(DC):
                            for c in range(DC):
                                mm = nc.tensor.matmul(ps_q[:, j * P:(j + 1) * P], wq[:, c, j * P:(j + 1) * P], xn_t[:, a.u, 0, c, :],
                                                      start=(c == 0), stop=(c == DC - 1))
                        mm.then_inc(s["q_done"], 1)
                    if has(3) or has(-UPD - 1):
                        if has(0):
                            pe.wait_ge(s["pt_ready"], NR * n + 2)
                        elif not (isinstance(n, int) and n == -LEAD):
                            pe.wait_ge(s["xn_t_ready"], n + 3)
                        if has(3):
                            a = un.shifted(3)
                            pe.wait_ge(s["xn_ready"], a.n + 1)
                            for j in range(DC):
                                mm = nc.tensor.transpose(ps_tx[:, j * P:(j + 1) * P], xn[:, a.u, j * P:(j + 1) * P], self.ident[:])
                        if has(-UPD - 1):
                            c = un.shifted(-UPD - 1)
                            pe.wait_ge(s["rows_ready"], c.n + 1)
                            for j in range(DC):
                                mm = nc.tensor.transpose(ps_tx[:, D + j * P:D + (j + 1) * P], rows_n[:, c.u, j * P:(j + 1) * P], self.ident[:])
                        mm.then_inc(s["xt_done"], 1)
                    if has(-1) and out_proj:
                        pe.wait_ge(s["att_t_ready"], n)
                        for j in range(DC):
                            nc.tensor.matmul(ps_o, att_t[:, j, :], wo[:, j, :], start=(j == 0), stop=False)
                        nc.tensor.matmul(ps_o, self.ones16[0:1, :], bo16[:, 0], start=False, stop=False)
                        nc.tensor.matmul(ps_o, self.ones16[0:1, :], bo16[:, 1], start=False, stop=True).then_inc(s["proj_done"], 1)
                    if has(-UPD - 2):
                        c = un.shifted(-UPD - 2)
                        pe.wait_ge(s["xn_t_ready"], n + 3)
                        if has(0):
                            pe.wait_ge(s["pt_ready"], NR * n + NR)
                        else:
                            pe.wait_ge(s["att_step"], 2 * NT + 2)
                        for j in range(DC):
                            mm = nc.tensor.matmul(ps_l[:, bass.ds(tile_of(c), 1), :].rearrange("p a e -> p (a e)"),
                                                  xn_t[:, un.shifted(2).u, 1, j, :], self.wg[:, j, 0:E], start=(j == 0), stop=(j == DC - 1))
                        mm.then_inc(s["logits_done"], 1)
                    if has(0):
                        pe.wait_ge(s["pt_ready"], NR * n + NR)
                        nc.tensor.matmul(ps_ta[:, 0:HEADS * (HD + 1)], self.zeros16[:, 0:P], self.zeros16[:], start=True, stop=True)
                        for c in range(PC):
                            h0, nh = chunk_heads(c)
                            mm = nc.tensor.matmul(ps_av[:, h0:h0 + nh, :].rearrange("p h e -> p (h e)"), probs_t[0:chunk_rows(c), c, :],
                                                  vals[0:chunk_rows(c), un.u, c, 0:nh, :].rearrange("p j e -> p (j e)"),
                                                  start=False, stop=True, skip_group_check=True)
                        mm.then_inc(s["av_done"], 1)
                run_pipeline(pe, step, NT, LEAD, LAG)

            @block.scalar
            def _(act):
                def weight_high(pieces):
                    for e, m in pieces:
                        act.wait_ge(s_stage[m], 16 * e + 16)
                        nc.scalar.activation(self.weights[:, bass.ds(e, 1), 0, m * WPART:(m + 1) * WPART].rearrange("p a n -> p (a n)"),
                                             stage[:, m, :], ACT.Copy, scale=WSCALE).then_inc(s["w_high"], 1)

                def step(un, has):
                    n = un.n
                    if has(0):
                        act.wait_ge(s["shifted"], n + 2)
                        rows_of = probs[:, un.u].rearrange("p h k -> p (h k)")
                        nc.scalar.activation(rows_of, rows_of, ACT.Exp, scale=float(HD) ** -0.5).then_inc(s["probs_ready"], 1)
                        weight_high(pieces(un)[:1])
                        for r, chunks in enumerate(rounds):
                            act.wait_ge(s["turned"], NR * n + r + 1)
                            if chunk_rows(chunks[-1]) < P:
                                nc.scalar.copy(probs_t[:, chunks[0]:chunks[-1], :], turned_at[r][:, 0:len(chunks) - 1, :])
                                rows = chunk_rows(chunks[-1])
                                nc.scalar.copy(probs_t[0:rows, chunks[-1], :], turned_at[r][0:rows, len(chunks) - 1, :]).then_inc(s["pt_ready"], 1)
                            else:
                                nc.scalar.copy(probs_t[:, chunks[0]:chunks[-1] + 1, :], turned_at[r][:, 0:len(chunks), :]).then_inc(s["pt_ready"], 1)
                    if has(-1) and out_proj:
                        act.wait_ge(s["att_turned"], n)
                        nc.scalar.copy(att_t[:].rearrange("p c t -> p (c t)"), ps_o).then_inc(s["att_t_ready"], 1)
                    if has(2):
                        a = un.shifted(2)
                        act.wait_ge(s["q_done"], a.n + 1)
                        for j in range(DC):
                            nc.scalar.activation(q_t[:, a.u, j, :], ps_q[:, j * P:(j + 1) * P], ACT.Identity,
                                                 bias=bq[:, j:j + 1]).then_inc(s["q_t_ready"], 1)
                    if has(3) or has(-UPD - 1):
                        lo, hi = (0 if has(3) else 1), (2 if has(-UPD - 1) else 1)
                        act.wait_ge(s["xt_done"], n + 4)
                        nc.scalar.copy(xn_t[:, un.shifted(3).u, lo:hi].rearrange("p k c t -> p (k c t)"), ps_tx[:, lo * D:hi * D]).then_inc(s["xn_t_ready"], 1)
                    if has(0):
                        weight_high(pieces(un)[1:])

                run_pipeline(act, step, NT, LEAD, LAG)

            @block.vector
            def _(dve):
                dve.sem_inc(s["x_updated"], 1)
                dve.sem_inc(s["shifted"], 1)
                dve.sem_inc(s["att_step"], 2)
                dve.sem_inc(s["w_low"], 2)

                def weight_low(pieces):
                    for e, m in pieces:
                        dve.wait_ge(s["w_high"], e * 2 + m + 1)
                        high, low = (self.weights[:, bass.ds(e, 1), w, m * WPART:(m + 1) * WPART].rearrange("p a n -> p (a n)") for w in (0, 1))
                        nc.vector.scalar_tensor_tensor(out=low, in0=stage[:, m, :], scalar=WSCALE, in1=high,
                                                       op0=ALU.mult, op1=ALU.subtract).then_inc(s["w_low"], 1)

                def residual(c):
                    row = self.x[:, bass.ds(tile_of(c), 1), :].rearrange("p a d -> p (a d)")
                    if out_proj:
                        dve.wait_ge(s["proj_done"], c.n + 1)
                    else:
                        dve.wait_ge(s["att_step"], 2 * c.n + 4)
                    branch = ps_o if out_proj else att[:].rearrange("p h d -> p (h d)")
                    nc.vector.scalar_tensor_tensor(out=x_new[:], in0=branch, scalar=self.tg[:, 2 * L:2 * L + 1],
                                                   in1=row, op0=ALU.mult, op1=ALU.add).then_inc(s["x_updated"], 1)

                def residual_sums(c):
                    dve.wait_ge(s["x_updated"], c.n + 2)
                    nc.vector.bn_stats(stats[:], x_new[:]).then_inc(s["stats_step"], 1)

                def keep_row(c):
                    dve.wait_ge(s["stats_step"], 3 * c.n + 1)
                    nc.vector.tensor_scalar(self.x[:, bass.ds(tile_of(c), 1), :].rearrange("p a d -> p (a d)"), x_new[:], 0.0, None, ALU.add)
                    nc.vector.bn_aggr(mv1[:], stats[:]).then_inc(s["stats_step"], 1)

                def keep_mean(c):
                    dve.wait_ge(s["stats_step"], 3 * c.n + 2)
                    nc.vector.tensor_scalar(self.mean[:, bass.ds(tile_of(c), 1)], mv1[:, 0:1], 0.0, None, ALU.add)
                    nc.vector.tensor_scalar(self.rstd[:, bass.ds(tile_of(c), 1)], mv1[:, 1:2], EPS, None, ALU.add).then_inc(s["stats_step"], 1)

                def reciprocals(c):
                    dve.wait_ge(s["av_done"], c.n + 1)
                    nc.vector.reciprocal(rec[:], ps_av[:, :, HD:HD + 1]).then_inc(s["att_step"], 1)

                def heads(c):
                    dve.wait_ge(s["att_step"], 2 * c.n + 3)
                    nc.vector.tensor_tensor(att[:], ps_av[:, :, 0:HD], rec[:].broadcast_to([P, HEADS, HD]),
                                            ALU.mult).then_inc(s["att_step"], 1)

                def rows_in(a, n):
                    T = tile_of(a)
                    if not (isinstance(n, int) and n < -1):
                        dve.wait_ge(s["xt_done"], n + 2)
                    nc.vector.tensor_scalar(xn[:, a.u, :], self.x[:, bass.ds(T, 1), :].rearrange("p a d -> p (a d)"),
                                            self.mean[:, bass.ds(T, 1)], self.rstd[:, bass.ds(T, 1)],
                                            ALU.subtract, ALU.mult).then_inc(s["xn_ready"], 1)

                def rows_out(c):
                    T = tile_of(c)
                    dve.wait_ge(s["rstd_done"], c.n + 1)
                    dve.wait_ge(s["rows_kept"], c.n + 1)
                    nc.vector.tensor_scalar(rows_n[:, c.u, :], self.x[:, bass.ds(T, 1), :].rearrange("p a d -> p (a d)"),
                                            self.mean[:, bass.ds(T, 1)], self.rstd[:, bass.ds(T, 1)],
                                            ALU.subtract, ALU.mult).then_inc(s["rows_ready"], 1)

                def maxima(a):
                    dve.wait_ge(s["scores_done"], a.n + 1)
                    nc.vector.tensor_reduce(smax[:, a.u], scores, AX_X, ALU.max).then_inc(s["smax_step"], 1)

                def shift(a):
                    dve.wait_ge(s["smax_step"], a.n + 1)
                    nc.vector.tensor_tensor(probs[:, a.u].rearrange("p (q h) k -> p q h k", q=NQ), scores,
                                            smax[:, a.u].unsqueeze(3).broadcast_to([P, NQ, HQ, KEYS]),
                                            ALU.subtract).then_inc(s["shifted"], 1)

                def step(un, has):
                    n, c = un.n, un.shifted(-UPD)
                    if out_proj:
                        if has(-UPD):
                            residual(c)
                        if has(-1):
                            reciprocals(un.shifted(-1))
                        if has(-UPD):
                            residual_sums(c)
                        if has(-1):
                            heads(un.shifted(-1))
                        if has(-UPD):
                            keep_row(c)
                        if has(3):
                            rows_in(un.shifted(3), n)
                        if has(-UPD):
                            keep_mean(c)
                    else:
                        if has(3):
                            rows_in(un.shifted(3), n)
                        if has(-1):
                            reciprocals(c)
                            heads(c)
                            residual(c)
                            residual_sums(c)
                    if has(1):
                        maxima(un.shifted(1))
                    if has(-UPD - 1):
                        rows_out(un.shifted(-UPD - 1))
                    if has(1):
                        shift(un.shifted(1))
                    if not out_proj and has(-1):
                        keep_row(c)
                    if has(0):
                        weight_low(pieces(un))
                    if not out_proj and has(-1):
                        keep_mean(c)

                run_pipeline(dve, step, NT, LEAD, LAG)
                dve.wait_ge(s["logits_done"], NT)
                nc.vector.tensor_tensor(self.logits[:, :, 0:E], ps_l, self.bg_row[:, 0:E].unsqueeze(1).broadcast_to([P, NT, E]),
                                        ALU.add).then_inc(s["logits_out"], 1)
                dve.wait_ge(s["logits_out"], 1)
        self.table_ctx.close()

    def eid_tables(self, L, sb):
        R, E = routed_tiles(L), LAYERS[L]["experts"]
        return sb("past", [1, R, E], F32), sb("routed_eid", [1, R], F32)

    def expert_of_tiles(self, L, tables, step):
        v, (past, eid_f) = self.nc.vector, tables
        R, E, shared = routed_tiles(L), LAYERS[L]["experts"], LAYERS[L]["shared"]
        step(v.tensor_tensor(past[:], self.tile_no[:, 0:R].unsqueeze(2).broadcast_to([1, R, E]),
                             self.ends[0:1, 0:E].unsqueeze(1).broadcast_to([1, R, E]), ALU.is_ge))
        step(v.tensor_reduce(eid_f[:], past[:], AX_X, ALU.add))
        step(v.tensor_scalar(eid_f[:], eid_f[:], float(E - 1), float(shared), ALU.min, ALU.add))
        step(v.tensor_copy(self.eid[:, shared * NT:shared * NT + R], eid_f[:]))

    def route(self, L):
        nc, cfg, ins = self.nc, LAYERS[L], self.ins
        E, K, shared = cfg["experts"], cfg["topk"], cfg["shared"]
        R = routed_tiles(L)
        pre = f"l{L}_"
        sem = lambda name: self.sem(pre + name)
        logits, slots, gate = self.logits[:, :, 0:E], self.slots[:, :, 0:K], self.gate[:, :, 0:K]
        with ExitStack() as tmp:
            sb = lambda name, shape, dt: tmp.enter_context(nc.sbuf_tensor(pre + name, shape, dt))
            psb = lambda name, shape: tmp.enter_context(nc.psum_tensor(pre + name, shape, F32))
            iota_e, iota_n = sb("iota_e", [P, E], F32), self.tile_no[:, 0:R]
            mx, den = sb("mx", [P, NT], F32), sb("den", [P, NT], F32)
            prob = sb("prob", [P, NT, E], F32)
            top8, idx8 = sb("top8", [P, NT, 8], F32), sb("idx8", [P, NT, 8], mybir.dt.uint32)
            idx_f = sb("idx_f", [P, NT, 8], F32)
            chosen = sb("chosen", [P, K, NT, E], F32)
            mask = sb("mask", [P, NT, E], BF16)
            tot_i, tiles, zero_e = sb("tot_i", [P, E], I32), sb("tiles", [P, E], F32), sb("zero_e", [P, E], F32)
            ends, first = self.ends[:, 0:E], sb("first_slot", [P, E], F32)
            slot_of, pick = sb("slot_of", [P, NT, E], F32), sb("pick", [P, NT, E], F32)
            slot_f = sb("slot_f", [P, NT, K], F32)
            eid_f = sb("eid_f", [1, NT * shared], F32) if shared else None
            eid_tables = self.eid_tables(L, sb) if not shared else None
            ps_rank, ps_tot = psb("ps_rank", [P, 512]), psb("ps_tot", [P, 512])
            q = {n: sem("q_" + n) for n in ("shifted", "exp", "mask", "rank", "iota", "step", "tile_hit", "place_hit", "token_part", "pairs", "halves", "totals", "hit")}
            if cfg["by_slot"]:
                NK = NT * K
                assert K & (K - 1) == 0
                room = self.weights[:, MAXE - DEFER:].rearrange("p e w n -> p (e w n)")
                place_hit = room[:, 0:NK * P].rearrange("p (k s) -> p k s", k=NK)
                tile_hit = room[:, NK * P:NK * (P + 2 * R)].rearrange("p (k v n) -> p k v n", k=NK, v=2)
                assert NK * (P + 2 * R) <= DEFER * 2 * WCOLS
                slot_i, place_i, tile_i = (sb(x, [P, NK], I32) for x in ("slot_i", "place_i", "tile_i"))
                place_f, tile_f, pair_no = (sb(x, [P, NK], F32) for x in ("place_f", "tile_f", "pair_no"))
                hit = sb("hit", [P, NK, R], F32)
                iota_s, iota_t, token, spare = sb("iota_s", [P, P], F32), sb("iota_t", [P, R], F32), sb("token", [P, 1], F32), sb("spare", [P, R], F32)
                found = sb("found", [P, 2, R], F32)
                none, number, tok_f, dest = (sb(x, [P, R], F32) for x in ("none", "number", "tok_f", "dest"))
                number_i = sb("number_i", [P, R], I32)
                ps_found = psb("ps_found", [P, 512])
                PARTS = 4
            bc = lambda ap: ap.unsqueeze(2).broadcast_to([P, NT, E])

            with nc.Block() as block:
                @block.gpsimd
                def _(pool):
                    nc.gpsimd.iota(iota_e[:], pattern=[[1, E]], base=0, channel_multiplier=0,
                                   allow_small_or_imprecise_dtypes=True).then_inc(q["iota"], 1)
                    nc.gpsimd.iota(iota_n, pattern=[[1, R]], base=0, channel_multiplier=0,
                                   allow_small_or_imprecise_dtypes=True).then_inc(q["iota"], 1)
                    nc.gpsimd.memset(zero_e[:], 0.0).then_inc(q["iota"], 1)
                    if cfg["by_slot"]:
                        for table, pattern, base, step in ((iota_s, [[1, P]], 0, 0), (iota_t, [[1, R]], 0, 0), (pair_no, [[1, NK]], 1, 0),
                                                           (token, [[0, 1]], 0, 1), (spare, [[P, R]], (NK + 1) * P, 1)):
                            nc.gpsimd.iota(table[:], pattern=pattern, base=base, channel_multiplier=step,
                                           allow_small_or_imprecise_dtypes=True).then_inc(q["iota"], 1)
                        pool.wait_ge(q["hit"], 1)
                        nc.gpsimd.tensor_tensor(tile_hit[:, :, 1, :], hit[:], pair_no[:].unsqueeze(2).broadcast_to([P, NK, R]),
                                                ALU.mult).then_inc(q["tile_hit"], 1)

                @block.scalar
                def _(act):
                    act.wait_ge(q["shifted"], 1)
                    nc.scalar.activation(prob[:], prob[:], ACT.Exp, scale=cfg["inv_temp"]).then_inc(q["exp"], 1)
                    if cfg["by_slot"]:
                        act.wait_ge(q["hit"], 1)
                        nc.scalar.activation(tile_hit[:, :, 0, :], hit[:], ACT.Copy, scale=token[:]).then_inc(q["token_part"], 1)

                @block.tensor
                def _(pe):
                    pe.wait_ge(q["mask"], 1)
                    for t in range(NT):
                        mm = nc.tensor.matmul(ps_tot[:, 0:E], self.ones_bf[:], mask[:, t, :], start=(t == 0), stop=(t == NT - 1))
                    mm.then_inc(q["totals"], 1)
                    flat = lambda ap: ap.rearrange("p t e -> p (t e)")
                    ranks = ps_rank[:, 0:NT * E].rearrange("p (t e) -> p t e", t=NT)
                    nc.tensor.matmul(ps_rank[:, 0:NT * E], self.before[:], flat(mask[:]), start=True, stop=False)
                    for t in range(NT - 1):
                        mm = nc.tensor.matmul(ranks[:, t + 1:, :], self.ones_bf[:],
                                         mask[:, t:t + 1, :].broadcast_to([P, NT - 1 - t, E]), start=False, stop=(t == NT - 2))
                    mm.then_inc(q["rank"], 1)
                    if cfg["by_slot"]:
                        pe.wait_ge(q["token_part"], 1)
                        pe.wait_ge(q["tile_hit"], 1)
                        for k in range(NK):
                            if k % (NK // PARTS) == 0:
                                pe.wait_ge(q["place_hit"], 1 + k // (NK // PARTS))
                            mm = nc.tensor.matmul(ps_found[:, 0:2 * R], place_hit[:, k, :], tile_hit[:, k].rearrange("p v n -> p (v n)"),
                                                  start=(k == 0), stop=(k == NK - 1))
                        mm.then_inc(q["pairs"], 1)

                @block.vector
                def _(dve):
                    v, step = nc.vector, Chain(dve, q["step"])
                    step(v.tensor_reduce(mx[:], logits, AX_X, ALU.max))
                    v.tensor_tensor(prob[:], logits, bc(mx[:]), ALU.subtract).then_inc(q["shifted"], 1)
                    dve.wait_ge(q["exp"], 1)
                    for t in range(NT):
                        ins_ = v.max(out=top8[:, t, :], in_=prob[:, t, :])
                    step(ins_)
                    for t in range(NT):
                        ins_ = v.max_index(out=idx8[:, t, :], in_max=top8[:, t, :], in_values=prob[:, t, :])
                    step(ins_)
                    step(v.tensor_copy(idx_f[:], idx8[:]))
                    dve.wait_ge(q["iota"], 3)
                    for j in range(K):
                        ins_ = v.tensor_tensor(chosen[:, j], bc(idx_f[:, :, j]), iota_e[:].unsqueeze(1).broadcast_to([P, NT, E]), ALU.is_equal)
                    step(ins_)
                    for j in range(1, K):
                        last = j == K - 1
                        ins_ = v.tensor_tensor(mask[:] if last else pick[:], chosen[:, 0] if j == 1 else pick[:], chosen[:, j], ALU.add)
                        if not last:
                            step(ins_)
                    ins_.then_inc(q["mask"], 1)
                    step(v.tensor_reduce(den[:], prob[:], AX_X, ALU.add))
                    step(v.reciprocal(den[:], den[:]))
                    by_choice = lambda ap: ap.unsqueeze(2).broadcast_to([P, NT, K])
                    step(v.tensor_tensor(gate, top8[:, :, 0:K], by_choice(den[:]), ALU.mult))
                    if cfg["renorm"]:
                        step(v.tensor_reduce(den[:], gate, AX_X, ALU.add))
                        step(v.tensor_scalar(den[:], den[:], 1e-9, None, ALU.add))
                        step(v.reciprocal(den[:], den[:]))
                        step(v.tensor_tensor(gate, gate, by_choice(den[:]), ALU.mult))
                    for h in range(shared):
                        v.memset(eid_f[:].rearrange("a (t h) -> a t h", h=shared)[:, :, h], float(h)).then_inc(q["halves"], 1)
                    if shared:
                        dve.wait_ge(q["halves"], shared)
                        step(v.tensor_copy(self.eid[:, 0:NT * shared], eid_f[:]))
                    dve.wait_ge(q["totals"], 1)
                    step(v.tensor_scalar(tot_i[:], ps_tot[:, 0:E], float(P - 1), None, ALU.add))
                    step(v.tensor_scalar(tot_i[:], tot_i[:], P.bit_length() - 1, None, ALU.logical_shift_right))
                    step(v.tensor_copy(tiles[:], tot_i[:]))
                    step(v.tensor_tensor_scan(ends, tiles[:], zero_e[:], 0.0, ALU.add, ALU.add))
                    step(v.tensor_tensor(first[:], ends, tiles[:], ALU.subtract))
                    step(v.tensor_scalar(first[:], first[:], 0.0 if cfg["by_slot"] else float(FILL_FROM), float(P), ALU.add, ALU.mult))
                    dve.wait_ge(q["rank"], 1)
                    step(v.tensor_tensor(slot_of[:], ps_rank[:, 0:NT * E].rearrange("p (t e) -> p t e", t=NT),
                                         first[:].unsqueeze(1).broadcast_to([P, NT, E]), ALU.add))
                    for j in range(K):
                        step(v.tensor_tensor(pick[:], slot_of[:], chosen[:, j], ALU.mult))
                        step(v.tensor_reduce(slot_f[:, :, j], pick[:], AX_X, ALU.add))
                    if not cfg["by_slot"]:
                        step(v.tensor_copy(slots, slot_f[:]))
                    else:
                        step(v.tensor_copy(slot_i[:], slot_f[:].rearrange("p t j -> p (t j)")))
                        v.tensor_scalar(tile_i[:], slot_i[:], P.bit_length() - 1, None, ALU.logical_shift_right)
                        step(v.tensor_scalar(place_i[:], slot_i[:], P - 1, None, ALU.bitwise_and))
                        v.tensor_copy(tile_f[:], tile_i[:])
                        step(v.tensor_copy(place_f[:], place_i[:]))
                        dve.wait_ge(q["iota"], 8)
                        hits = (v.tensor_tensor(hit[:], tile_f[:].unsqueeze(2).broadcast_to([P, NK, R]),
                                             iota_t[:].unsqueeze(1).broadcast_to([P, NK, R]), ALU.is_equal))
                        hits.then_inc(q["hit"], 1)
                        for i in range(PARTS):
                            part = slice(i * NK // PARTS, (i + 1) * NK // PARTS)
                            v.tensor_tensor(place_hit[:, part], place_f[:, part].unsqueeze(2).broadcast_to([P, NK // PARTS, P]),
                                            iota_s[:].unsqueeze(1).broadcast_to([P, NK // PARTS, P]), ALU.is_equal).then_inc(q["place_hit"], 1)
                    if not shared:
                        self.expert_of_tiles(L, eid_tables, step)
                    if cfg["by_slot"]:
                        dve.wait_ge(q["pairs"], 1)
                        step(v.tensor_copy(found[:].rearrange("p v n -> p (v n)"), ps_found[:, 0:2 * R]))
                        v.tensor_scalar(none[:], found[:, 1, :], 0.0, None, ALU.is_equal)
                        step(v.tensor_scalar(number_i[:], found[:, 1, :], -1.0, 0.0, ALU.add, ALU.max))
                        v.tensor_tensor(none[:], none[:], spare[:], ALU.mult)
                        step(v.tensor_scalar(number_i[:], number_i[:], K.bit_length() - 1, None, ALU.logical_shift_right))
                        v.tensor_scalar(dest[:], found[:, 1, :], -1.0, float(P), ALU.add, ALU.mult)
                        step(v.tensor_copy(tok_f[:], number_i[:]))
                        v.tensor_tensor(dest[:], dest[:], found[:, 0, :], ALU.add)
                        step(v.tensor_scalar(tok_f[:], tok_f[:], float(P), None, ALU.mult))
                        v.tensor_tensor(self.dest_of_slot[:, 0:R], dest[:], none[:], ALU.add)
                        step(v.tensor_tensor(self.row_of_slot[:, 0:R], tok_f[:], found[:, 0, :], ALU.add))

    def experts(self, L):
        nc, cfg, ins = self.nc, LAYERS[L], self.ins
        K, shared = cfg["topk"], cfg["shared"]
        n_exp = cfg["experts"] + shared
        N = shared * NT + routed_tiles(L)
        by_slot = cfg["by_slot"]
        off = (FILL_FROM - shared * NT) * P
        pre = f"l{L}_e_"
        sem = lambda name: self.sem(pre + name)
        with ExitStack() as tmp:
            sb = lambda name, shape, dt: tmp.enter_context(nc.sbuf_tensor(pre + name, shape, dt))
            psb = lambda name, shape: tmp.enter_context(nc.psum_tensor(pre + name, shape, F32))
            xin = sb("xin", [P, 2, D], F32)
            xh, xl = sb("xh", [P, 2, DC, P], F16), sb("xl", [P, 2, DC, P], F16)
            b1, b2 = sb("b1", [2, 2, HID], F16), sb("b2", [2, 2, D], F16)
            h = sb("h", [P, 2, HID], F32)
            hh, hl = sb("hh", [P, 2, HC, P], F16), sb("hl", [P, 2, HC, P], F16)
            y = sb("y", [P, 2, D], F32)
            ps_x, ps_h, ps_t, ps_y = psb("ps_x", [P, 2, 512]), psb("ps_h", [P, HID]), psb("ps_t", [P, HID]), psb("ps_y", [P, 2, 512])
            s = {n: sem(n) for n in ("scattered", "x_turned", "xh_ready", "xl_ready", "h_done", "h_ready", "h_turned",
                                     "hh_ready", "hl_ready", "y_done", "y_ready", "late_step", "late_split", "h_biased", "eid_step", "eid_ready")}
            AHEAD = 2 if by_slot else 1
            h_pre = sb("h_pre", [P, HID], F32) if by_slot else None

            def bias_row(e, a, n):
                return self.bias_rows(cfg["experts"])[:, bass.ds(e, 1), a:a + n].rearrange("p e n -> p (e n)")

            s_x, s_b1, s_b2, s_y = ([sem(f"{n}{u}") for u in range(2)] for n in ("x_in", "b1_in", "b2_in", "y_stored"))
            block = tmp.enter_context(nc.Block())

            late = [(e, m) for e in range(MAXE - DEFER, n_exp) for m in range(2)]
            stage = sb("stage", [P, 2, WPART], F32) if late else None
            eid_tables = self.eid_tables(L, sb) if shared else None
            s_stage = [sem("late_staged0"), sem("late_staged1")]
            routed = shared == 0

            def reach_routed(sp):
                nonlocal routed
                sp.wait_ge(s["scattered"], 16 * NT * K)
                sp.wait_ge(s["eid_ready"], 1)
                routed = True

            @block.gpsimd
            def _(pool):
                if by_slot:
                    pool.wait_ge(self.rows_stored, 16 * NT)
                    for n in range(-AHEAD - 2, N + 2):
                        if n + AHEAD + 2 < N:
                            a = n + AHEAD + 2
                            pool.wait_ge(s["x_turned"], a + 1)
                            nc.gpsimd.indirect_dma_start(xin[:, a % 2, :], None, self.xd,
                                                         bass.IndirectOffsetOnAxis(ap=self.row_of_slot[:, a:a + 1], axis=0)).then_inc(s_x[a % 2], 16)
                        if n >= 2:
                            c = n - 2
                            pool.wait_ge(s["y_ready"], c + 3)
                            nc.gpsimd.indirect_dma_start(self.yg, bass.IndirectOffsetOnAxis(ap=self.dest_of_slot[:, c:c + 1], axis=0),
                                                         y[:, c % 2, :], None).then_inc(s_y[c % 2], 16)
                    for u in range(2):
                        pool.wait_ge(s_y[u], 16 * ((N + 1 - u) // 2))
                    return
                for t in range(NT):
                    for j in range(K):
                        nc.gpsimd.indirect_dma_start(self.xg, bass.IndirectOffsetOnAxis(ap=self.slots[:, t, j:j + 1], axis=0),
                                                     self.xn[:, t, :], None).then_inc(s["scattered"], 16)
                def load(i):
                    e, m = late[i]
                    nc.gpsimd.dma_start(stage[:, m, :], ins[f"weights{L}"][e, :, m * WPART:(m + 1) * WPART]).then_inc(s_stage[m], 16)

                for i in range(min(2, len(late))):
                    load(i)
                for i, (e, m) in enumerate(late):
                    pool.wait_ge(s_stage[m], 16 * (i // 2) + 16)
                    high, low = (self.weights[:, e, w, m * WPART:(m + 1) * WPART] for w in (0, 1))
                    step = Chain(pool, s["late_step"], 2 * i)
                    step(nc.gpsimd.tensor_scalar(stage[:, m, :], stage[:, m, :], WSCALE, None, ALU.mult))
                    step(nc.gpsimd.tensor_copy(high, stage[:, m, :]))
                    nc.gpsimd.tensor_tensor(low, stage[:, m, :], high, ALU.subtract).then_inc(s["late_split"], 1)
                    if i + 2 < len(late):
                        pool.wait_ge(s["late_split"], i + 1)
                        load(i + 2)
                pool.wait_ge(s["scattered"], 16 * NT * K)

            @block.sync
            def _(sp):
                for u in range(0 if by_slot else 2):
                    sp.sem_inc(s_y[u], 16)

                if by_slot:
                    return

                def expert(m):
                    return sp.value_load(self.eid[0:1, bass.ds(m.n, 1)], min_val=0, max_val=n_exp - 1)

                def step(t, has):
                    if has(4):
                        m = t.shifted(4)
                        sp.wait_ge(s["x_turned"], m.n + 1)
                        src = self.xg[bass.ds(m.n * P + off, P), :] if routed else self.xn[:, bass.ds(m.i, 1), :].rearrange("p a d -> p (a d)")
                        sp.dma_start(xin[:, m.u, :], src).then_inc(s_x[m.u], 16)
                    if has(3):
                        m = t.shifted(3)
                        e = expert(m)
                        sp.wait_ge(s["h_done"], m.n + 1)
                        sp.dma_start(b1[:, m.u, :], self.bg[bass.ds(e, 1), :, 0:HID].rearrange("e r n -> (e r) n")).then_inc(s_b1[m.u], 16)
                    if has(2):
                        m = t.shifted(2)
                        e = expert(m)
                        sp.wait_ge(s["y_done"], m.n + 1)
                        sp.dma_start(b2[:, m.u, :], self.bg[bass.ds(e, 1), :, HID:BCOLS].rearrange("e r n -> (e r) n")).then_inc(s_b2[m.u], 16)
                    if has(0):
                        sp.wait_ge(s["y_ready"], t.n + 3)
                        sp.dma_start(self.yg[bass.ds(t.n * P + off, P), :], y[:, t.u, :]).then_inc(s_y[t.u], 16)

                run_pipeline(sp, step, N, 4, 0, per=4, pause=shared * NT - 4,
                             at_pause=lambda: reach_routed(sp))
                for u in range(0 if by_slot else 2):
                    sp.wait_ge(s_y[u], 16 * ((N + 1 - u) // 2) + 16)

            @block.tensor
            def _(pe):
                pe.sem_inc(s["x_turned"], 2)
                pe.sem_inc(s["h_done"], 2)
                pe.sem_inc(s["y_done"], 2)

                def weight(e, part, a, n):
                    return self.weights[:, bass.ds(e, 1), part, a:a + n].rearrange("p e n -> p (e n)")

                def step(t, has):
                    if has(0):
                        pe.wait_ge(s["h_ready"], t.n + 1)
                        for c in range(HC):
                            mm = nc.tensor.transpose(ps_t[:, c * P:(c + 1) * P], h[:, t.u, c * P:(c + 1) * P], self.ident[:])
                        mm.then_inc(s["h_turned"], 1)
                    if has(AHEAD + 1):
                        m = t.shifted(AHEAD + 1)
                        pe.wait_ge(s_x[m.u], 16 * m.i + 16)
                        for c in range(DC):
                            mm = nc.tensor.transpose(ps_x[:, m.u, c * P:(c + 1) * P], xin[:, m.u, c * P:(c + 1) * P], self.ident[:])
                        mm.then_inc(s["x_turned"], 1)
                    if has(AHEAD):
                        m = t.shifted(AHEAD)
                        e = pe.value_load(self.eid[0:1, bass.ds(m.n, 1)], min_val=0, max_val=n_exp - 1)
                        pe.wait_ge(s["xl_ready"], m.n + 1)
                        if by_slot:
                            pe.wait_ge(s["h_biased"], m.n + 1)
                        for c in range(DC):
                            for part, w in ((xh, 0), (xh, 1), (xl, 0)):
                                mm = nc.tensor.matmul(ps_h[:], part[:, m.u, c, :], weight(e, w, c * HID, HID),
                                                      start=(c == 0 and part is xh and w == 0), stop=(by_slot and c == DC - 1 and part is xl))
                        if not by_slot:
                            pe.wait_ge(s_b1[m.u], 16 * m.i + 16)
                            mm = nc.tensor.matmul(ps_h[:], self.ones16[:], b1[:, m.u, :], start=False, stop=True)
                        mm.then_inc(s["h_done"], 1)
                    if has(0):
                        e = pe.value_load(self.eid[0:1, bass.ds(t.n, 1)], min_val=0, max_val=n_exp - 1)
                        pe.wait_ge(s["hl_ready"], t.n + 1)
                        pe.wait_ge(s["y_ready"], t.n + 1)
                        for c in range(HC):
                            for part, w in ((hh, 0), (hh, 1), (hl, 0)):
                                mm = nc.tensor.matmul(ps_y[:, t.u, 0:D], part[:, t.u, c, :], weight(e, w, DC * HID + c * D, D),
                                                      start=(c == 0 and part is hh and w == 0), stop=(by_slot and c == HC - 1 and part is hl))
                        if not by_slot:
                            pe.wait_ge(s_b2[t.u], 16 * t.i + 16)
                            mm = nc.tensor.matmul(ps_y[:, t.u, 0:D], self.ones16[:], b2[:, t.u, :], start=False, stop=True)
                        mm.then_inc(s["y_done"], 1)

                run_pipeline(pe, step, N, AHEAD + 1, 0, per=4, pause=shared * NT - 2 if late else None,
                             at_pause=lambda: (pe.wait_ge(s["late_split"], len(late)), pe.wait_ge(s["eid_ready"], 1)))

            @block.scalar
            def _(act):
                def step(t, has):
                    if has(0):
                        act.wait_ge(s["h_turned"], t.n + 1)
                        nc.scalar.copy(hh[:, t.u].rearrange("p c t -> p (c t)"), ps_t[:]).then_inc(s["hh_ready"], 1)
                    if has(AHEAD + 1):
                        m = t.shifted(AHEAD + 1)
                        act.wait_ge(s["x_turned"], m.n + 3)
                        nc.scalar.copy(xh[:, m.u].rearrange("p c t -> p (c t)"), ps_x[:, m.u, 0:D]).then_inc(s["xh_ready"], 1)
                    if has(AHEAD):
                        m = t.shifted(AHEAD)
                        if by_slot:
                            act.wait_ge(s["h_biased"], m.n + 2)
                            nc.scalar.activation(h[:, m.u, :], h_pre[:], ACT.Gelu).then_inc(s["h_ready"], 1)
                        else:
                            act.wait_ge(s["h_done"], m.n + 3)
                            nc.scalar.activation(h[:, m.u, :], ps_h[:], ACT.Gelu, scale=1.0 / WSCALE).then_inc(s["h_ready"], 1)

                run_pipeline(act, step, N, AHEAD + 1, 0, per=4)

            @block.vector
            def _(dve):
                dve.sem_inc(s["y_ready"], 2)
                if shared:
                    self.expert_of_tiles(L, eid_tables, Chain(dve, s["eid_step"]))
                    dve.sem_inc(s["eid_ready"], 1)
                if by_slot:
                    dve.sem_inc(s["h_biased"], 1)
                    dve.wait_ge(self.biases_in, 16)

                def step(t, has):
                    if has(0):
                        dve.wait_ge(s["hh_ready"], t.n + 1)
                        nc.vector.tensor_tensor(hl[:, t.u].rearrange("p c t -> p (c t)"), ps_t[:], hh[:, t.u].rearrange("p c t -> p (c t)"),
                                                ALU.subtract).then_inc(s["hl_ready"], 1)
                    if has(AHEAD + 1):
                        m = t.shifted(AHEAD + 1)
                        dve.wait_ge(s["xh_ready"], m.n + 1)
                        nc.vector.tensor_tensor(xl[:, m.u].rearrange("p c t -> p (c t)"), ps_x[:, m.u, 0:D],
                                                xh[:, m.u].rearrange("p c t -> p (c t)"), ALU.subtract).then_inc(s["xl_ready"], 1)
                    if has(AHEAD) and by_slot:
                        m = t.shifted(AHEAD)
                        e = dve.value_load(self.eid[0:1, bass.ds(m.n, 1)], min_val=0, max_val=n_exp - 1)
                        dve.wait_ge(s["h_done"], m.n + 3)
                        nc.vector.scalar_tensor_tensor(out=h_pre[:], in0=ps_h[:], scalar=1.0 / WSCALE, in1=bias_row(e, 0, HID),
                                                       op0=ALU.mult, op1=ALU.add).then_inc(s["h_biased"], 1)
                    if has(0):
                        if by_slot:
                            e = dve.value_load(self.eid[0:1, bass.ds(t.n, 1)], min_val=0, max_val=n_exp - 1)
                        dve.wait_ge(s["y_done"], t.n + 3)
                        if not by_slot:
                            dve.wait_ge(s_y[t.u], 16 * t.i + 16)
                        elif not (isinstance(t.n, int) and t.n < 2):
                            dve.wait_ge(s_y[t.u], 16 * t.i)
                        if by_slot:
                            nc.vector.scalar_tensor_tensor(out=y[:, t.u, :], in0=ps_y[:, t.u, 0:D], scalar=1.0 / WSCALE, in1=bias_row(e, HID, D),
                                                           op0=ALU.mult, op1=ALU.add).then_inc(s["y_ready"], 1)
                        else:
                            nc.vector.tensor_scalar(y[:, t.u, :], ps_y[:, t.u, 0:D], 1.0 / WSCALE, None, ALU.mult).then_inc(s["y_ready"], 1)

                run_pipeline(dve, step, N, AHEAD + 1, 2 if by_slot else 0, per=4)

    def combine(self, L):
        nc, cfg = self.nc, LAYERS[L]
        K, shared = cfg["topk"], cfg["shared"]
        pre = f"l{L}_c_"
        sem = lambda name: self.sem(pre + name)
        DEPTH = 4 if shared else 8
        if L + 1 < len(LAYERS):
            self.tables(L + 1)
        with ExitStack() as tmp:
            sb = lambda name, shape, dt: tmp.enter_context(nc.sbuf_tensor(pre + name, shape, dt))
            at, yr = self.lent(0, [P, DEPTH * K * D])
            yr = yr.rearrange("p (u k d) -> p u k d", u=DEPTH, k=K)
            if shared:
                at, ys = self.lent(at, [P, DEPTH * shared * D])
                ys = ys.rearrange("p (u k d) -> p u k d", u=DEPTH, k=shared)
            ps_base = tmp.enter_context(nc.psum_tensor(pre + "ps_base", [P, DEPTH, 2 * D], F32)) if shared else None
            acc, x_new = sb("acc", [P, 2, D], F32), sb("x_new", [P, 2, D], F32)
            stats, mv = sb("stats", [P, 2, 6], F32), sb("mv", [P, 2, 2], F32)
            s = {n: sem(n) for n in ("summed", "used", "rstd_step", "stats_step", "stored", "base_done")}
            last = L + 1 == len(LAYERS)
            s_r, s_s = ([sem(f"{n}{u}") for u in range(DEPTH)] for n in ("gathered", "shared_in"))
            prepare = self.prepare(L + 1, tmp, lambda eng: None) if L + 1 < len(LAYERS) else None
            block = tmp.enter_context(nc.Block())

            @block.gpsimd
            def _(pool):
                for t in range(0 if cfg["by_slot"] else NT):
                    if t >= DEPTH:
                        pool.wait_ge(s["used"], t - DEPTH + 1)
                    for j in range(K):
                        nc.gpsimd.indirect_dma_start(yr[:, t % DEPTH, j, :], None, self.yg,
                                                     bass.IndirectOffsetOnAxis(ap=self.slots[:, t, j:j + 1], axis=0)).then_inc(s_r[t % DEPTH], 16)
                if not last:
                    for t0, t1 in ((0, NT - DEPTH), (NT - DEPTH, NT)):
                        pool.wait_ge(s["stats_step"], 5 * t1 // 2)
                        nc.gpsimd.tensor_tensor(self.rstd[:, t0:t1], self.rstd[:, t0:t1], self.half[:, t0:t1], ALU.pow).then_inc(s["rstd_step"], 1)
                    pool.wait_ge(s["rstd_step"], 2)

            @block.sync
            def _(sp):
                rows, s_rows, per = (yr, s_r, K) if cfg["by_slot"] else (ys, s_s, shared) if shared else (None, None, 0)

                def load(t, u):
                    sp.dma_start(rows[:, u], self.yg[bass.ds(t * (per * P), per * P), :].rearrange("(q p) d -> p q d", p=P)).then_inc(s_rows[u], 16)

                def first_rows():
                    for t in range(DEPTH):
                        load(t, t)

                def other_rows():
                    with sp.Fori(0, (NT - DEPTH) // DEPTH) as k:
                        for u in range(DEPTH):
                            if shared:
                                sp.wait_ge(s["base_done"], k * (DEPTH // 2) + (u // 2 + 1))
                            else:
                                sp.wait_ge(s["used"], k * DEPTH + (u + 1))
                            load(k * DEPTH + (DEPTH + u), u)

                if per:
                    first_rows()
                if prepare:
                    prepare[0](sp, other_rows if per else lambda: None)
                elif per:
                    other_rows()
                if last:
                    with sp.Fori(0, NT // 2) as k:
                        sp.wait_ge(s["used"], k * 2 + 2)
                        sp.dma_start(self.out[bass.ds(k * (2 * P), 2 * P), :].rearrange("(t p) d -> p t d", p=P),
                                     self.x[:, bass.ds(k * 2, 2), :]).then_inc(s["stored"], 16)
                    sp.wait_ge(s["stored"], 16 * (NT // 2))

            half_groups = NT // DEPTH // 2

            @block.tensor
            def _(pe):
                def base_sums(k, k0):
                    for pair in range(DEPTH // 2):
                        if k0:
                            pe.wait_ge(s["used"], (k - half_groups) * DEPTH + 2 * (pair + 1))
                        at = (k - k0) * (DEPTH // 2) + pair
                        for i in range(2):
                            u = 2 * pair + i
                            pe.wait_ge(s_s[u], k * 16 + 16)
                            rows = [self.xn[:, bass.ds(k * DEPTH + u, 1), :].rearrange("p a d -> p (a d)")] + [ys[:, u, q, :] for q in range(shared)]
                            for j, src in enumerate(rows):
                                mm = nc.tensor.matmul(ps_base[:, bass.ds(at, 1), i * D:(i + 1) * D].rearrange("p a d -> p (a d)"), self.ident[:], src,
                                                      start=(j == 0), stop=(j == shared))
                        mm.then_inc(s["base_done"], 1)

                if shared:
                    with pe.Fori(0, half_groups) as k:
                        base_sums(k, 0)
                    prepare[1](pe, lambda: base_sums(half_groups, half_groups))
                    base_sums(half_groups + 1, half_groups)

            if prepare:
                @block.scalar
                def _(act):
                    prepare[2](act)

            @block.vector
            def _(dve):
                loads = 1 if cfg["by_slot"] else K
                def group(k, k0):
                    for u0 in range(0, DEPTH, 2):
                        t0, both = k * DEPTH + u0, slice(u0, u0 + 2)
                        rows = self.x[:, bass.ds(t0, 2), :]
                        pairs_before = k * (DEPTH // 2) + u0 // 2
                        n_sum = 2 * K
                        base, done = pairs_before * n_sum, 0

                        def summed(ins_):
                            nonlocal done
                            done += 1
                            ins_.then_inc(s["summed"], 1)

                        if shared:
                            dve.wait_ge(s["base_done"], pairs_before + 1)
                        for u in (u0, u0 + 1):
                            dve.wait_ge(s_r[u], k * (16 * loads) + 16 * loads)
                        for j in range(K):
                            for i, u in enumerate((u0, u0 + 1)):
                                g = self.gate[:, bass.ds(t0 + i, 1), j]
                                if j:
                                    dve.wait_ge(s["summed"], base + done - 1)
                                if j:
                                    summed(nc.vector.scalar_tensor_tensor(out=acc[:, i, :], in0=yr[:, u, j, :], scalar=g, in1=acc[:, i, :],
                                                                          op0=ALU.mult, op1=ALU.add))
                                elif shared:
                                    first = ps_base[:, bass.ds((k - k0) * (DEPTH // 2) + u0 // 2, 1), i * D:(i + 1) * D].rearrange("p a d -> p (a d)")
                                    summed(nc.vector.scalar_tensor_tensor(out=acc[:, i, :], in0=yr[:, u, j, :], scalar=g, in1=first,
                                                                          op0=ALU.mult, op1=ALU.add))
                                else:
                                    summed(nc.vector.tensor_scalar(acc[:, i, :], yr[:, u, j, :], g, None, ALU.mult))
                        for i in range(2):
                            dve.wait_ge(s["summed"], base + n_sum - 1 + i)
                            nc.vector.scalar_tensor_tensor(out=rows[:, i, :] if last else x_new[:, i, :], in0=acc[:, i, :], scalar=self.tg[:, 2 * L + 1:2 * L + 2],
                                                           in1=rows[:, i, :], op0=ALU.mult, op1=ALU.add).then_inc(s["used"], 1)
                        if last:
                            dve.wait_ge(s["used"], t0 + 2)
                            continue
                        for i in range(2):
                            dve.wait_ge(s["used"], t0 + i + 1)
                            nc.vector.bn_stats(stats[:, i, :], x_new[:, i, :]).then_inc(s["stats_step"], 1)
                        dve.wait_ge(s["stats_step"], pairs_before * 5 + 2)
                        nc.vector.tensor_scalar(rows, x_new[:], 0.0, None, ALU.add)
                        for i in range(2):
                            nc.vector.bn_aggr(mv[:, i, :], stats[:, i, :]).then_inc(s["stats_step"], 1)
                        dve.wait_ge(s["stats_step"], pairs_before * 5 + 4)
                        nc.vector.tensor_scalar(self.mean[:, bass.ds(t0, 2)], mv[:, :, 0], 0.0, None, ALU.add)
                        nc.vector.tensor_scalar(self.rstd[:, bass.ds(t0, 2)], mv[:, :, 1], EPS, None, ALU.add).then_inc(s["stats_step"], 1)

                def first_half():
                    with dve.Fori(0, half_groups) as k:
                        group(k, 0)

                if prepare:
                    prepare[3](dve, first_half, lambda: group(half_groups, half_groups))
                    group(half_groups + 1, half_groups)
                else:
                    first_half()
                    with dve.Fori(half_groups, 2 * half_groups) as k:
                        group(k, half_groups)


def flamingo_layers(nc, ins, out):
    with ExitStack() as ctx:
        b = Build(nc, ctx, ins, out)
        b.start()
        for L in range(len(LAYERS)):
            b.attention(L)
            b.route(L)
            b.experts(L)
            b.combine(L)
            if L + 1 < len(LAYERS):
                b.recycle_semaphores()


def laid_out(v):
    rows = lambda w: np.ascontiguousarray(w)
    cols = lambda b: np.ascontiguousarray(b.reshape(DC, P).T)
    ctx = v["ctx_1024"].reshape(B * KEYS, D)

    def experts(w1, w2):
        e = w1.shape[0]
        a = w1.reshape(e, DC, P, HID).transpose(0, 2, 1, 3).reshape(e, P, DC * HID)
        b = w2.reshape(e, HC, P, D).transpose(0, 2, 1, 3).reshape(e, P, HC * D)
        return np.ascontiguousarray(np.concatenate([a, b], axis=2))

    sw1 = v["L0_ffn_sW1"].reshape(D, 2, HID).transpose(1, 0, 2)
    sw2 = v["L0_ffn_sW2"].reshape(2, HID, D)
    sb1 = v["L0_ffn_sb1"].reshape(2, HID)
    sb2 = np.concatenate([v["L0_ffn_sb2"], np.zeros((1, D), np.float32)], axis=0)
    return {
        "x": rows(v["x"].reshape(B * S, D)),
        "ctx_t": rows(ctx.T),
        "gates": rows(np.broadcast_to(np.stack([v["g_xattn"][0], v["g_ffn"][0], v["g_xattn"][1], v["g_ffn"][1]]), (P, 4))),
        "mask0": rows(np.broadcast_to(v["mask_Bx1x1xS2_bf1"].reshape(1, B * KEYS).view(np.uint8), (P, B * KEYS))),
        "mask_col0": rows(v["mask_Bx1x1xS2_bf1"].reshape(B, KEYS).view(np.uint8).T),
        "mask1": rows(np.broadcast_to(v["mask_BxS2_ik0"].reshape(1, B * KEYS), (P, B * KEYS))),
        "mask_col1": rows(v["mask_BxS2_ik0"].T),
        "wq0": rows(v["L0_xattn_Wq"]), "wk0": rows(v["L0_xattn_Wk"]), "wv0": rows(v["L0_xattn_Wv"]), "wo0": rows(v["L0_xattn_Wo"]),
        "bq0": cols(v["L0_xattn_bq"]), "bk0": cols(v["L0_xattn_bk"]), "bv0": rows(v["L0_xattn_bv"][None]), "bo0": rows(v["L0_xattn_bo"][None]),
        "wq1": rows(v["L1_xattn_q_w"].T), "wk1": rows(v["L1_xattn_k_w"].T), "wv1": rows(v["L1_xattn_v_w"].T),
        "bq1": cols(v["L1_xattn_q_b"]), "bk1": cols(v["L1_xattn_k_b"]), "bv1": rows(v["L1_xattn_v_b"][None]),
        "weights0": experts(np.concatenate([sw1, v["L0_ffn_rW1"]]), np.concatenate([sw2, v["L0_ffn_rW2"]])),
        "biases0": rows(np.concatenate([np.concatenate([sb1, v["L0_ffn_rb1"]]), np.concatenate([sb2, v["L0_ffn_rb2"]])], axis=1)),
        "weights1": experts(v["L1_ffn_W1"], v["L1_ffn_W2"]),
        "biases1": rows(np.concatenate([v["L1_ffn_b1"], v["L1_ffn_b2"]], axis=1)),
        "wg0": rows(v["L0_ffn_gW"]), "bg0": rows(np.broadcast_to(v["L0_ffn_gb"], (P, 15))),
        "wg1": rows(v["L1_ffn_Wg"]), "bg1": rows(np.broadcast_to(v["L1_ffn_bg"], (P, 8))),
    }


def kernel(**inputs):
    import concourse.bacc as bacc
    from concourse.bass_utils import run_bass_kernel_spmd

    arrays = {f"in_{k}": a for k, a in laid_out({k: np.asarray(a) for k, a in inputs.items()}).items()}
    nc = bacc.Bacc("TRN2", target_bir_lowering=False, num_devices=1)
    ins = {k[3:]: nc.dram_tensor(k, a.shape, mybir.dt.from_np(a.dtype), kind="ExternalInput").ap() for k, a in arrays.items()}
    out = nc.dram_tensor("out", (B * S, D), F32, kind="ExternalOutput").ap()
    flamingo_layers(nc, ins, out)
    r = run_bass_kernel_spmd(nc, [arrays], core_ids=[0])
    return r.results[0]["out"].reshape(B, S, D)
```
